# Optimizing a Trainium2 kernel written in Bass

```python
import numpy as np
import jax
import jax.numpy as jnp

def _softmax(x, axis=-1):
    return jax.nn.softmax(x, axis=axis)

def _gelu(x):
    return jax.nn.gelu(x, approximate=True)

def _silu(x):
    return jax.nn.silu(x)

def _sigmoid(x):
    return jax.nn.sigmoid(x)

def _layernorm(x, axis=-1, eps=1e-05):
    m = jnp.mean(x, axis=axis, keepdims=True)
    v = jnp.var(x, axis=axis, keepdims=True)
    return (x - m) / jnp.sqrt(v + eps)

def _scatter_add(tgt, idx, src, axis=0):
    return tgt.at[idx].add(src)

def _segment_sum(src, seg, n):
    return jax.ops.segment_sum(src, seg, n)
kernel_name = 'mk_perceiver_d1_seqx_r4_2b2d76'

def setup_inputs(seed: int=0):
    np.random.seed(seed)
    _w = jnp.asarray

    def _rec_inputs():
        import jax
        import jax.numpy as jnp
        _rk = jax.random.key(seed)
        x = -0.000125 + 0.9999 * jax.random.normal(jax.random.fold_in(_rk, 1), (32, 32, 512), jnp.float32)
        _lenS = 32 - jax.random.randint(jax.random.fold_in(_rk, 7), (32,), 0, max(1, 32 // 4) + 1, jnp.int32)
        _lenS2 = 257 - jax.random.randint(jax.random.fold_in(_rk, 8), (32,), 0, max(1, 257 // 4) + 1, jnp.int32)
        _ctx_2048P = jax.random.normal(jax.random.fold_in(_rk, 11), (32, 16, 512), jnp.float32)
        _ctx_2048c = jax.random.dirichlet(jax.random.fold_in(_rk, 511), 0.3 * jnp.ones((16,), jnp.float32), (32, 257))
        _ctx_2048t = jnp.einsum('bsk,bkd->bsd', _ctx_2048c, _ctx_2048P)
        _ctx_2048t = _ctx_2048t * jax.lax.rsqrt(jnp.mean(jnp.square(_ctx_2048t)) + 1e-12) * 0.953939
        ctx_2048 = -1.52775e-05 + 0.999936 * (_ctx_2048t + 0.3 * jax.random.normal(jax.random.fold_in(_rk, 611), (32, 257, 512), jnp.float32))
        return (x, ctx_2048)
    x, ctx_2048 = _rec_inputs()

    def _L0_xattn_setup():
        import jax, jax.numpy as jnp
        import numpy as np
        EPS = 1e-06
        NUM_HEADS = 16

        def _feature_map(x):
            return jnp.where(x > 0, x + 1.0, jnp.exp(x))
        key = jax.random.key(seed)
        ks = jax.random.split(key, 7)
        B, L, S, D = (4, 1024, 1024, 512)
        sc = 1.0 / np.sqrt(D)
        return {'query': jax.random.normal(ks[0], (B, L, D), jnp.float32), 'kv': jax.random.normal(ks[1], (B, S, D), jnp.float32), 'Wq': jax.random.normal(ks[2], (D, D), jnp.float32) * sc, 'Wg': jax.random.normal(ks[3], (D, D), jnp.float32) * sc, 'bg': jnp.ones((D,), jnp.float32), 'Wkv': jax.random.normal(ks[4], (2 * D, D), jnp.float32) * sc, 'Wo': jax.random.normal(ks[5], (D, D), jnp.float32) * sc}
    _L0_xattn_all = _L0_xattn_setup()
    _L0_xattn_in = {k: v for k, v in _L0_xattn_all.items() if k in ('Wq', 'Wg', 'bg', 'Wkv', 'Wo')}
    del _L0_xattn_all

    def _L0_attn_setup():
        import jax, jax.numpy as jnp
        import numpy as np
        BLOCK = 32
        NUM_HEADS = 16
        HEAD_DIM = 128
        FP4_GRID = jnp.array([0.0, 0.5, 1.0, 1.5, 2.0, 3.0, 4.0, 6.0], dtype=jnp.float32)

        def quantize_to_mxfp4(w, block_size=BLOCK):
            D, F = w.shape
            blocks = w.reshape(D // block_size, block_size, F)
            amax = jnp.max(jnp.abs(blocks), axis=1)
            e = jnp.floor(jnp.log2(jnp.maximum(amax, 1e-12) / 6.0))
            scale = jnp.exp2(e)
            v = blocks / scale[:, None, :]
            idx = jnp.argmin(jnp.abs(jnp.abs(v)[..., None] - FP4_GRID), axis=-1)
            codes = jnp.sign(v) * FP4_GRID[idx]
            return (codes.reshape(D, F).astype(jnp.float32), scale.astype(jnp.float32))

        def _mxfp4_matmul(x, codes, scales, block_size=BLOCK):
            w = codes * jnp.repeat(scales, block_size, axis=0)
            return x @ w
        key = jax.random.key(seed)
        ks = jax.random.split(key, 9)
        B, S, D = (2, 512, 512)
        feat = NUM_HEADS * HEAD_DIM
        x = jax.random.normal(ks[0], (B, S, D), dtype=jnp.float32)

        def make_w(k, din, dout):
            w = jax.random.normal(k, (din, dout), dtype=jnp.float32) * (1.0 / np.sqrt(din))
            return quantize_to_mxfp4(w, BLOCK)
        wq_codes, wq_scales = make_w(ks[1], D, feat)
        wk_codes, wk_scales = make_w(ks[2], D, feat)
        wv_codes, wv_scales = make_w(ks[3], D, feat)
        wo_codes, wo_scales = make_w(ks[4], feat, D)
        bq = jnp.zeros((feat,), jnp.float32)
        bk = jnp.zeros((feat,), jnp.float32)
        bv = jnp.zeros((feat,), jnp.float32)
        bo = jnp.zeros((D,), jnp.float32)
        return {'x': x, 'wq_codes': wq_codes, 'wq_scales': wq_scales, 'bq': bq, 'wk_codes': wk_codes, 'wk_scales': wk_scales, 'bk': bk, 'wv_codes': wv_codes, 'wv_scales': wv_scales, 'bv': bv, 'wo_codes': wo_codes, 'wo_scales': wo_scales, 'bo': bo}
    _L0_attn_all = _L0_attn_setup()
    _L0_attn_in = {k: v for k, v in _L0_attn_all.items() if k in ('wq_codes', 'wq_scales', 'bq', 'wk_codes', 'wk_scales', 'bk', 'wv_codes', 'wv_scales', 'bv', 'wo_codes', 'wo_scales', 'bo')}
    del _L0_attn_all

    def _L0_ffn_setup():
        import jax, jax.numpy as jnp
        import numpy as np
        E = 32
        K = 4
        G = 4
        TG = 2
        H = 512
        F = 256
        FS = 512
        SCALE = 2.0
        B, S = (2, 256)
        N = B * S
        CAP = 2 * (N * K // E)

        def _gate(x, gate_w, gate_bias):
            logits = x @ gate_w.T
            scores = jax.nn.sigmoid(logits)
            sc = scores + gate_bias
            n = x.shape[0]
            grp = sc.reshape(n, G, E // G)
            group_scores = jax.lax.top_k(grp, 2)[0].sum(-1)
            _, gidx = jax.lax.top_k(group_scores, TG)
            gmask = jnp.zeros((n, G), sc.dtype).at[jnp.arange(n)[:, None], gidx].set(1.0)
            smask = jnp.repeat(gmask, E // G, axis=1)
            tmp = jnp.where(smask > 0, sc, 0.0)
            _, topk_idx = jax.lax.top_k(tmp, K)
            topk_w = jnp.take_along_axis(scores, topk_idx, axis=1)
            topk_w = topk_w / (topk_w.sum(-1, keepdims=True) + 1e-20)
            return (topk_idx, topk_w * SCALE)

        def _moe(x, topk_idx, topk_w, w1, w2, w3):
            n = x.shape[0]
            flat_e = topk_idx.reshape(-1)
            oh = jax.nn.one_hot(flat_e, E, dtype=jnp.int32)
            pos = (jnp.cumsum(oh, axis=0) * oh).sum(-1) - 1
            keep = pos < CAP
            slot = jnp.where(keep, pos, CAP)
            x_rep = jnp.repeat(x, K, axis=0)
            buf = jnp.zeros((E, CAP, H), x.dtype).at[flat_e, slot].set(x_rep, mode='drop')
            h = jax.nn.silu(jnp.einsum('ech,ehf->ecf', buf, w1)) * jnp.einsum('ech,ehf->ecf', buf, w3)
            ob = jnp.einsum('ecf,efh->ech', h, w2)
            y = ob[flat_e, jnp.minimum(slot, CAP - 1)]
            y = jnp.where(keep[:, None], y, 0.0)
            return (y.reshape(n, K, H) * topk_w[:, :, None]).sum(1)
        key = jax.random.key(seed)
        ks = jax.random.split(key, 9)
        w = 0.02
        return {'hidden_states': jax.random.normal(ks[0], (B, S, H), jnp.float32), 'gate_w': jax.random.normal(ks[1], (E, H), jnp.float32) * w, 'gate_bias': jax.random.normal(ks[2], (E,), jnp.float32) * w, 'w1': jax.random.normal(ks[3], (E, H, F), jnp.float32) * w, 'w2': jax.random.normal(ks[4], (E, F, H), jnp.float32) * w, 'w3': jax.random.normal(ks[5], (E, H, F), jnp.float32) * w, 'shared_gate': jax.random.normal(ks[6], (H, FS), jnp.float32) * w, 'shared_up': jax.random.normal(ks[7], (H, FS), jnp.float32) * w, 'shared_down': jax.random.normal(ks[8], (FS, H), jnp.float32) * w}
    _L0_ffn_all = _L0_ffn_setup()
    _L0_ffn_in = {k: v for k, v in _L0_ffn_all.items() if k in ('gate_w', 'gate_bias', 'w1', 'w2', 'w3', 'shared_gate', 'shared_up', 'shared_down')}
    del _L0_ffn_all
    return {'x': x, 'ctx_2048': ctx_2048, 'L0_xattn_Wq': _L0_xattn_in['Wq'], 'L0_xattn_Wg': _L0_xattn_in['Wg'], 'L0_xattn_bg': _L0_xattn_in['bg'], 'L0_xattn_Wkv': _L0_xattn_in['Wkv'], 'L0_xattn_Wo': _L0_xattn_in['Wo'], 'L0_attn_wq_codes': _L0_attn_in['wq_codes'], 'L0_attn_wq_scales': _L0_attn_in['wq_scales'], 'L0_attn_bq': _L0_attn_in['bq'], 'L0_attn_wk_codes': _L0_attn_in['wk_codes'], 'L0_attn_wk_scales': _L0_attn_in['wk_scales'], 'L0_attn_bk': _L0_attn_in['bk'], 'L0_attn_wv_codes': _L0_attn_in['wv_codes'], 'L0_attn_wv_scales': _L0_attn_in['wv_scales'], 'L0_attn_bv': _L0_attn_in['bv'], 'L0_attn_wo_codes': _L0_attn_in['wo_codes'], 'L0_attn_wo_scales': _L0_attn_in['wo_scales'], 'L0_attn_bo': _L0_attn_in['bo'], 'L0_ffn_gate_w': _L0_ffn_in['gate_w'], 'L0_ffn_gate_bias': _L0_ffn_in['gate_bias'], 'L0_ffn_w1': _L0_ffn_in['w1'], 'L0_ffn_w2': _L0_ffn_in['w2'], 'L0_ffn_w3': _L0_ffn_in['w3'], 'L0_ffn_shared_gate': _L0_ffn_in['shared_gate'], 'L0_ffn_shared_up': _L0_ffn_in['shared_up'], 'L0_ffn_shared_down': _L0_ffn_in['shared_down']}

def reference(x, ctx_2048, L0_xattn_Wq, L0_xattn_Wg, L0_xattn_bg, L0_xattn_Wkv, L0_xattn_Wo, L0_attn_wq_codes, L0_attn_wq_scales, L0_attn_bq, L0_attn_wk_codes, L0_attn_wk_scales, L0_attn_bk, L0_attn_wv_codes, L0_attn_wv_scales, L0_attn_bv, L0_attn_wo_codes, L0_attn_wo_scales, L0_attn_bo, L0_ffn_gate_w, L0_ffn_gate_bias, L0_ffn_w1, L0_ffn_w2, L0_ffn_w3, L0_ffn_shared_gate, L0_ffn_shared_up, L0_ffn_shared_down):
    import jax
    import jax.numpy as jnp

    def _L0_xattn_ref(query, kv, Wq, Wg, bg, Wkv, Wo):
        import jax, jax.numpy as jnp
        import numpy as np
        EPS = 1e-06
        NUM_HEADS = 16

        def _feature_map(x):
            return jnp.where(x > 0, x + 1.0, jnp.exp(x))
        B, L, D = query.shape
        S = kv.shape[1]
        H = NUM_HEADS
        hd = D // H
        q = query @ Wq.T
        gate = jax.nn.sigmoid(query @ Wg.T + bg)
        kvp = kv @ Wkv.T
        k, v = jnp.split(kvp, 2, axis=-1)
        q = _feature_map(q.reshape(B, L, H, hd).transpose(0, 2, 1, 3))
        k = _feature_map(k.reshape(B, S, H, hd).transpose(0, 2, 1, 3))
        v = v.reshape(B, S, H, hd).transpose(0, 2, 1, 3)
        kv_summary = jnp.einsum('bhsd,bhse->bhde', k, v)
        k_sum = k.sum(axis=-2)
        z = 1.0 / (jnp.einsum('bhld,bhd->bhl', q, k_sum)[..., None] + EPS)
        attn = jnp.einsum('bhld,bhde->bhle', q, kv_summary) * z
        attn = attn.transpose(0, 2, 1, 3).reshape(B, L, D)
        out = attn * gate @ Wo.T
        return out

    def _L0_attn_ref(x, wq_codes, wq_scales, bq, wk_codes, wk_scales, bk, wv_codes, wv_scales, bv, wo_codes, wo_scales, bo):
        import jax, jax.numpy as jnp
        import numpy as np
        BLOCK = 32
        NUM_HEADS = 16
        HEAD_DIM = 128
        FP4_GRID = jnp.array([0.0, 0.5, 1.0, 1.5, 2.0, 3.0, 4.0, 6.0], dtype=jnp.float32)

        def quantize_to_mxfp4(w, block_size=BLOCK):
            D, F = w.shape
            blocks = w.reshape(D // block_size, block_size, F)
            amax = jnp.max(jnp.abs(blocks), axis=1)
            e = jnp.floor(jnp.log2(jnp.maximum(amax, 1e-12) / 6.0))
            scale = jnp.exp2(e)
            v = blocks / scale[:, None, :]
            idx = jnp.argmin(jnp.abs(jnp.abs(v)[..., None] - FP4_GRID), axis=-1)
            codes = jnp.sign(v) * FP4_GRID[idx]
            return (codes.reshape(D, F).astype(jnp.float32), scale.astype(jnp.float32))

        def _mxfp4_matmul(x, codes, scales, block_size=BLOCK):
            w = codes * jnp.repeat(scales, block_size, axis=0)
            return x @ w
        B, S, D = x.shape
        q = _mxfp4_matmul(x, wq_codes, wq_scales) + bq
        k = _mxfp4_matmul(x, wk_codes, wk_scales) + bk
        v = _mxfp4_matmul(x, wv_codes, wv_scales) + bv
        q = q.reshape(B, S, NUM_HEADS, HEAD_DIM)
        k = k.reshape(B, S, NUM_HEADS, HEAD_DIM)
        v = v.reshape(B, S, NUM_HEADS, HEAD_DIM)
        scores = jnp.einsum('bqhd,bkhd->bhqk', q, k) / jnp.sqrt(jnp.float32(HEAD_DIM))
        attn = jax.nn.softmax(scores, axis=-1)
        out = jnp.einsum('bhqk,bkhd->bqhd', attn, v).reshape(B, S, NUM_HEADS * HEAD_DIM)
        return _mxfp4_matmul(out, wo_codes, wo_scales) + bo

    def _L0_ffn_ref(hidden_states, gate_w, gate_bias, w1, w2, w3, shared_gate, shared_up, shared_down):
        import jax, jax.numpy as jnp
        import numpy as np
        E = 32
        K = 4
        G = 4
        TG = 2
        H = 512
        F = 256
        FS = 512
        SCALE = 2.0
        B, S = (2, 256)
        N = B * S
        CAP = 2 * (N * K // E)

        def _gate(x, gate_w, gate_bias):
            logits = x @ gate_w.T
            scores = jax.nn.sigmoid(logits)
            sc = scores + gate_bias
            n = x.shape[0]
            grp = sc.reshape(n, G, E // G)
            group_scores = jax.lax.top_k(grp, 2)[0].sum(-1)
            _, gidx = jax.lax.top_k(group_scores, TG)
            gmask = jnp.zeros((n, G), sc.dtype).at[jnp.arange(n)[:, None], gidx].set(1.0)
            smask = jnp.repeat(gmask, E // G, axis=1)
            tmp = jnp.where(smask > 0, sc, 0.0)
            _, topk_idx = jax.lax.top_k(tmp, K)
            topk_w = jnp.take_along_axis(scores, topk_idx, axis=1)
            topk_w = topk_w / (topk_w.sum(-1, keepdims=True) + 1e-20)
            return (topk_idx, topk_w * SCALE)

        def _moe(x, topk_idx, topk_w, w1, w2, w3):
            n = x.shape[0]
            flat_e = topk_idx.reshape(-1)
            oh = jax.nn.one_hot(flat_e, E, dtype=jnp.int32)
            pos = (jnp.cumsum(oh, axis=0) * oh).sum(-1) - 1
            keep = pos < CAP
            slot = jnp.where(keep, pos, CAP)
            x_rep = jnp.repeat(x, K, axis=0)
            buf = jnp.zeros((E, CAP, H), x.dtype).at[flat_e, slot].set(x_rep, mode='drop')
            h = jax.nn.silu(jnp.einsum('ech,ehf->ecf', buf, w1)) * jnp.einsum('ech,ehf->ecf', buf, w3)
            ob = jnp.einsum('ecf,efh->ech', h, w2)
            y = ob[flat_e, jnp.minimum(slot, CAP - 1)]
            y = jnp.where(keep[:, None], y, 0.0)
            return (y.reshape(n, K, H) * topk_w[:, :, None]).sum(1)
        b, s, h = hidden_states.shape
        x = hidden_states.reshape(-1, h)
        topk_idx, topk_w = _gate(x, gate_w, gate_bias)
        out = _moe(x, topk_idx, topk_w, w1, w2, w3)
        shared = jax.nn.silu(x @ shared_gate) * (x @ shared_up) @ shared_down
        return (out + shared).reshape(b, s, h)
    x = x + _L0_xattn_ref(_layernorm(x, axis=-1), ctx_2048, L0_xattn_Wq, L0_xattn_Wg, L0_xattn_bg, L0_xattn_Wkv, L0_xattn_Wo)
    x = x + _L0_attn_ref(_layernorm(x, axis=-1), L0_attn_wq_codes, L0_attn_wq_scales, L0_attn_bq, L0_attn_wk_codes, L0_attn_wk_scales, L0_attn_bk, L0_attn_wv_codes, L0_attn_wv_scales, L0_attn_bv, L0_attn_wo_codes, L0_attn_wo_scales, L0_attn_bo)
    x = x + _L0_ffn_ref(_layernorm(x, axis=-1), L0_ffn_gate_w, L0_ffn_gate_bias, L0_ffn_w1, L0_ffn_w2, L0_ffn_w3, L0_ffn_shared_gate, L0_ffn_shared_up, L0_ffn_shared_down)
    return x

_drawn_inputs = setup_inputs


def setup_inputs(seed=0):
    import zlib

    import numpy as np

    out = dict(_drawn_inputs(seed))
    spreads = {'L0_xattn_bg': (1.0, 0.6),
     'L0_attn_bq': (0.0, 0.567),
     'L0_attn_bk': (0.0, 2.0),
     'L0_attn_bv': (0.0, 0.1),
     'L0_attn_bo': (0.0, 0.1)}
    factors = {'L0_xattn_Wq': 46.4,
     'L0_ffn_gate_bias': 36.699,
     'L0_ffn_gate_w': 3.929,
     'L0_ffn_w1': 3.32,
     'L0_ffn_w2': 3.233,
     'L0_ffn_w3': 3.224}
    for name, (base, spread) in spreads.items():
        noise = np.random.default_rng([zlib.crc32(name.encode()), seed]).standard_normal(out[name].shape)
        drawn = base * np.exp(spread * noise) if base else spread * noise
        out[name] = jnp.asarray(drawn.astype(out[name].dtype))
    for name, factor in factors.items():
        out[name] = (out[name] * factor).astype(out[name].dtype)
    return out
```

```python
from contextlib import ExitStack

import concourse.bass as bass
from concourse import mybir

F32 = mybir.dt.float32
F16 = mybir.dt.float16
I32 = mybir.dt.int32
ALU = mybir.AluOpType
ACT = mybir.ActivationFunctionType
AX = mybir.AxisListType

P = 128
B = 32
L = 32
D = 512
S = 257
CC = D // P
T = B * L // P
N = B * L
H = 16
HL = D // H
HG = 4
G = H // HG
E = 32
EG = 4
K = 4
F = 256
CAP = 128
ROUTE_SCALE = 2.0
EPS_LN = 1e-5
EPS_Z = 1e-6
EPS_W = 1e-20
BIG = 3.0e38
HALF = N // 2


class Steps:

    def __init__(self, eng, sem):
        self.eng, self.sem, self.n = eng, sem, 0

    def done(self, ins):
        ins.then_inc(self.sem, 1)
        self.n = self.n + 1

    def wait(self):
        self.eng.wait_ge(self.sem, self.n)


def split_matmuls(pe, out, lhs, rhs, chunks):
    n = len(chunks) * 3
    k = 0
    for c in chunks:
        for a, b in ((0, 0), (0, 1), (1, 0)):
            ins = pe.matmul(out, lhs(a, c), rhs(b, c), start=(k == 0), stop=(k == n - 1))
            k += 1
    return ins


class Norm:

    def __init__(self, nc, ctx, name, xres, ident, xT, banks, keep=None):
        def sb(n, shape, dt=F32):
            return ctx.enter_context(nc.sbuf_tensor(f"{name}_{n}", shape, dt))

        def sem(n):
            return ctx.enter_context(nc.semaphore(f"{name}_{n}"))

        self.xres, self.ident, self.xT, self.banks, self.keep = xres, ident, xT, banks, keep
        self.stats = sb("stats", [P, T, 6])
        self.mv = sb("mv", [P, T, 2])
        self.std = sb("std", [P, T])
        self.rstd = sb("rstd", [P, T])
        self.xn = sb("xn", [P, 2, D]) if keep is None else None
        self.var_ready = sem("var_ready")
        self.std_ready = sem("std_ready")
        self.normed = sem("normed")
        self.turned = sem("turned")
        self.hi_ready = sem("hi_ready")
        self.lo_ready = sem("lo_ready")
        self.steps = sem("dve_steps")

    def buf(self, t, par):
        return self.xn[:, par, :] if self.keep is None else self.keep[:, t, :]

    def vector(self, dve):
        st = Steps(dve, self.steps)
        for t in range(T):
            st.done(dve.bn_stats(self.stats[:, t, :], self.xres[:, t, :]))
        st.wait()
        for t in range(T):
            st.done(dve.bn_aggr(self.mv[:, t, :], self.stats[:, t, :]))
        st.wait()
        dve.tensor_scalar(self.std[:, :], self.mv[:, :, 1], EPS_LN, None, ALU.add).then_inc(self.var_ready, 1)
        dve.wait_ge(self.std_ready, 1)
        st.done(dve.reciprocal(self.rstd[:, :], self.std[:, :]))
        st.wait()

        def norm(t, par, reuse):
            if reuse:
                dve.wait_ge(self.turned, t - 1)
            dve.tensor_scalar(self.buf(t, par), self.xres[:, t, :], self.mv[:, t, 0:1], self.rstd[:, bass.ds(t, 1)],
                              ALU.subtract, ALU.mult).then_inc(self.normed, 1)

        def low(t, par):
            dve.wait_ge(self.hi_ready, t + 1)
            dve.tensor_tensor(self.xT[1][:, :, bass.ds(t * P, P)],
                              self.banks[par][:, :].rearrange("p (c t) -> p c t", c=CC),
                              self.xT[0][:, :, bass.ds(t * P, P)], ALU.subtract).then_inc(self.lo_ready, 1)

        free = self.keep is None
        norm(0, 0, False)
        norm(1, 1, False)
        low(0, 0)
        with dve.Fori(1, T // 2) as i:
            t = dve.snap(i * 2)
            norm(t, 0, free)
            low(t - 1, 1)
            norm(t + 1, 1, free)
            low(t, 0)
        low(T - 1, 1)

    def scalar(self, act):
        act.wait_ge(self.var_ready, 1)
        act.activation(self.std[:, :], self.std[:, :], ACT.Sqrt).then_inc(self.std_ready, 1)
        with act.Fori(0, T // 2) as i:
            for par in range(2):
                t = act.snap(i * 2 + par)
                act.wait_ge(self.turned, t + 1)
                act.activation(self.xT[0][:, :, bass.ds(t * P, P)],
                               self.banks[par][:, :].rearrange("p (c t) -> p c t", c=CC),
                               ACT.Copy).then_inc(self.hi_ready, 1)

    def tensor(self, pe):
        def turn(t, par, reuse):
            pe.wait_ge(self.normed, t + 1)
            if reuse:
                pe.wait_ge(self.lo_ready, t - 1)
            for c in range(CC):
                ins = pe.transpose(self.banks[par][:, c * P:(c + 1) * P],
                                   self.buf(t, par)[:, c * P:(c + 1) * P], self.ident)
            ins.then_inc(self.turned, 1)

        if self.keep is not None:
            for t in range(T):
                turn(t, t % 2, t >= 2)
            return
        turn(0, 0, False)
        turn(1, 1, False)
        with pe.Fori(1, T // 2) as i:
            for par in range(2):
                turn(pe.snap(i * 2 + par), par, True)


def stage_a(nc, a, g):
    xres, xT, ident, pb = g["xres"], g["xT"], g["ident"], g["pb"]
    CM = S - 1
    CT = CM // P
    W1 = P + 1
    with ExitStack() as ctx:
        def sb(n, shape, dt=F32):
            return ctx.enter_context(nc.sbuf_tensor(n, shape, dt))

        def sem(n):
            return ctx.enter_context(nc.semaphore(n))

        raw = {n: sb(f"raw_{n}", [P, CC, w]) for n, w in (("Wq", D), ("Wg", D), ("Wkv", 2 * D), ("Wo", D))}
        w = {n: (sb(f"{n}_hi", [P, CC, r.shape[2]], F16), sb(f"{n}_lo", [P, CC, r.shape[2]], F16))
             for n, r in raw.items()}
        names = ["Wq", "Wg", "Wkv", "Wo"]
        bg = sb("bg", [P, CC])
        qT = sb("qT", [P, CC, N])
        gT = sb("gT", [P, CC, N])
        fneg = sb("fneg", [P, 2, D])
        craw = sb("craw", [P, 2, CC, CM])
        chl = (sb("c_hi", [P, 2, CC, CM], F16), sb("c_lo", [P, 2, CC, CM], F16))
        lraw = sb("lraw", [P, CC, B])
        lhl = (sb("l_hi", [P, CC, B], F16), sb("l_lo", [P, CC, B], F16))
        klast = sb("klast", [B, D])
        klsel = sb("klsel", [B, 2, D])
        vlast = sb("vlast", [B, CC, W1])
        ksb = sb("ksb", [P, 2, CT, D])
        vsb = sb("vsb", [P, 2, CT, CC, W1])
        quad = sb("quad", [P, P])
        kvbd = sb("kvbd", [P, CC, P])
        ksbd = sb("ksbd", [P, CC, P])
        den = sb("den", [P, CC, L])
        rden = sb("rden", [P, CC, L])
        att = sb("att", [P, CC, L])

        x_loaded = sem("x_loaded")
        w_loaded = {n: sem(f"{n}_loaded") for n in names}
        small_loaded = sem("small_loaded")
        w_hi = sem("w_hi")
        w_lo = sem("w_lo")
        last_loaded = sem("last_loaded")
        last_hi = sem("last_hi")
        last_lo = sem("last_lo")
        consts = sem("consts")
        ones_set = sem("ones_set")
        qg_proj = sem("qg_proj")
        q_neg = sem("q_neg")
        q_exp = sem("q_exp")
        q_feat = sem("q_feat")
        g_ready = sem("g_ready")
        kl_proj = sem("kl_proj")
        vl_proj = sem("vl_proj")
        kl_neg = sem("kl_neg")
        kl_exp = sem("kl_exp")
        kl_feat = sem("kl_feat")
        vl_ready = sem("vl_ready")
        ctx_loaded = [sem(f"ctx_loaded{i}") for i in range(2)]
        ctx_hi = sem("ctx_hi")
        ctx_lo = sem("ctx_lo")
        k_proj = sem("k_proj")
        v_proj = sem("v_proj")
        k_neg = sem("k_neg")
        k_exp = sem("k_exp")
        k_feat = sem("k_feat")
        v_ready = sem("v_ready")
        kl_sel = sem("kl_sel")
        kvs_done = sem("kvs_done")
        bd_ready = sem("bd_ready")
        att_done = sem("att_done")
        den_eps = sem("den_eps")
        den_rec = sem("den_rec")
        att_z = sem("att_z")
        att_ready = sem("att_ready")
        att_hi = sem("att_hi")
        att_lo = sem("att_lo")
        o_proj = sem("o_proj")
        o_added = sem("o_added")

        norm = Norm(nc, ctx, "n1", xres, ident, xT, pb)
        block = ctx.enter_context(nc.Block())

        @block.sync
        def _(sp):
            sp.dma_start(xres[:, :, :], a["x"].rearrange("(t p) d -> p t d", p=P)).then_inc(x_loaded, 16)
            sp.dma_start(raw["Wq"][:, :, :], a["Wq"]).then_inc(w_loaded["Wq"], 16)
            sp.dma_start(raw["Wg"][:, :, :], a["Wg"]).then_inc(w_loaded["Wg"], 16)
            sp.dma_start(bg[:, :], a["bg"]).then_inc(small_loaded, 16)
            sp.dma_start(raw["Wkv"][:, :, :], a["Wkv"]).then_inc(w_loaded["Wkv"], 16)
            sp.dma_start(lraw[:, :, :], a["ctx_last"]).then_inc(last_loaded, 16)
            for b in range(2):
                sp.dma_start(craw[:, b, :, :], a["ctx"][b]).then_inc(ctx_loaded[b], 16)
            sp.dma_start(raw["Wo"][:, :, :], a["Wo"]).then_inc(w_loaded["Wo"], 16)
            with sp.Fori(1, B // 2) as i:
                for par in range(2):
                    b = sp.snap(i * 2 + par)
                    sp.wait_ge(ctx_lo, b - 1)
                    sp.dma_start(craw[:, par, :, :], a["ctx"][b]).then_inc(ctx_loaded[par], 16)

        @block.gpsimd
        def _(pool):
            pool.memset(ident[:, :], 0.0).then_inc(consts, 1)
            pool.wait_ge(consts, 1)
            pool.affine_select(out=ident[:, :], in_=ident[:, :], compare_op=ALU.not_equal, fill=1.0, base=0,
                               pattern=[[-1, P]], channel_multiplier=1).then_inc(consts, 1)
            pool.memset(quad[:, :], 0.0).then_inc(consts, 1)
            pool.wait_ge(consts, 3)
            for q in range(4):
                pool.memset(quad[32 * q:32 * q + 32, 32 * q:32 * q + 32], 1.0).then_inc(consts, 1)
            pool.wait_ge(consts, 7)
            pool.memset(vlast[:, :, P:W1], 1.0).then_inc(ones_set, 1)
            pool.wait_ge(ones_set, 1)
            pool.memset(vsb[:, :, :, :, P:W1], 1.0).then_inc(ones_set, 1)

            def low(b, par, reuse):
                pool.wait_ge(ctx_hi, b + 1)
                if reuse:
                    pool.wait_ge(v_proj, CT * (b - 1))
                pool.tensor_tensor(chl[1][:, par, :, :], craw[:, par, :, :], chl[0][:, par, :, :],
                                   ALU.subtract).then_inc(ctx_lo, 1)

            low(0, 0, False)
            low(1, 1, False)
            with pool.Fori(1, B // 2) as i:
                for par in range(2):
                    low(pool.snap(i * 2 + par), par, True)

        @block.scalar
        def _(act):
            act.wait_ge(x_loaded, 16)
            norm.scalar(act)
            for k, n in enumerate(names):
                act.wait_ge(w_loaded[n], 16)
                act.activation(w[n][0][:, :, :], raw[n][:, :, :], ACT.Copy).then_inc(w_hi, 1)
            act.wait_ge(last_loaded, 16)
            act.activation(lhl[0][:, :, :], lraw[:, :, :], ACT.Copy).then_inc(last_hi, 1)

            def q_chunk(j, reuse):
                for half in range(2):
                    n = j * 2 + half
                    act.wait_ge(qg_proj, n + 1)
                    if reuse:
                        act.wait_ge(q_feat, j * 2)
                    act.activation(fneg[:, half, :], pb[half][:, :], ACT.Relu, scale=-1.0).then_inc(q_neg, 1)
                    act.wait_ge(q_neg, n + 1)
                    act.activation(fneg[:, half, :], fneg[:, half, :], ACT.Exp, scale=-1.0).then_inc(q_exp, 1)

            q_chunk(0, False)
            with act.Fori(1, CC) as j:
                q_chunk(j, True)
            act.wait_ge(small_loaded, 16)
            with act.Fori(0, CC) as j:
                for half in range(2):
                    n = act.snap(j * 2 + half)
                    act.wait_ge(qg_proj, n + 2 * CC + 1)
                    act.activation(gT[:, j, half * HALF:(half + 1) * HALF], pb[2 + half][:, :], ACT.Sigmoid,
                                   bias=bg[:, bass.ds(j, 1)]).then_inc(g_ready, 1)

            act.wait_ge(kl_proj, 1)
            act.wait_ge(q_feat, 2 * CC)
            act.activation(fneg[0:B, 0, :], pb[4][0:B, :], ACT.Relu, scale=-1.0).then_inc(kl_neg, 1)
            act.wait_ge(kl_neg, 1)
            act.activation(fneg[0:B, 0, :], fneg[0:B, 0, :], ACT.Exp, scale=-1.0).then_inc(kl_exp, 1)
            act.wait_ge(vl_proj, 1)
            act.activation(vlast[:, :, 0:P], pb[5][0:B, :].rearrange("p (c n) -> p c n", c=CC),
                           ACT.Copy).then_inc(vl_ready, 1)

            def high(b, par, loads, reuse):
                act.wait_ge(ctx_loaded[par], loads)
                if reuse:
                    act.wait_ge(v_proj, CT * (b - 1))
                act.activation(chl[0][:, par, :, :], craw[:, par, :, :], ACT.Copy).then_inc(ctx_hi, 1)

            def tiles(b, par, t, first):
                n = b * CT + t
                act.wait_ge(k_proj, n + 1)
                if first and t == 0 and par == 0:
                    act.wait_ge(kl_feat, 1)
                elif first and par == 0:
                    pass
                else:
                    act.wait_ge(k_feat, n - 1)
                act.activation(fneg[:, t, :], pb[t][:, :], ACT.Relu, scale=-1.0).then_inc(k_neg, 1)
                act.wait_ge(k_neg, n + 1)
                act.activation(fneg[:, t, :], fneg[:, t, :], ACT.Exp, scale=-1.0).then_inc(k_exp, 1)
                act.wait_ge(v_proj, n + 1)
                if not first:
                    act.wait_ge(kvs_done, b - 1)
                act.activation(vsb[:, par, t, :, 0:P], pb[2 + t][:, :].rearrange("p (c n) -> p c n", c=CC),
                               ACT.Copy).then_inc(v_ready, 1)

            def pair(i, first, last):
                for par in range(2):
                    b = act.snap(i * 2 + par) if not first else par
                    tiles(b, par, 0, first)
                    if not (last and par == 1):
                        nb = b + 1
                        if first and par == 0:
                            high(nb, 1, 16, False)
                        elif par == 0:
                            high(nb, 1, i * 16 + 16, True)
                        else:
                            high(nb, 0, i * 16 + 32, True)
                    tiles(b, par, 1, first)

            act.wait_ge(ones_set, 2)
            high(0, 0, 16, False)
            pair(0, True, False)
            with act.Fori(1, B // 2 - 1) as i:
                pair(i, False, False)
            pair(B // 2 - 1, False, True)

            with act.Fori(0, T) as t:
                act.wait_ge(att_ready, B)
                act.activation(xT[0][:, :, bass.ds(t * P, P)], qT[:, :, bass.ds(t * P, P)],
                               ACT.Copy).then_inc(att_hi, 1)

        @block.vector
        def _(dve):
            dve.wait_ge(x_loaded, 16)
            norm.vector(dve)
            for k, n in enumerate(names):
                dve.wait_ge(w_hi, k + 1)
                dve.tensor_tensor(w[n][1][:, :, :], raw[n][:, :, :], w[n][0][:, :, :],
                                  ALU.subtract).then_inc(w_lo, 1)
            dve.wait_ge(last_hi, 1)
            dve.tensor_tensor(lhl[1][:, :, :], lraw[:, :, :], lhl[0][:, :, :], ALU.subtract).then_inc(last_lo, 1)

            with dve.Fori(0, CC) as j:
                for half in range(2):
                    dve.wait_ge(q_exp, j * 2 + (half + 1))
                    dve.scalar_tensor_tensor(out=qT[:, j, half * HALF:(half + 1) * HALF], in0=pb[half][:, :],
                                             scalar=1.0, in1=fneg[:, half, :], op0=ALU.add,
                                             op1=ALU.max).then_inc(q_feat, 1)
            dve.wait_ge(kl_exp, 1)
            dve.scalar_tensor_tensor(out=klast[:, :], in0=pb[4][0:B, :], scalar=1.0, in1=fneg[0:B, 0, :],
                                     op0=ALU.add, op1=ALU.max).then_inc(kl_feat, 1)
            dve.wait_ge(consts, 7)
            dve.wait_ge(kl_feat, 1)

            def select(b, par, reuse):
                if reuse:
                    dve.wait_ge(kvs_done, b - 1)
                dve.tensor_scalar(klsel[:, par, :], klast[:, :], ident[0:B, bass.ds(b, 1)], None,
                                  ALU.mult).then_inc(kl_sel, 1)

            def feature(b, par, t):
                dve.wait_ge(k_exp, b * CT + (t + 1))
                dve.scalar_tensor_tensor(out=ksb[:, par, t, :], in0=pb[t][:, :], scalar=1.0,
                                         in1=fneg[:, t, :], op0=ALU.add, op1=ALU.max).then_inc(k_feat, 1)

            def diagonal(b, reuse):
                dve.wait_ge(kvs_done, b + 1)
                if reuse:
                    dve.wait_ge(att_done, b)
                for u in range(2):
                    kv = pb[4 + u][:, 0:2 * W1].rearrange("p (c n) -> p c n", c=2)
                    m = quad[:, :].unsqueeze(1).to_broadcast([P, 2, P])
                    dve.tensor_tensor(kvbd[:, 2 * u:2 * u + 2, :], kv[:, :, 0:P], m, ALU.mult)
                    ins = dve.tensor_tensor(ksbd[:, 2 * u:2 * u + 2, :],
                                            kv[:, :, P:W1].to_broadcast([P, 2, P]), m, ALU.mult)
                ins.then_inc(bd_ready, 1)

            def output(b):
                num = pb[6][:, 0:P].rearrange("p (c l) -> p c l", c=CC)
                dn = pb[6][:, P:2 * P].rearrange("p (c l) -> p c l", c=CC)
                dve.wait_ge(att_done, b + 1)
                dve.tensor_scalar(den[:, :, :], dn, EPS_Z, None, ALU.add).then_inc(den_eps, 1)
                dve.wait_ge(den_eps, b + 1)
                dve.reciprocal(rden[:, :, :], den[:, :, :]).then_inc(den_rec, 1)
                dve.wait_ge(den_rec, b + 1)
                dve.tensor_tensor(att[:, :, :], num, rden[:, :, :], ALU.mult).then_inc(att_z, 1)
                dve.wait_ge(att_z, b + 1)
                dve.tensor_tensor(qT[:, :, bass.ds(b * L, L)], att[:, :, :], gT[:, :, bass.ds(b * L, L)],
                                  ALU.mult).then_inc(att_ready, 1)

            def pair(i, first):
                for par in range(2):
                    b = dve.snap(i * 2 + par) if not first else par
                    start = first and par == 0
                    select(b, par, not first)
                    feature(b, par, 0)
                    if not start:
                        diagonal(b - 1, not (first and par == 1))
                    feature(b, par, 1)
                    if not start:
                        output(b - 1)

            dve.wait_ge(g_ready, 2 * CC)
            pair(0, True)
            with dve.Fori(1, B // 2) as i:
                pair(i, False)
            diagonal(B - 1, True)
            output(B - 1)

            def low(t):
                dve.wait_ge(att_hi, t + 1)
                dve.tensor_tensor(xT[1][:, :, bass.ds(t * P, P)], qT[:, :, bass.ds(t * P, P)],
                                  xT[0][:, :, bass.ds(t * P, P)], ALU.subtract).then_inc(att_lo, 1)

            def add(t, par):
                dve.wait_ge(o_proj, t + 1)
                dve.tensor_tensor(xres[:, t, :], xres[:, t, :], pb[par][:, :], ALU.add).then_inc(o_added, 1)

            low(0)
            low(1)
            with dve.Fori(1, T // 2) as i:
                for par in range(2):
                    t = dve.snap(i * 2 + par)
                    low(t)
                    add(t - 2, par)
            add(T - 2, 0)
            add(T - 1, 1)

        @block.tensor
        def _(pe):
            pe.wait_ge(consts, 2)
            norm.tensor(pe)
            pe.wait_ge(norm.lo_ready, T)
            for m in range(2):
                pe.wait_ge(w_hi, m + 1)
                pe.wait_ge(w_lo, m + 1)
                ww = w[names[m]]

                def chunk(j, reuse):
                    for half in range(2):
                        if reuse:
                            n = j * 2 + (half - 1)
                            pe.wait_ge(g_ready if m else q_feat, n)
                        split_matmuls(pe, pb[2 * m + half][:, :],
                                      lambda s, c: ww[s][:, c, bass.ds(j * P, P)],
                                      lambda s, c: xT[s][:, c, half * HALF:(half + 1) * HALF],
                                      range(CC)).then_inc(qg_proj, 1)

                chunk(0, False)
                with pe.Fori(1, CC) as j:
                    chunk(j, True)
            pe.wait_ge(w_hi, 3)
            pe.wait_ge(w_lo, 3)
            pe.wait_ge(last_lo, 1)
            wkv = w["Wkv"]

            def kv(out, stat, v):
                return split_matmuls(pe, out, stat, lambda s, c: wkv[s][:, c, v * D:(v + 1) * D], range(CC))

            kv(pb[4][0:B, :], lambda s, c: lhl[s][:, c, :], 0).then_inc(kl_proj, 1)
            kv(pb[5][0:B, :], lambda s, c: lhl[s][:, c, :], 1).then_inc(vl_proj, 1)

            def project(b, par, t, reuse):
                n = b * CT + t
                if t == 0:
                    pe.wait_ge(ctx_lo, b + 1)
                stat = lambda s, c: chl[s][:, par, c, t * P:(t + 1) * P]
                if reuse:
                    pe.wait_ge(k_feat, n - 1)
                kv(pb[t][:, :], stat, 0).then_inc(k_proj, 1)
                if reuse:
                    pe.wait_ge(v_ready, n - 1)
                kv(pb[2 + t][:, :], stat, 1).then_inc(v_proj, 1)

            def summary(b, par, reuse):
                pe.wait_ge(k_feat, CT * b + CT)
                pe.wait_ge(v_ready, CT * b + CT)
                pe.wait_ge(kl_sel, b + 1)
                if reuse:
                    pe.wait_ge(bd_ready, b)
                for c in range(CC):
                    out = pb[4 + c // 2][:, (c % 2) * W1:(c % 2 + 1) * W1]
                    for t in range(CT):
                        pe.matmul(out, ksb[:, par, t, c * P:(c + 1) * P], vsb[:, par, t, c, :],
                                  start=(t == 0), stop=False)
                    ins = pe.matmul(out, klsel[:, par, c * P:(c + 1) * P], vlast[:, c, :],
                                    start=False, stop=True)
                ins.then_inc(kvs_done, 1)

            def attend(b, reuse):
                pe.wait_ge(bd_ready, b + 1)
                if reuse:
                    pe.wait_ge(att_ready, b)
                for c in range(CC):
                    q = qT[:, c, bass.ds(b * L, L)]
                    pe.matmul(pb[6][:, c * L:(c + 1) * L], kvbd[:, c, :], q, start=True, stop=True)
                    ins = pe.matmul(pb[6][:, P + c * L:P + (c + 1) * L], ksbd[:, c, :], q, start=True, stop=True)
                ins.then_inc(att_done, 1)

            def pair(i, first):
                for par in range(2):
                    b = pe.snap(i * 2 + par) if not first else par
                    start = first and par == 0
                    project(b, par, 0, not start)
                    if not start:
                        summary(b - 1, 1 - par, not (first and par == 1))
                    project(b, par, 1, not start)
                    if not start:
                        attend(b - 1, not (first and par == 1))

            pe.wait_ge(q_feat, 2 * CC)
            pe.wait_ge(g_ready, 2 * CC)
            pe.wait_ge(vl_ready, 1)
            pe.wait_ge(kl_feat, 1)
            pair(0, True)
            with pe.Fori(1, B // 2) as i:
                pair(i, False)
            summary(B - 1, 1, True)
            attend(B - 1, True)

            pe.wait_ge(w_lo, 4)

            def out_proj(t, par, reuse):
                pe.wait_ge(att_lo, t + 1)
                if reuse:
                    pe.wait_ge(o_added, t - 1)
                split_matmuls(pe, pb[par][:, :], lambda s, c: xT[s][:, c, bass.ds(t * P, P)],
                              lambda s, c: w["Wo"][s][:, c, :], range(CC)).then_inc(o_proj, 1)

            out_proj(0, 0, False)
            out_proj(1, 1, False)
            with pe.Fori(1, T // 2) as i:
                for par in range(2):
                    out_proj(pe.snap(i * 2 + par), par, True)


def stage_b(nc, a, g):
    xres, xT, ident, pb, psum = g["xres"], g["xT"], g["ident"], g["pb"], g["psum"]
    SCALE = float(P) ** -0.5
    GT = HG * P
    with ExitStack() as ctx:
        def sb(n, shape, dt=F32):
            return ctx.enter_context(nc.sbuf_tensor(n, shape, dt))

        def sem(n):
            return ctx.enter_context(nc.semaphore(n))

        bq, bk, bv = (sb(n + "_sb", [P, H]) for n in ("bq", "bk", "bv"))
        bo = sb("bo_sb", [P, D])
        zero = sb("zero", [P, D])
        qk_raw = sb("qk_raw", [P, 2, 2 * CC * P])
        qk_sc = sb("qk_sc", [P, 2, 2 * CC * P])
        qk_w = tuple(sb(f"qk_w_{s}", [P, 2, 2, CC, P], F16) for s in ("hi", "lo"))
        v_raw, v_sc = sb("v_raw", [P, CC * GT]), sb("v_sc", [P, CC * GT])
        v_w = tuple(sb(f"v_w_{s}", [P, CC, GT], F16) for s in ("hi", "lo"))
        o_raw, o_sc = sb("o_raw", [P, HG * D]), sb("o_sc", [P, HG * D])
        o_w = tuple(sb(f"o_w_{s}", [P, HG, D], F16) for s in ("hi", "lo"))
        qT, kT = sb("qT_h", [P, N]), sb("kT_h", [P, N])
        vsb = sb("v_g", [P, T, GT])
        sc = sb("scores", [P, T, L])
        smax, ssum, srec = sb("smax", [P, T]), sb("ssum", [P, T]), sb("srec", [P, T])
        pT = sb("pT", [P, T, P])
        oT = tuple(sb(f"oT_{s}", [P, HG, N], F16) for s in ("hi", "lo"))

        bias_loaded = sem("bias_loaded")
        qk_loaded = [sem(f"qk_loaded{i}") for i in range(2)]
        v_loaded = sem("v_loaded")
        o_loaded = sem("o_loaded")
        qk_deq = sem("qk_deq")
        qk_hi = sem("qk_hi")
        qk_lo = sem("qk_lo")
        v_deq = sem("v_deq")
        vw_hi = sem("vw_hi")
        vw_lo = sem("vw_lo")
        o_deq = sem("o_deq")
        ow_hi = sem("ow_hi")
        ow_lo = sem("ow_lo")
        bo_added = sem("bo_added")
        zeroed = sem("zeroed")
        xbuf_zeroed = sem("xbuf_zeroed")
        v_proj = sem("b_v_proj")
        v_evac = sem("v_evac")
        q_proj = sem("b_q_proj")
        q_evac = sem("q_evac")
        k_proj = sem("b_k_proj")
        k_evac = sem("k_evac")
        s_done = sem("s_done")
        s_evac = sem("s_evac")
        s_steps = sem("s_steps")
        s_shift = sem("s_shift")
        s_exp = sem("s_exp")
        pt_ready = sem("pt_ready")
        pv_done = sem("pv_done")
        o_hi = sem("o_hi")
        o_lo = sem("o_lo")
        o_proj = sem("b_o_proj")
        o_added = sem("b_o_added")

        norm = Norm(nc, ctx, "n2", xres, ident, xT, pb)
        S2 = psum[:, 4:6, :].rearrange("p b (t k) -> p (b t) k", k=P)
        O2 = psum[:, 6:8, :].rearrange("p b n -> p (b n)")
        block = ctx.enter_context(nc.Block())

        @block.sync
        def _(sp):
            for dst, n in ((bq, "bq"), (bk, "bk"), (bv, "bv")):
                sp.dma_start(dst[:, :], a[n]).then_inc(bias_loaded, 16)
            sp.dma_start(bo[:, :], a["bo"].to_broadcast([P, D])).then_inc(bias_loaded, 16)

            def scales(dst, src, s):
                for q in range(4):
                    sp.dma_start(dst[32 * q:32 * q + 32, :], src[q:q + 1, :].to_broadcast([32, dst.shape[1]])
                                 ).then_inc(s, 16)

            def load_v(gr):
                sp.dma_start(v_raw[:, :], a["v_codes"][gr]).then_inc(v_loaded, 16)
                scales(v_sc[:, :], a["v_scales"][gr], v_loaded)

            def load_o(gr):
                sp.dma_start(o_raw[:, :], a["o_codes"][gr]).then_inc(o_loaded, 16)
                scales(o_sc[:, :], a["o_scales"][gr], o_loaded)

            def load_qk(h, par):
                sp.dma_start(qk_raw[:, par, :], a["qk_codes"][h]).then_inc(qk_loaded[par], 16)
                scales(qk_sc[:, par, :], a["qk_scales"][h], qk_loaded[par])

            load_v(0)
            load_qk(0, 0)
            load_qk(1, 1)
            load_o(0)
            for e in range(4):
                sp.dma_start(g["w13"][:, e, :, :], a["w13"][e]).then_inc(g["ew_loaded"][e], 16)
                sp.dma_start(g["w2"][:, e, :, :], a["w2"][e]).then_inc(g["ew_loaded"][e], 16)
            sp.wait_ge(zeroed, 2)
            RT = 8
            for i in range(E // RT):
                dst = g["xbuf"].rearrange("(i r p) d -> i p r d", r=RT, p=P)[i]
                sp.dma_start(dst, zero[:, :].unsqueeze(1).to_broadcast([P, RT, D])).then_inc(xbuf_zeroed, 16)

            def group(gr, last):
                for j in range(HG):
                    if last and j >= HG - 2:
                        break
                    h = gr * HG + j
                    sp.wait_ge(qk_lo, h + 1)
                    load_qk(h + 2, j % 2)
                    if j == 1 and not last:
                        sp.wait_ge(vw_lo, gr + 1)
                        load_v(gr + 1)
                if not last:
                    sp.wait_ge(ow_lo, gr + 1)
                    load_o(gr + 1)

            with sp.Fori(0, G - 1) as gr:
                group(gr, False)
            group(G - 1, True)
            sp.wait_ge(xbuf_zeroed, 16 * (E // RT))

        @block.gpsimd
        def _(pool):
            pool.memset(pT[:, :, :], 0.0).then_inc(zeroed, 1)
            pool.memset(zero[:, :], 0.0).then_inc(zeroed, 1)
            pool.wait_ge(zeroed, 2)

            def dequant(w, s, hi, lo, loaded, lval, deq, hi_sem, lo_sem, n, mm, mval):
                pool.wait_ge(loaded, lval)
                pool.tensor_tensor(w, w, s, ALU.mult).then_inc(deq, 1)
                pool.wait_ge(deq, n + 1)
                pool.wait_ge(hi_sem, n + 1)
                if mval is not None:
                    pool.wait_ge(mm, mval)
                pool.tensor_tensor(lo, w, hi, ALU.subtract).then_inc(lo_sem, 1)

            def flat(t):
                return t.rearrange("p a c n -> p (a c n)") if len(t.shape) == 4 else t.rearrange("p c n -> p (c n)")

            def v_part(gr, first):
                dequant(v_raw[:, :], v_sc[:, :], flat(v_w[0][:, :, :]), flat(v_w[1][:, :, :]), v_loaded,
                        gr * 80 + 80, v_deq, vw_hi, vw_lo, gr, v_proj, None if first else gr * T)

            def o_part(gr, first):
                dequant(o_raw[:, :], o_sc[:, :], flat(o_w[0][:, :, :]), flat(o_w[1][:, :, :]), o_loaded,
                        gr * 80 + 80, o_deq, ow_hi, ow_lo, gr, o_proj, None if first else gr * T)

            def qk_part(h, par, lval, first):
                dequant(qk_raw[:, par, :], qk_sc[:, par, :], flat(qk_w[0][:, par]), flat(qk_w[1][:, par]),
                        qk_loaded[par], lval, qk_deq, qk_hi, qk_lo, h, k_proj, None if first else h * 2 - 2)

            v_part(0, True)
            qk_part(0, 0, 80, True)
            pool.wait_ge(norm.normed, T)
            pool.wait_ge(bias_loaded, 64)
            for t in range(T):
                pool.tensor_tensor(xres[:, t, :], xres[:, t, :], bo[:, :], ALU.add).then_inc(bo_added, 1)
            def group(gr, heads, first, last):
                for j in heads:
                    qk_part(gr * HG + j, j % 2, gr * 160 + 80 * (j // 2 + 1), first and j < 2)
                    if j == 1:
                        o_part(gr, first)
                if not last:
                    v_part(gr + 1, False)

            group(0, range(1, HG), True, False)
            with pool.Fori(1, G - 1) as gr:
                group(gr, range(HG), False, False)
            group(G - 1, range(HG), False, True)

        @block.scalar
        def _(act):
            norm.scalar(act)

            def high(dst, src, deq, n, hi_sem, mm, mval):
                act.wait_ge(deq, n + 1)
                if mval is not None:
                    act.wait_ge(mm, mval)
                act.activation(dst, src, ACT.Copy).then_inc(hi_sem, 1)

            def v_part(gr, first):
                high(v_w[0][:, :, :].rearrange("p c n -> p (c n)"), v_raw[:, :], v_deq, gr, vw_hi, v_proj,
                     None if first else gr * T)

            def o_part(gr, first):
                high(o_w[0][:, :, :].rearrange("p c n -> p (c n)"), o_raw[:, :], o_deq, gr, ow_hi, o_proj,
                     None if first else gr * T)

            def qk_part(h, par, first):
                high(qk_w[0][:, par].rearrange("p a c n -> p (a c n)"), qk_raw[:, par, :], qk_deq, h, qk_hi,
                     k_proj, None if first else h * 2 - 2)

            def evac_q(h):
                act.wait_ge(q_proj, h + 1)
                act.activation(qT[:, :], psum[:, 0:2, :].rearrange("p b n -> p (b n)"), ACT.Identity,
                               bias=bq[:, bass.ds(h, 1)]).then_inc(q_evac, 1)

            def softmax(h):
                act.wait_ge(s_done, h + 1)
                for q in range(4):
                    r = slice(32 * q, 32 * q + 32)
                    ins = act.activation(sc[r, :, :], S2[r, :, r], ACT.Copy)
                ins.then_inc(s_evac, 1)
                act.wait_ge(s_shift, h + 1)
                act.activation(sc[:, :, :], sc[:, :, :], ACT.Exp, scale=SCALE).then_inc(s_exp, 1)

            def evac_o(h, j):
                act.wait_ge(pv_done, h + 1)
                act.activation(oT[0][:, j, :], O2, ACT.Identity, bias=bv[:, bass.ds(h, 1)]).then_inc(o_hi, 1)

            act.wait_ge(bias_loaded, 64)
            v_part(0, True)
            qk_part(0, 0, True)

            def group(gr, first, last):
                for t in range(T):
                    act.wait_ge(v_proj, gr * T + (t + 1))
                    act.activation(vsb[:, t, :], pb[t % 4][:, :], ACT.Copy).then_inc(v_evac, 1)
                for j in range(HG):
                    h = gr * HG + j
                    if j == 0:
                        evac_q(h)
                    if not (last and j == HG - 1):
                        qk_part(h + 1, (j + 1) % 2, first and j == 0)
                    softmax(h)
                    if j == 0:
                        o_part(gr, first)
                    if j < HG - 1:
                        evac_q(h + 1)
                    evac_o(h, j)
                    if j == 2 and not last:
                        v_part(gr + 1, False)

            group(0, True, False)
            with act.Fori(1, G - 1) as gr:
                group(gr, False, False)
            group(G - 1, False, True)

        @block.vector
        def _(dve):
            norm.vector(dve)
            st = Steps(dve, s_steps)
            dve.wait_ge(bias_loaded, 64)
            dve.wait_ge(zeroed, 1)
            dve.wait_ge(bo_added, T)

            def evac_k(h):
                for half in range(2):
                    dve.wait_ge(k_proj, h * 2 + (half + 1))
                    dve.tensor_scalar(kT[:, half * HALF:(half + 1) * HALF], pb[2 + half][:, :],
                                      bk[:, bass.ds(h, 1)], None, ALU.add).then_inc(k_evac, 1)

            def softmax(h):
                st.n = h * 4
                dve.wait_ge(s_evac, h + 1)
                st.done(dve.tensor_reduce(smax[:, :], sc[:, :, :], AX.X, ALU.max))
                st.wait()
                dve.tensor_tensor(sc[:, :, :], sc[:, :, :], smax[:, :].unsqueeze(2).to_broadcast([P, T, L]),
                                  ALU.subtract).then_inc(s_shift, 1)
                dve.wait_ge(s_exp, h + 1)
                st.done(dve.tensor_reduce(ssum[:, :], sc[:, :, :], AX.X, ALU.add))
                st.wait()
                st.done(dve.reciprocal(srec[:, :], ssum[:, :]))
                st.wait()
                st.done(dve.tensor_tensor(sc[:, :, :], sc[:, :, :],
                                          srec[:, :].unsqueeze(2).to_broadcast([P, T, L]), ALU.mult))
                st.wait()
                for q in range(4):
                    r = slice(32 * q, 32 * q + 32)
                    ins = dve.transpose(pT[r, :, r], sc[r, :, :])
                ins.then_inc(pt_ready, 1)

            def evac_o(h, j):
                dve.wait_ge(o_hi, h + 1)
                dve.scalar_tensor_tensor(out=oT[1][:, j, :], in0=O2, scalar=bv[:, bass.ds(h, 1)],
                                         in1=oT[0][:, j, :], op0=ALU.add, op1=ALU.subtract).then_inc(o_lo, 1)

            with dve.Fori(0, G) as gr:
                for j in range(HG):
                    h = dve.snap(gr * HG + j)
                    if j == 0:
                        evac_k(h)
                    softmax(h)
                    if j < HG - 1:
                        evac_k(h + 1)
                    evac_o(h, j)
                for t in range(T):
                    dve.wait_ge(o_proj, gr * T + (t + 1))
                    dve.tensor_tensor(xres[:, t, :], xres[:, t, :], pb[t % 4][:, :], ALU.add).then_inc(o_added, 1)

        @block.tensor
        def _(pe):
            norm.tensor(pe)
            pe.wait_ge(norm.lo_ready, T)

            def v_tiles(gr, first):
                pe.wait_ge(vw_lo, gr + 1)
                for t in range(T):
                    if t >= 4:
                        pe.wait_ge(v_evac, gr * T + (t - 3))
                    elif not first:
                        pe.wait_ge(o_added, gr * T + (t - 3))
                    split_matmuls(pe, pb[t % 4][:, :], lambda s, c: xT[s][:, c, t * P:(t + 1) * P],
                                  lambda s, c: v_w[s][:, c, :], range(CC)).then_inc(v_proj, 1)

            def qk(h, par, after_v, gr):
                pe.wait_ge(qk_lo, h + 1)
                if after_v:
                    pe.wait_ge(v_evac, gr * T + T)
                for m in range(2):
                    for half in range(2):
                        ins = split_matmuls(pe, pb[2 * m + half][:, :], lambda s, c: qk_w[s][:, par, m, c, :],
                                            lambda s, c: xT[s][:, c, half * HALF:(half + 1) * HALF], range(CC))
                        if m:
                            ins.then_inc(k_proj, 1)
                    if not m:
                        ins.then_inc(q_proj, 1)

            def scores(h, first):
                pe.wait_ge(q_evac, h + 1)
                pe.wait_ge(k_evac, h * 2 + 2)
                if not (first and h == 0):
                    pe.wait_ge(s_evac, h)
                for t in range(T):
                    r = slice(t * P, (t + 1) * P)
                    ins = pe.matmul(S2[:, t, :], qT[:, r], kT[:, r], start=True, stop=True)
                ins.then_inc(s_done, 1)

            def values(h, j, first):
                pe.wait_ge(pt_ready, h + 1)
                if not (first and h == 0):
                    pe.wait_ge(o_lo, h)
                for t in range(T):
                    ins = pe.matmul(O2[:, t * P:(t + 1) * P], vsb[:, t, j * P:(j + 1) * P], pT[:, t, :],
                                    start=True, stop=True)
                ins.then_inc(pv_done, 1)

            def out_part(gr, t, heads):
                for j in heads:
                    for s, (u, v) in enumerate(((0, 0), (0, 1), (1, 0))):
                        ins = pe.matmul(pb[t % 4][:, :], oT[u][:, j, t * P:(t + 1) * P], o_w[v][:, j, :],
                                        start=(j == 0 and s == 0), stop=(j == HG - 1 and s == 2))
                return ins

            def group(gr, first):
                v_tiles(gr, first)
                qk(gr * HG, 0, True, gr)
                for j in range(HG):
                    h = gr * HG + j
                    scores(h, first)
                    if j < HG - 1:
                        qk(h + 1, (j + 1) % 2, False, gr)
                    else:
                        pe.wait_ge(ow_lo, gr + 1)
                        pe.wait_ge(o_lo, h)
                        for t in range(4):
                            out_part(gr, t, range(HG - 1))
                    values(h, j, first)
                pe.wait_ge(o_lo, gr * HG + HG)
                for t in range(4):
                    out_part(gr, t, [HG - 1]).then_inc(o_proj, 1)
                for t in range(4, T):
                    pe.wait_ge(o_added, gr * T + (t - 3))
                    out_part(gr, t, range(HG)).then_inc(o_proj, 1)

            group(0, True)
            with pe.Fori(1, G) as gr:
                group(gr, False)


def stage_c(nc, a, g):
    xres, xT, ident, pb, psum = g["xres"], g["xT"], g["ident"], g["pb"], g["psum"]
    w13, w2, ew_loaded = g["w13"], g["w2"], g["ew_loaded"]
    xbuf, ybuf, out = g["xbuf"], g["ybuf"], g["out"]
    FC = F // P
    PAD = 8
    LAST = E // 4 - 1
    with ExitStack() as ctx:
        def sb(n, shape, dt=F32):
            return ctx.enter_context(nc.sbuf_tensor(n, shape, dt))

        def sem(n):
            return ctx.enter_context(nc.semaphore(n))

        x3 = sb("x3", [P, T, D])
        names = ["sg", "su", "sd"]
        raw = {n: sb(f"raw_{n}", [P, CC, D]) for n in names}
        w = {n: (sb(f"{n}_hi", [P, CC, D], F16), sb(f"{n}_lo", [P, CC, D], F16)) for n in names}
        gw_raw = sb("gw_raw", [P, CC, E])
        gw = (sb("gw_hi", [P, CC, E], F16), sb("gw_lo", [P, CC, E], F16))
        gb = sb("gb", [P, E])
        tri, tri_f = sb("tri", [P, P], F16), sb("tri_f", [P, P])
        ones = sb("ones16", [P, P], F16)
        e256i, e256 = sb("e256i", [P, E], I32), sb("e256", [P, E])
        score = sb("score", [P, T, E])
        biased = sb("biased", [P, T, E])
        m8 = sb("m8", [P, T * EG, 8])
        gs = sb("gs", [P, T, EG + PAD])
        gm8 = sb("gm8", [P, T, 8])
        gsel = sb("gsel", [P, T, EG + PAD])
        gmask = sb("gmask", [P, T, EG])
        tmp = sb("tmp", [P, T, E + PAD])
        em8 = sb("em8", [P, T, 8])
        esel = sb("esel", [P, T, E + PAD])
        chosen = sb("chosen", [P, T, E])
        chosen16 = sb("chosen16", [P, T, E], F16)
        wt = sb("wt", [P, T, E])
        wsum = sb("wsum", [P, T])
        pos = sb("pos", [P, T, E])
        keep = sb("keep", [P, T, E])
        key = sb("key", [P, T, E])
        k8 = sb("k8", [P, T, 8])
        eq = sb("eq", [P, T, K, E])
        wtok = sb("wtok", [P, T, K])
        ki, kp, ke, kd = (sb(n, [P, T, K], I32) for n in ("ki", "kp", "ke", "kd"))
        scat, gath = sb("scat", [P, T, K], I32), sb("gath", [P, T, K], I32)
        ssil, sup, sh = sb("ssil", [P, D]), sb("sup", [P, D]), sb("sh", [P, D])
        sT = tuple(sb(f"sT_{s}", [P, CC, N], F16) for s in ("hi", "lo"))
        xe = sb("xe", [P, 2, D])
        xeT = sb("xeT", [P, CC, P])
        hsil, hh = sb("hsil", [P, F]), sb("hh", [P, F])
        hT = sb("hT", [P, FC, P])
        y = sb("y", [P, 2, D])

        sh_loaded = {n: sem(f"{n}_loaded") for n in names}
        gw_loaded = sem("gw_loaded")
        w_hi = sem("c_w_hi")
        w_lo = sem("c_w_lo")
        consts = sem("c_consts")
        logits = sem("logits")
        score_ready = sem("score_ready")
        r_steps = sem("r_steps")
        chosen_ready = sem("chosen_ready")
        pos_done = sem("pos_done")
        idx_ready = sem("idx_ready")
        scattered = sem("scattered")
        sg_proj = sem("sg_proj")
        su_proj = sem("su_proj")
        s_silu = sem("s_silu")
        s_up = sem("s_up")
        s_h = sem("s_h")
        s_hi = sem("s_hi")
        s_lo = sem("s_lo")
        sd_proj = sem("sd_proj")
        s_added = sem("s_added")
        xe_loaded = [sem(f"xe_loaded{i}") for i in range(2)]
        xe_turned = sem("xe_turned")
        xeT_ready = sem("xeT_ready")
        up_done = sem("up_done")
        e_silu = sem("e_silu")
        h_ready = sem("h_ready")
        h_turned = sem("h_turned")
        hT_ready = sem("hT_ready")
        down_done = sem("down_done")
        y_ready = sem("y_ready")
        y_stored = [sem(f"y_stored{i}") for i in range(2)]
        gathered = [sem(f"gathered{i}") for i in range(T)]
        combined = sem("combined")
        out_stored = sem("out_stored")

        norm = Norm(nc, ctx, "n3", xres, ident, xT, pb, keep=x3)
        LG = pb[6][:, 0:T * E].rearrange("p (t e) -> p t e", e=E)
        PS = pb[7][:, 0:T * E].rearrange("p (t e) -> p t e", e=E)
        block = ctx.enter_context(nc.Block())

        @block.sync
        def _(sp):
            sp.dma_start(gw_raw[:, :, :], a["gate_w"]).then_inc(gw_loaded, 16)
            sp.dma_start(gb[:, :], a["gate_bias"].to_broadcast([P, E])).then_inc(gw_loaded, 16)
            for n in names:
                sp.dma_start(raw[n][:, :, :], a[n]).then_inc(sh_loaded[n], 16)
            sp.wait_ge(scattered, 16 * T * K)
            for e in range(2):
                sp.dma_start(xe[:, e, :], xbuf[e * CAP:(e + 1) * CAP, :]).then_inc(xe_loaded[e], 16)

            def loads(i, q, first, last):
                e = i * 4 + q
                if not (last and q >= 2):
                    sp.wait_ge(xe_turned, e + 1)
                    sp.dma_start(xe[:, q % 2, :], xbuf[bass.ds((e + 2) * CAP, CAP), :]
                                 ).then_inc(xe_loaded[q % 2], 16)
                if (first and q == 0) or (last and q >= 1):
                    return
                sp.wait_ge(down_done, e)
                slot = (q + 3) % 4
                sp.dma_start(w13[:, slot, :, :], a["w13"][e + 3]).then_inc(ew_loaded[slot], 16)
                sp.dma_start(w2[:, slot, :, :], a["w2"][e + 3]).then_inc(ew_loaded[slot], 16)

            for q in range(4):
                loads(0, q, True, False)
            with sp.Fori(1, LAST) as i:
                for q in range(4):
                    loads(i, q, False, False)
            for q in range(4):
                loads(LAST, q, False, True)
            o = out.rearrange("(t p) d -> t p d", p=P)
            for t in range(T):
                sp.wait_ge(combined, K * (t + 1))
                sp.dma_start(o[t], xres[:, t, :]).then_inc(out_stored, 16)
            sp.wait_ge(out_stored, 16 * T)

        @block.gpsimd
        def _(pool):
            pool.memset(tri_f[:, :], 1.0).then_inc(consts, 1)
            pool.wait_ge(consts, 1)
            pool.affine_select(out=tri_f[:, :], in_=tri_f[:, :], compare_op=ALU.is_gt, fill=0.0, base=0,
                               pattern=[[1, P]], channel_multiplier=-1).then_inc(consts, 1)
            pool.wait_ge(consts, 2)
            pool.tensor_copy(tri[:, :], tri_f[:, :]).then_inc(consts, 1)
            pool.memset(ones[:, :], 1.0).then_inc(consts, 1)
            pool.iota(e256i[:, :], [[2 * CAP, E]], base=1, channel_multiplier=0).then_inc(consts, 1)
            pool.wait_ge(consts, 5)
            pool.tensor_copy(e256[:, :], e256i[:, :]).then_inc(consts, 1)

            def shared_half(j, half, first):
                n = j * 2 + half
                if not first:
                    pool.wait_ge(s_lo, n)
                pool.wait_ge(s_up, n + 1)
                pool.tensor_tensor(sh[:, :], ssil[:, :], sup[:, :], ALU.mult).then_inc(s_h, 1)
                pool.wait_ge(s_hi, n + 1)
                pool.tensor_tensor(sT[1][:, j, half * HALF:(half + 1) * HALF], sh[:, :],
                                   sT[0][:, j, half * HALF:(half + 1) * HALF], ALU.subtract).then_inc(s_lo, 1)

            shared_half(0, 0, True)
            shared_half(0, 1, False)
            with pool.Fori(1, CC) as j:
                shared_half(j, 0, False)
                shared_half(j, 1, False)
            pool.wait_ge(idx_ready, 2)
            for t in range(T):
                for k in range(K):
                    pool.indirect_dma_start(xbuf, bass.IndirectOffsetOnAxis(ap=scat[:, t, k:k + 1], axis=0),
                                            x3[:, t, :], None, bounds_check=E * CAP - 1,
                                            oob_is_err=False).then_inc(scattered, 16)
            with pool.Fori(0, E // 2) as i:
                for q in range(2):
                    e = pool.snap(i * 2 + q)
                    pool.wait_ge(y_ready, e + 1)
                    pool.dma_start(ybuf[bass.ds(e * CAP, CAP), :], y[:, q, :]).then_inc(y_stored[q], 16)
            for q in range(2):
                pool.wait_ge(y_stored[q], 16 * E // 2)
            pool.wait_ge(scattered, 16 * T * K)
            for n in range(T * K):
                if n >= T:
                    pool.wait_ge(combined, n - T + 1)
                pool.indirect_dma_start(x3[:, n % T, :], None, ybuf,
                                        bass.IndirectOffsetOnAxis(ap=gath[:, n // K, n % K:n % K + 1], axis=0)
                                        ).then_inc(gathered[n % T], 16)

        @block.scalar
        def _(act):
            norm.scalar(act)
            act.wait_ge(gw_loaded, 32)
            act.activation(gw[0][:, :, :], gw_raw[:, :, :], ACT.Copy).then_inc(w_hi, 1)
            for n in names:
                act.wait_ge(sh_loaded[n], 16)
                act.activation(w[n][0][:, :, :], raw[n][:, :, :], ACT.Copy).then_inc(w_hi, 1)
            act.wait_ge(logits, 1)
            act.activation(score[:, :, :], LG, ACT.Sigmoid).then_inc(score_ready, 1)

            def shared_half(j, half, first):
                n = j * 2 + half
                act.wait_ge(sg_proj, n + 1)
                if not first:
                    act.wait_ge(s_h, n)
                act.activation(ssil[:, :], pb[half][:, :], ACT.Silu).then_inc(s_silu, 1)
                act.wait_ge(su_proj, n + 1)
                act.activation(sup[:, :], pb[2 + half][:, :], ACT.Copy).then_inc(s_up, 1)
                act.wait_ge(s_h, n + 1)
                act.activation(sT[0][:, j, half * HALF:(half + 1) * HALF], sh[:, :], ACT.Copy).then_inc(s_hi, 1)

            shared_half(0, 0, True)
            shared_half(0, 1, False)
            with act.Fori(1, CC) as j:
                shared_half(j, 0, False)
                shared_half(j, 1, False)

            def expert(i, q, first):
                e = i * 4 + q
                act.wait_ge(up_done, e + 1)
                if not (first and q == 0):
                    act.wait_ge(h_ready, e)
                act.activation(hsil[:, :], pb[1][:, 0:F], ACT.Silu).then_inc(e_silu, 1)
                act.wait_ge(h_turned, e + 1)
                act.activation(hT[:, :, :], pb[3][:, 0:F].rearrange("p (c n) -> p c n", c=FC),
                               ACT.Copy).then_inc(hT_ready, 1)
                act.wait_ge(down_done, e + 1)
                if not (first and q < 2):
                    act.wait_ge(y_stored[q % 2], i * 32 + 16 * (q // 2))
                act.activation(y[:, q % 2, :], pb[6][:, :], ACT.Copy).then_inc(y_ready, 1)

            for q in range(4):
                expert(0, q, True)
            with act.Fori(1, E // 4) as i:
                for q in range(4):
                    expert(i, q, False)

        @block.vector
        def _(dve):
            norm.vector(dve)
            st = Steps(dve, r_steps)

            def then(ins):
                st.done(ins)
                st.wait()

            dve.wait_ge(w_hi, 1)
            dve.tensor_tensor(gw[1][:, :, :], gw_raw[:, :, :], gw[0][:, :, :], ALU.subtract).then_inc(w_lo, 1)
            for k, n in enumerate(names):
                dve.wait_ge(w_hi, k + 2)
                dve.tensor_tensor(w[n][1][:, :, :], raw[n][:, :, :], w[n][0][:, :, :],
                                  ALU.subtract).then_inc(w_lo, 1)
            st.done(dve.memset(gs[:, :, EG:EG + PAD], -BIG))
            st.done(dve.memset(tmp[:, :, E:E + PAD], -BIG))
            dve.wait_ge(score_ready, 1)
            then(dve.tensor_tensor(biased[:, :, :], score[:, :, :],
                                   gb[:, :].unsqueeze(1).to_broadcast([P, T, E]), ALU.add))
            per = E // EG
            for t in range(T):
                for gr in range(EG):
                    st.done(dve.max(m8[:, t * EG + gr, :], biased[:, t, gr * per:(gr + 1) * per]))
            st.wait()
            m8v = m8[:, :, :].rearrange("p (t g) k -> p t g k", g=EG)
            then(dve.tensor_tensor(gs[:, :, 0:EG], m8v[:, :, :, 0], m8v[:, :, :, 1], ALU.add))
            for t in range(T):
                st.done(dve.max(gm8[:, t, :], gs[:, t, :]))
            st.wait()
            then(dve.memset(gm8[:, :, 2:8], -BIG))
            for t in range(T):
                st.done(dve.match_replace(gsel[:, t, :], gm8[:, t, :], gs[:, t, :], BIG))
            st.wait()
            then(dve.tensor_scalar(gmask[:, :, :], gsel[:, :, 0:EG], BIG, None, ALU.is_equal))
            then(dve.tensor_tensor(tmp[:, :, 0:E].rearrange("p t (g n) -> p t g n", g=EG),
                                   biased[:, :, :].rearrange("p t (g n) -> p t g n", g=EG),
                                   gmask[:, :, :].unsqueeze(3).to_broadcast([P, T, EG, per]), ALU.mult))
            then(dve.tensor_scalar(tmp[:, :, 0:E], tmp[:, :, 0:E], 0.0, None, ALU.add))
            for t in range(T):
                st.done(dve.max(em8[:, t, :], tmp[:, t, 0:E]))
            st.wait()
            then(dve.memset(em8[:, :, K:8], -BIG))
            for t in range(T):
                st.done(dve.match_replace(esel[:, t, :], em8[:, t, :], tmp[:, t, :], BIG))
            st.wait()
            then(dve.tensor_scalar(chosen[:, :, :], esel[:, :, 0:E], BIG, None, ALU.is_equal))
            dve.tensor_copy(chosen16[:, :, :], chosen[:, :, :]).then_inc(chosen_ready, 1)
            then(dve.tensor_tensor(wt[:, :, :], score[:, :, :], chosen[:, :, :], ALU.mult))
            then(dve.tensor_reduce(wsum[:, :], wt[:, :, :], AX.X, ALU.add))
            then(dve.tensor_scalar(wsum[:, :], wsum[:, :], EPS_W, None, ALU.add))
            then(dve.reciprocal(wsum[:, :], wsum[:, :]))
            then(dve.tensor_scalar(wsum[:, :], wsum[:, :], ROUTE_SCALE, None, ALU.mult))
            then(dve.tensor_tensor(wt[:, :, :], wt[:, :, :], wsum[:, :].unsqueeze(2).to_broadcast([P, T, E]),
                                   ALU.mult))
            dve.wait_ge(pos_done, 1)
            dve.wait_ge(consts, 6)
            st.done(dve.tensor_scalar(keep[:, :, :], PS, float(CAP), None, ALU.is_lt))
            then(dve.tensor_scalar(pos[:, :, :], PS, float(CAP), None, ALU.min))
            st.done(dve.tensor_tensor(wt[:, :, :], wt[:, :, :], keep[:, :, :], ALU.mult))
            then(dve.tensor_tensor(pos[:, :, :], pos[:, :, :],
                                   e256[:, :].unsqueeze(1).to_broadcast([P, T, E]), ALU.add))
            then(dve.tensor_tensor(key[:, :, :], pos[:, :, :], chosen[:, :, :], ALU.mult))
            for t in range(T):
                st.done(dve.max(k8[:, t, :], key[:, t, :]))
            st.wait()
            then(dve.tensor_scalar(ki[:, :, :], k8[:, :, 0:K], -1.0, None, ALU.add))
            st.done(dve.tensor_scalar(ke[:, :, :], ki[:, :, :], 8, 7, ALU.logical_shift_right,
                                      ALU.logical_shift_left))
            then(dve.tensor_scalar(kp[:, :, :], ki[:, :, :], 255, None, ALU.bitwise_and))
            then(dve.tensor_scalar(kd[:, :, :], kp[:, :, :], 7, 13, ALU.logical_shift_right,
                                   ALU.logical_shift_left))
            then(dve.tensor_tensor(scat[:, :, :], ke[:, :, :], kp[:, :, :], ALU.add))
            dve.tensor_tensor(scat[:, :, :], scat[:, :, :], kd[:, :, :], ALU.add).then_inc(idx_ready, 1)
            then(dve.tensor_scalar(kp[:, :, :], kp[:, :, :], CAP - 1, None, ALU.min))
            dve.tensor_tensor(gath[:, :, :], ke[:, :, :], kp[:, :, :], ALU.add).then_inc(idx_ready, 1)
            then(dve.tensor_tensor(eq[:, :, :, :], key[:, :, :].unsqueeze(2).to_broadcast([P, T, K, E]),
                                   k8[:, :, 0:K].unsqueeze(3).to_broadcast([P, T, K, E]), ALU.is_equal))
            then(dve.tensor_tensor(eq[:, :, :, :], eq[:, :, :, :],
                                   wt[:, :, :].unsqueeze(2).to_broadcast([P, T, K, E]), ALU.mult))
            then(dve.tensor_reduce(wtok[:, :, :], eq[:, :, :, :], AX.X, ALU.add))
            with dve.Fori(0, T // 2) as i:
                for par in range(2):
                    t = dve.snap(i * 2 + par)
                    dve.wait_ge(sd_proj, t + 1)
                    dve.tensor_tensor(xres[:, t, :], xres[:, t, :], pb[4 + par][:, :], ALU.add).then_inc(s_added, 1)
            with dve.Fori(0, E) as e:
                dve.wait_ge(xe_turned, e + 1)
                dve.tensor_copy(xeT[:, :, :], pb[0][:, :].rearrange("p (c n) -> p c n", c=CC)).then_inc(xeT_ready, 1)
                dve.wait_ge(e_silu, e + 1)
                dve.tensor_tensor(hh[:, :], hsil[:, :], pb[1][:, F:2 * F], ALU.mult).then_inc(h_ready, 1)
            dve.wait_ge(s_added, T)
            for n in range(T * K):
                t, k = n // K, n % K
                dve.wait_ge(gathered[n % T], 16 * (n // T + 1))
                if n:
                    dve.wait_ge(combined, n)
                dve.scalar_tensor_tensor(out=xres[:, t, :], in0=x3[:, n % T, :], scalar=wtok[:, t, k:k + 1],
                                         in1=xres[:, t, :], op0=ALU.mult, op1=ALU.add).then_inc(combined, 1)

        @block.tensor
        def _(pe):
            norm.tensor(pe)
            pe.wait_ge(norm.lo_ready, T)
            pe.wait_ge(w_lo, 1)
            for t in range(T):
                ins = split_matmuls(pe, LG[:, t, :], lambda s, c: xT[s][:, c, t * P:(t + 1) * P],
                                    lambda s, c: gw[s][:, c, :], range(CC))
            ins.then_inc(logits, 1)
            pe.wait_ge(w_lo, 3)

            def shared(j, reuse):
                for m, n in enumerate(("sg", "su")):
                    for half in range(2):
                        if reuse:
                            pe.wait_ge(s_up if m else s_silu, j * 2 + (half - 1))
                        split_matmuls(pe, pb[2 * m + half][:, :], lambda s, c: w[n][s][:, c, bass.ds(j * P, P)],
                                      lambda s, c: xT[s][:, c, half * HALF:(half + 1) * HALF],
                                      range(CC)).then_inc(su_proj if m else sg_proj, 1)

            shared(0, False)
            shared(1, True)
            pe.wait_ge(chosen_ready, 1)
            pe.wait_ge(consts, 4)
            for t in range(T):
                for u in range(t + 1):
                    ins = pe.matmul(PS[:, t, :], (tri if u == t else ones)[:, :], chosen16[:, u, :],
                                    start=(u == 0), stop=(u == t))
            ins.then_inc(pos_done, 1)
            with pe.Fori(2, CC) as j:
                shared(j, True)
            pe.wait_ge(s_lo, 2 * CC)
            pe.wait_ge(w_lo, 4)

            def down(t, par, reuse):
                if reuse:
                    pe.wait_ge(s_added, t - 1)
                split_matmuls(pe, pb[4 + par][:, :], lambda s, c: sT[s][:, c, bass.ds(t * P, P)],
                              lambda s, c: w["sd"][s][:, c, :], range(CC)).then_inc(sd_proj, 1)

            down(0, 0, False)
            down(1, 1, False)
            with pe.Fori(1, T // 2) as i:
                for par in range(2):
                    down(pe.snap(i * 2 + par), par, True)

            def turn_x(e, par, loads):
                pe.wait_ge(xe_loaded[par], loads)
                for c in range(CC):
                    ins = pe.transpose(pb[0][:, c * P:(c + 1) * P], xe[:, par, c * P:(c + 1) * P], ident)
                ins.then_inc(xe_turned, 1)

            def expert_down(e, slot, reuse):
                pe.wait_ge(hT_ready, e + 1)
                if reuse:
                    pe.wait_ge(y_ready, e)
                for f in range(FC):
                    ins = pe.matmul(pb[6][:, :], hT[:, f, :], w2[:, slot, f, :], start=(f == 0), stop=(f == FC - 1))
                ins.then_inc(down_done, 1)

            def expert(i, q, first, last):
                e = i * 4 + q
                pe.wait_ge(ew_loaded[q], i * 32 + 32)
                pe.wait_ge(xeT_ready, e + 1)
                for c in range(CC):
                    ins = pe.matmul(pb[1][:, :], xeT[:, c, :], w13[:, q, c, :], start=(c == 0), stop=(c == CC - 1))
                ins.then_inc(up_done, 1)
                if not (last and q == 3):
                    turn_x(e + 1, (q + 1) % 2, i * 32 + 16 * ((q + 1) // 2 + 1))
                if not (first and q == 0):
                    expert_down(e - 1, (q + 3) % 4, not (first and q == 1))
                pe.wait_ge(h_ready, e + 1)
                for f in range(FC):
                    ins = pe.transpose(pb[3][:, f * P:(f + 1) * P], hh[:, f * P:(f + 1) * P], ident)
                ins.then_inc(h_turned, 1)

            turn_x(0, 0, 16)
            for q in range(4):
                expert(0, q, True, False)
            with pe.Fori(1, LAST) as i:
                for q in range(4):
                    expert(i, q, False, False)
            for q in range(4):
                expert(LAST, q, False, True)
            expert_down(E - 1, 3, True)


def build(nc, a, out):
    with ExitStack() as ctx:
        g = {
            "xres": ctx.enter_context(nc.sbuf_tensor("xres", [P, T, D], F32)),
            "xT": tuple(ctx.enter_context(nc.sbuf_tensor(f"xT_{s}", [P, CC, N], F16)) for s in ("hi", "lo")),
            "ident": ctx.enter_context(nc.sbuf_tensor("ident", [P, P], F32)),
            "out": out,
        }
        psum = ctx.enter_context(nc.psum_tensor("psum", [P, 8, 512], F32))
        g["psum"] = psum
        g["pb"] = [psum[:, i, :] for i in range(8)]
        g["ident"] = g["ident"][:, :]
        stage_a(nc, a, g)
        g["w13"] = ctx.enter_context(nc.sbuf_tensor("w13_sb", [P, 4, CC, 2 * F], F32))
        g["w2"] = ctx.enter_context(nc.sbuf_tensor("w2_sb", [P, 4, F // P, D], F32))
        g["ew_loaded"] = [ctx.enter_context(nc.semaphore(f"ew_loaded{i}")) for i in range(4)]
        g["xbuf"] = nc.dram_tensor("xbuf", [E * CAP, D], F32).ap()
        g["ybuf"] = nc.dram_tensor("ybuf", [E * CAP, D], F32).ap()
        stage_b(nc, a, g)
        stage_c(nc, a, g)



def layouts(i):
    import numpy as np

    c=np.ascontiguousarray
    Pn=128
    def kc(m):
        return c(m.reshape(m.shape[0]//Pn,Pn,-1).transpose(1,0,2))
    o={}
    o['x']=c(i['x'].reshape(1024,512))
    ctx=i['ctx_2048']
    o['ctx']=c(ctx[:,:256].transpose(0,2,1).reshape(32,4,Pn,256).transpose(0,2,1,3))
    o['ctx_last']=c(ctx[:,256].T.reshape(4,Pn,32).transpose(1,0,2))
    for n in ('Wq','Wg','Wkv','Wo'): o[n]=kc(i['L0_xattn_'+n].T)
    o['bg']=c(i['L0_xattn_bg'].reshape(4,Pn).T)
    def sw(n): return i['L0_attn_w%s_codes'%n], i['L0_attn_w%s_scales'%n]
    def heads(w): return w.reshape(4,Pn,16,Pn).transpose(2,1,0,3)
    def hsc(w): return w.reshape(4,4,16,Pn).transpose(2,1,0,3)
    q,qs=sw('q'); k,ks=sw('k'); v,vs=sw('v'); w,ws=sw('o')
    o['qk_codes']=c(np.stack([heads(q),heads(k)],2).reshape(16,Pn,1024))
    o['qk_scales']=c(np.stack([hsc(qs),hsc(ks)],2).reshape(16,4,1024))
    o['v_codes']=c(v.reshape(4,Pn,4,512).transpose(2,1,0,3).reshape(4,Pn,2048))
    o['v_scales']=c(vs.reshape(4,4,4,512).transpose(2,1,0,3).reshape(4,4,2048))
    o['o_codes']=c(w.reshape(4,4,Pn,512).transpose(0,2,1,3).reshape(4,Pn,2048))
    o['o_scales']=c(ws.reshape(4,4,4,512).transpose(0,2,1,3).reshape(4,4,2048))
    for n in ('bq','bk','bv'): o[n]=c(i['L0_attn_'+n].reshape(16,Pn).T)
    o['gate_w']=kc(i['L0_ffn_gate_w'].T)
    o['gate_bias']=c(i['L0_ffn_gate_bias'].reshape(1,32))
    for n,m in (('sg','gate'),('su','up'),('sd','down')): o[n]=kc(i['L0_ffn_shared_'+m])
    w1=i['L0_ffn_w1'].reshape(32,4,Pn,256).transpose(0,2,1,3); w3=i['L0_ffn_w3'].reshape(32,4,Pn,256).transpose(0,2,1,3)
    o['w13']=c(np.concatenate([w1,w3],3))
    o['w2']=c(i['L0_ffn_w2'].reshape(32,2,Pn,512).transpose(0,2,1,3))
    o['bo']=c(i['L0_attn_bo'].reshape(1,512))
    return o


def kernel(**inputs):
    import numpy as np
    import concourse.bacc as bacc
    from concourse.bass_utils import run_bass_kernel_spmd

    arrays = layouts({n: np.asarray(v) for n, v in inputs.items()})
    nc = bacc.Bacc("TRN2", target_bir_lowering=False, num_devices=1)
    aps = {n: nc.dram_tensor(f"in_{n}", v.shape, mybir.dt.from_np(v.dtype), kind="ExternalInput").ap()
           for n, v in arrays.items()}
    out = nc.dram_tensor("out_y", (N, D), F32, kind="ExternalOutput").ap()
    build(nc, aps, out)
    r = run_bass_kernel_spmd(nc, [{f"in_{n}": v for n, v in arrays.items()}], core_ids=[0])
    return r.results[0]["out_y"].reshape(B, L, D)
```

```python
from contextlib import ExitStack

import concourse.bass as bass
from concourse import mybir

F32 = mybir.dt.float32
F16 = mybir.dt.float16
I32 = mybir.dt.int32
ALU = mybir.AluOpType
ACT = mybir.ActivationFunctionType
AX = mybir.AxisListType

P = 128
B = 32
L = 32
D = 512
S = 257
CC = D // P
T = B * L // P
N = B * L
H = 16
HL = D // H
HG = 4
G = H // HG
E = 32
EG = 4
K = 4
F = 256
CAP = 128
ROUTE_SCALE = 2.0
EPS_LN = 1e-5
EPS_Z = 1e-6
EPS_W = 1e-20
BIG = 3.0e38
HALF = N // 2
DX = D + 48
NUM = D + E


class Steps:

    def __init__(self, eng, sem):
        self.eng, self.sem, self.n = eng, sem, 0

    def done(self, ins):
        ins.then_inc(self.sem, 1)
        self.n = self.n + 1

    def wait(self):
        self.eng.wait_ge(self.sem, self.n)


def split_matmuls(pe, out, lhs, rhs, chunks):
    n = len(chunks) * 3
    k = 0
    for c in chunks:
        for a, b in ((0, 0), (0, 1), (1, 0)):
            ins = pe.matmul(out, lhs(a, c), rhs(b, c), start=(k == 0), stop=(k == n - 1))
            k += 1
    return ins


class Norm:

    def __init__(self, nc, ctx, name, xres, ident, xT, banks, xn=None, keep=None):
        def sb(n, shape, dt=F32):
            return ctx.enter_context(nc.sbuf_tensor(f"{name}_{n}", shape, dt))

        def sem(n):
            return ctx.enter_context(nc.semaphore(f"{name}_{n}"))

        self.xres, self.ident, self.xT, self.banks = xres, ident, xT, banks
        self.stats = sb("stats", [P, T, 6])
        self.mv = sb("mv", [P, T, 2])
        self.std = sb("std", [P, T])
        self.rstd = sb("rstd", [P, T])
        self.keep, self.xn = keep, xn
        self.stats_ready = sem("stats_ready")
        self.var_ready = sem("var_ready")
        self.std_ready = sem("std_ready")
        self.normed = sem("normed")
        self.turned = sem("turned")
        self.hi_ready = sem("hi_ready")
        self.lo_ready = sem("lo_ready")
        self.steps = sem("dve_steps")

    def buf(self, t, par):
        return self.xn[:, par, :] if self.keep is None else self.keep[:, t, :]

    def statistics(self, dve, t):
        dve.bn_stats(self.stats[:, t, :], self.xres[:, t, :]).then_inc(self.stats_ready, 1)

    def vector(self, dve, between=None):
        st = Steps(dve, self.steps)
        for t in range(T):
            st.done(dve.bn_aggr(self.mv[:, t, :], self.stats[:, t, :]))
        st.wait()
        dve.tensor_scalar(self.std[:, :], self.mv[:, :, 1], EPS_LN, None, ALU.add).then_inc(self.var_ready, 1)
        dve.wait_ge(self.std_ready, 1)
        st.done(dve.reciprocal(self.rstd[:, :], self.std[:, :]))
        st.wait()

        def norm(t, par, reuse):
            if reuse:
                dve.wait_ge(self.turned, t - 1)
            dve.tensor_scalar(self.buf(t, par), self.xres[:, t, :], self.mv[:, t, 0:1], self.rstd[:, bass.ds(t, 1)],
                              ALU.subtract, ALU.mult).then_inc(self.normed, 1)

        def low(t, par):
            dve.wait_ge(self.hi_ready, t + 1)
            dve.tensor_tensor(self.xT[1][:, :, bass.ds(t * P, P)],
                              self.banks[par][:, :].rearrange("p (c t) -> p c t", c=CC),
                              self.xT[0][:, :, bass.ds(t * P, P)], ALU.subtract).then_inc(self.lo_ready, 1)

        free = self.keep is None
        norm(0, 0, False)
        norm(1, 1, False)
        low(0, 0)
        if between is not None:
            for t in range(1, T):
                if t - 1 in between:
                    between[t - 1]()
                if t + 1 < T:
                    norm(t + 1, (t + 1) % 2, free)
                low(t, t % 2)
            return
        with dve.Fori(1, T // 2) as i:
            t = dve.snap(i * 2)
            norm(t, 0, free)
            low(t - 1, 1)
            norm(t + 1, 1, free)
            low(t, 0)
        low(T - 1, 1)

    def root(self, act):
        act.wait_ge(self.var_ready, 1)
        act.activation(self.std[:, :], self.std[:, :], ACT.Sqrt).then_inc(self.std_ready, 1)

    def high(self, act, t, par):
        act.wait_ge(self.turned, t + 1)
        act.activation(self.xT[0][:, :, bass.ds(t * P, P)],
                       self.banks[par][:, :].rearrange("p (c t) -> p c t", c=CC), ACT.Copy).then_inc(self.hi_ready, 1)

    def turn(self, pe, t):
        pe.wait_ge(self.normed, t + 1)
        if t >= 2:
            pe.wait_ge(self.lo_ready, t - 1)
        for c in range(CC):
            ins = pe.transpose(self.banks[t % 2][:, c * P:(c + 1) * P],
                               self.buf(t, t % 2)[:, c * P:(c + 1) * P], self.ident)
        ins.then_inc(self.turned, 1)


class Dequant:

    def __init__(self, nc, ctx, name, raw, scale, hi, lo, loads):
        self.raw, self.scale, self.hi, self.lo = raw, scale, hi, lo
        self.loaded = [ctx.enter_context(nc.semaphore(f"{name}_loaded{i}")) for i in range(loads)]
        self.multiplied = ctx.enter_context(nc.semaphore(f"{name}_multiplied"))
        self.hi_ready = ctx.enter_context(nc.semaphore(f"{name}_hi_ready"))
        self.lo_ready = ctx.enter_context(nc.semaphore(f"{name}_lo_ready"))

    PER_LOAD = 5 * 16

    def load(self, sp, n_par, codes, scales):
        s = self.loaded[n_par]
        sp.dma_start(self.raw[n_par], codes).then_inc(s, 16)
        for q in range(4):
            dst = self.scale[n_par][32 * q:32 * q + 32, :]
            sp.dma_start(dst, scales[q:q + 1, :].to_broadcast([32, dst.shape[1]])).then_inc(s, 16)

    def pool(self, pool, n, par, load, used=None):
        pool.wait_ge(self.loaded[par], load * self.PER_LOAD)
        pool.tensor_tensor(self.raw[par], self.raw[par], self.scale[par], ALU.mult).then_inc(self.multiplied, 1)
        pool.wait_ge(self.multiplied, n + 1)
        pool.wait_ge(self.hi_ready, n + 1)
        if used is not None:
            pool.wait_ge(used[0], used[1])
        pool.tensor_tensor(self.lo[par], self.raw[par], self.hi[par], ALU.subtract).then_inc(self.lo_ready, 1)

    def scalar(self, act, n, par, used=None):
        act.wait_ge(self.multiplied, n + 1)
        if used is not None:
            act.wait_ge(used[0], used[1])
        act.activation(self.hi[par], self.raw[par], ACT.Copy).then_inc(self.hi_ready, 1)


def stage_a(nc, a, g):
    xres, xT, ident, pb = g["xres"], g["xT"], g["ident"], g["pb"]
    CM = S - 1
    CT = CM // P
    W1 = P + 1
    with ExitStack() as ctx:
        def sb(n, shape, dt=F32):
            return ctx.enter_context(nc.sbuf_tensor(n, shape, dt))

        def sem(n):
            return ctx.enter_context(nc.semaphore(n))

        stage, split = g["stage"], g["split"]

        def slots(ap, n):
            return ap.rearrange("p s (c n) -> p (s c) n", c=CC) if n == 1 else ap.rearrange("p s m -> p (s m)"
                                                                      ).rearrange("p (c n) -> p c n", c=CC)

        raw = {"Wq": slots(stage[:, 0:1, :], 1), "Wg": slots(stage[:, 1:2, :], 1),
               "Wkv": slots(stage[:, 2:4, :], 2), "Wo": slots(stage[:, 4:5, :], 1)}
        w = {"Wq": tuple(slots(split[:, i:i + 1, :], 1) for i in (0, 1)),
             "Wg": tuple(slots(split[:, i:i + 1, :], 1) for i in (2, 3)),
             "Wkv": tuple(sb(f"Wkv_{i}", [P, CC, 2 * D], F16)[:, :, :] for i in ("hi", "lo")),
             "Wo": tuple(sb(f"Wo_{i}", [P, CC, D], F16)[:, :, :] for i in ("hi", "lo"))}
        names = ["Wkv", "Wq", "Wg", "Wo"]
        bg = sb("bg", [P, CC])
        qT = sb("qT", [P, CC, N])
        gT = sb("gT", [P, CC, N])
        fneg = sb("fneg", [P, 2, D])
        craw = sb("craw", [P, 2, CC, CM])
        chl = (sb("c_hi", [P, 2, CC, CM], F16), sb("c_lo", [P, 2, CC, CM], F16))
        lraw = sb("lraw", [P, CC, B])
        lhl = (sb("l_hi", [P, CC, B], F16), sb("l_lo", [P, CC, B], F16))
        klast = sb("klast", [B, D])
        klsel = sb("klsel", [B, 2, D])
        vlast = sb("vlast", [B, CC, W1])
        ksb = sb("ksb", [P, 2, CT, D])
        vsb = sb("vsb", [P, 2, CT, CC, W1])
        quad = sb("quad", [P, P])
        kvbd = sb("kvbd", [P, CC, P])
        ksbd = sb("ksbd", [P, CC, P])
        den = sb("den", [P, CC, L])
        rden = sb("rden", [P, CC, L])
        att = sb("att", [P, CC, L])

        x_loaded = [sem(f"x_loaded{i}") for i in range(2)]
        w_loaded = {n: sem(f"{n}_loaded") for n in names}
        small_loaded = sem("small_loaded")
        w_hi = sem("w_hi")
        w_lo = sem("w_lo")
        last_loaded = sem("last_loaded")
        last_hi = sem("last_hi")
        last_lo = sem("last_lo")
        consts = sem("consts")
        ones_set = sem("ones_set")
        qg_proj = sem("qg_proj")
        q_neg = sem("q_neg")
        q_exp = sem("q_exp")
        q_feat = sem("q_feat")
        g_ready = sem("g_ready")
        kl_proj = sem("kl_proj")
        vl_proj = sem("vl_proj")
        kl_neg = sem("kl_neg")
        kl_exp = sem("kl_exp")
        kl_feat = sem("kl_feat")
        vl_ready = sem("vl_ready")
        ctx_loaded = [sem(f"ctx_loaded{i}") for i in range(2)]
        ctx_hi = sem("ctx_hi")
        ctx_lo = sem("ctx_lo")
        k_proj = sem("k_proj")
        v_proj = sem("v_proj")
        k_neg = sem("k_neg")
        k_exp = sem("k_exp")
        k_feat = sem("k_feat")
        v_ready = sem("v_ready")
        kl_sel = sem("kl_sel")
        kvs_done = sem("kvs_done")
        bd_ready = sem("bd_ready")
        att_done = sem("att_done")
        den_eps = sem("den_eps")
        den_rec = sem("den_rec")
        att_z = sem("att_z")
        att_ready = sem("att_ready")
        att_hi = sem("att_hi")
        att_lo = sem("att_lo")
        o_proj = sem("o_proj")
        o_added = sem("o_added")

        norm = Norm(nc, ctx, "n1", xres, ident, xT, [pb[6], pb[7]],
                    xn=gT[:, 0, :].rearrange("p (b n) -> p b n", b=2))
        dq_v, dq_qk, n2 = g["dq_v"], g["dq_qk"], g["n2"]
        block = ctx.enter_context(nc.Block())

        @block.sync
        def _(sp):
            sp.dma_start(raw["Wkv"], a["Wkv"]).then_inc(w_loaded["Wkv"], 16)
            sp.dma_start(craw[:, 0, :, :], a["ctx"][0]).then_inc(ctx_loaded[0], 16)
            xt = a["x"].rearrange("(t p) d -> p t d", p=P)
            for i in range(2):
                r = slice(i * T // 2, (i + 1) * T // 2)
                sp.dma_start(xres[:, r, :], xt[:, r, :]).then_inc(x_loaded[i], 16)
            sp.dma_start(craw[:, 1, :, :], a["ctx"][1]).then_inc(ctx_loaded[1], 16)
            sp.dma_start(raw["Wq"], a["Wq"]).then_inc(w_loaded["Wq"], 16)
            sp.dma_start(raw["Wg"], a["Wg"]).then_inc(w_loaded["Wg"], 16)
            sp.dma_start(bg[:, :], a["bg"]).then_inc(small_loaded, 16)
            sp.dma_start(lraw[:, :, :], a["ctx_last"]).then_inc(last_loaded, 16)
            sp.dma_start(raw["Wo"], a["Wo"]).then_inc(w_loaded["Wo"], 16)
            with sp.Fori(1, B // 2) as i:
                for par in range(2):
                    b = sp.snap(i * 2 + par)
                    sp.wait_ge(ctx_lo, b - 1)
                    sp.dma_start(craw[:, par, :, :], a["ctx"][b]).then_inc(ctx_loaded[par], 16)
            sp.wait_ge(w_lo, 3)
            dq_v.load(sp, 0, a["v_codes"][0], a["v_scales"][0])
            for h in range(2):
                dq_qk.load(sp, h, a["qk_codes"][h], a["qk_scales"][h])

        @block.gpsimd
        def _(pool):
            pool.memset(ident[:, :], 0.0).then_inc(consts, 1)
            pool.wait_ge(consts, 1)
            pool.affine_select(out=ident[:, :], in_=ident[:, :], compare_op=ALU.not_equal, fill=1.0, base=0,
                               pattern=[[-1, P]], channel_multiplier=1).then_inc(consts, 1)
            pool.memset(quad[:, :], 0.0).then_inc(consts, 1)
            pool.wait_ge(consts, 3)
            for q in range(4):
                pool.memset(quad[32 * q:32 * q + 32, 32 * q:32 * q + 32], 1.0).then_inc(consts, 1)
            pool.wait_ge(consts, 7)
            pool.memset(vlast[:, :, P:W1], 1.0).then_inc(ones_set, 1)
            pool.wait_ge(ones_set, 1)
            pool.memset(vsb[:, :, :, :, P:W1], 1.0).then_inc(ones_set, 1)

            def low(b, par, reuse):
                pool.wait_ge(ctx_hi, b + 1)
                if reuse:
                    pool.wait_ge(v_proj, CT * (b - 1))
                pool.tensor_tensor(chl[1][:, par, :, :], craw[:, par, :, :], chl[0][:, par, :, :],
                                   ALU.subtract).then_inc(ctx_lo, 1)

            low(0, 0, False)
            low(1, 1, False)
            with pool.Fori(1, B // 2) as i:
                for par in range(2):
                    low(pool.snap(i * 2 + par), par, True)
            dq_v.pool(pool, 0, 0, 1)
            for h in range(2):
                dq_qk.pool(pool, h, h, 1)

        @block.scalar
        def _(act):
            def w_high(n):
                act.wait_ge(w_loaded[n], 16)
                act.activation(w[n][0], raw[n], ACT.Copy).then_inc(w_hi, 1)

            def high(b, par, loads, reuse):
                act.wait_ge(ctx_loaded[par], loads)
                if reuse:
                    act.wait_ge(v_proj, CT * (b - 1))
                act.activation(chl[0][:, par, :, :], craw[:, par, :, :], ACT.Copy).then_inc(ctx_hi, 1)

            def tiles(b, par, t, first):
                n = b * CT + t
                act.wait_ge(k_proj, n + 1)
                if not (first and par == 0):
                    act.wait_ge(k_feat, n - 1)
                act.activation(fneg[:, t, :], pb[t][:, :], ACT.Relu, scale=-1.0).then_inc(k_neg, 1)
                act.wait_ge(k_neg, n + 1)
                act.activation(fneg[:, t, :], fneg[:, t, :], ACT.Exp, scale=-1.0).then_inc(k_exp, 1)
                act.wait_ge(v_proj, n + 1)
                if not first:
                    act.wait_ge(kvs_done, b - 1)
                act.activation(vsb[:, par, t, :, 0:P], pb[2 + t][:, :].rearrange("p (c n) -> p c n", c=CC),
                               ACT.Copy).then_inc(v_ready, 1)

            w_high("Wkv")
            high(0, 0, 16, False)
            norm.root(act)
            act.wait_ge(ones_set, 2)
            high(1, 1, 16, False)
            tiles(0, 0, 0, True)
            w_high("Wq")
            tiles(0, 0, 1, True)
            for t in range(T):
                norm.high(act, t, t % 2)
                if t == 1:
                    tiles(1, 1, 0, True)
                if t == 3:
                    tiles(1, 1, 1, True)
                if t == 5:
                    w_high("Wg")
            act.wait_ge(last_loaded, 16)
            act.activation(lhl[0][:, :, :], lraw[:, :, :], ACT.Copy).then_inc(last_hi, 1)
            act.wait_ge(k_feat, 2 * CT)
            w_high("Wo")

            def q_chunk(j, reuse):
                for half in range(2):
                    n = j * 2 + half
                    act.wait_ge(qg_proj, n + 1)
                    if reuse:
                        act.wait_ge(q_feat, j * 2)
                    act.activation(fneg[:, half, :], pb[half][:, :], ACT.Relu, scale=-1.0).then_inc(q_neg, 1)
                    act.wait_ge(q_neg, n + 1)
                    act.activation(fneg[:, half, :], fneg[:, half, :], ACT.Exp, scale=-1.0).then_inc(q_exp, 1)

            q_chunk(0, False)
            with act.Fori(1, CC) as j:
                q_chunk(j, True)
            act.wait_ge(small_loaded, 16)
            with act.Fori(0, CC) as j:
                for half in range(2):
                    n = act.snap(j * 2 + half)
                    act.wait_ge(qg_proj, n + 2 * CC + 1)
                    act.activation(gT[:, j, half * HALF:(half + 1) * HALF], pb[2 + half][:, :], ACT.Sigmoid,
                                   bias=bg[:, bass.ds(j, 1)]).then_inc(g_ready, 1)

            act.wait_ge(kl_proj, 1)
            act.wait_ge(q_feat, 2 * CC)
            act.activation(fneg[0:B, 0, :], pb[4][0:B, :], ACT.Relu, scale=-1.0).then_inc(kl_neg, 1)
            act.wait_ge(kl_neg, 1)
            act.activation(fneg[0:B, 0, :], fneg[0:B, 0, :], ACT.Exp, scale=-1.0).then_inc(kl_exp, 1)
            act.wait_ge(vl_proj, 1)
            act.activation(vlast[:, :, 0:P], pb[5][0:B, :].rearrange("p (c n) -> p c n", c=CC),
                           ACT.Copy).then_inc(vl_ready, 1)

            def pair(i, last):
                for par in range(2):
                    b = act.snap(i * 2 + par)
                    tiles(b, par, 0, False)
                    if not last:
                        high(b + 1, 1 - par, i * 16 + 16 * (par + 1), True)
                    elif par == 0:
                        high(b + 1, 1, i * 16 + 16, True)
                    tiles(b, par, 1, False)

            act.wait_ge(kl_feat, 1)
            high(2, 0, 32, True)
            with act.Fori(1, B // 2 - 1) as i:
                pair(i, False)
            pair(B // 2 - 1, True)
            dq_v.scalar(act, 0, 0)
            for h in range(2):
                dq_qk.scalar(act, h, h)

            with act.Fori(0, T) as t:
                act.wait_ge(att_ready, B)
                act.activation(xT[0][:, :, bass.ds(t * P, P)], qT[:, :, bass.ds(t * P, P)],
                               ACT.Copy).then_inc(att_hi, 1)

        @block.vector
        def _(dve):
            def w_low(k):
                n = names[k]
                dve.wait_ge(w_hi, k + 1)
                dve.tensor_tensor(w[n][1], raw[n], w[n][0], ALU.subtract).then_inc(w_lo, 1)

            def feature(b, par, t):
                dve.wait_ge(k_exp, b * CT + (t + 1))
                dve.scalar_tensor_tensor(out=ksb[:, par, t, :], in0=pb[t][:, :], scalar=1.0,
                                         in1=fneg[:, t, :], op0=ALU.add, op1=ALU.max).then_inc(k_feat, 1)

            w_low(0)
            for t in range(T):
                if t % (T // 2) == 0:
                    dve.wait_ge(x_loaded[t // (T // 2)], 16)
                norm.statistics(dve, t)
            dve.wait_ge(norm.stats_ready, T)
            norm.vector(dve, {0: lambda: feature(0, 0, 0), 1: lambda: feature(0, 0, 1), 2: lambda: w_low(1),
                              3: lambda: feature(1, 1, 0), 5: lambda: feature(1, 1, 1), 6: lambda: w_low(2)})
            dve.wait_ge(last_hi, 1)
            dve.tensor_tensor(lhl[1][:, :, :], lraw[:, :, :], lhl[0][:, :, :], ALU.subtract).then_inc(last_lo, 1)
            w_low(3)

            with dve.Fori(0, CC) as j:
                for half in range(2):
                    dve.wait_ge(q_exp, j * 2 + (half + 1))
                    dve.scalar_tensor_tensor(out=qT[:, j, half * HALF:(half + 1) * HALF], in0=pb[half][:, :],
                                             scalar=1.0, in1=fneg[:, half, :], op0=ALU.add,
                                             op1=ALU.max).then_inc(q_feat, 1)
            dve.wait_ge(kl_exp, 1)
            dve.scalar_tensor_tensor(out=klast[:, :], in0=pb[4][0:B, :], scalar=1.0, in1=fneg[0:B, 0, :],
                                     op0=ALU.add, op1=ALU.max).then_inc(kl_feat, 1)
            dve.wait_ge(consts, 7)
            dve.wait_ge(kl_feat, 1)

            def select(b, par, reuse):
                if reuse:
                    dve.wait_ge(kvs_done, b - 1)
                dve.tensor_scalar(klsel[:, par, :], klast[:, :], ident[0:B, bass.ds(b, 1)], None,
                                  ALU.mult).then_inc(kl_sel, 1)

            def diagonal(b, reuse):
                dve.wait_ge(kvs_done, b + 1)
                if reuse:
                    dve.wait_ge(att_done, b)
                for u in range(2):
                    kv = pb[4 + u][:, 0:2 * W1].rearrange("p (c n) -> p c n", c=2)
                    m = quad[:, :].unsqueeze(1).to_broadcast([P, 2, P])
                    dve.tensor_tensor(kvbd[:, 2 * u:2 * u + 2, :], kv[:, :, 0:P], m, ALU.mult)
                    ins = dve.tensor_tensor(ksbd[:, 2 * u:2 * u + 2, :],
                                            kv[:, :, P:W1].to_broadcast([P, 2, P]), m, ALU.mult)
                ins.then_inc(bd_ready, 1)

            def output(b):
                num = pb[6][:, 0:P].rearrange("p (c l) -> p c l", c=CC)
                dn = pb[6][:, P:2 * P].rearrange("p (c l) -> p c l", c=CC)
                dve.wait_ge(att_done, b + 1)
                dve.tensor_scalar(den[:, :, :], dn, EPS_Z, None, ALU.add).then_inc(den_eps, 1)
                dve.wait_ge(den_eps, b + 1)
                dve.reciprocal(rden[:, :, :], den[:, :, :]).then_inc(den_rec, 1)
                dve.wait_ge(den_rec, b + 1)
                dve.tensor_tensor(att[:, :, :], num, rden[:, :, :], ALU.mult).then_inc(att_z, 1)
                dve.wait_ge(att_z, b + 1)
                dve.tensor_tensor(qT[:, :, bass.ds(b * L, L)], att[:, :, :], gT[:, :, bass.ds(b * L, L)],
                                  ALU.mult).then_inc(att_ready, 1)

            dve.wait_ge(g_ready, 2 * CC)
            select(0, 0, False)
            select(1, 1, False)
            diagonal(0, False)
            output(0)
            with dve.Fori(1, B // 2) as i:
                for par in range(2):
                    b = dve.snap(i * 2 + par)
                    feature(b, par, 0)
                    diagonal(b - 1, True)
                    select(b, par, True)
                    feature(b, par, 1)
                    output(b - 1)
            diagonal(B - 1, True)
            output(B - 1)

            def low(t):
                dve.wait_ge(att_hi, t + 1)
                dve.tensor_tensor(xT[1][:, :, bass.ds(t * P, P)], qT[:, :, bass.ds(t * P, P)],
                                  xT[0][:, :, bass.ds(t * P, P)], ALU.subtract).then_inc(att_lo, 1)

            def add(t, par):
                dve.wait_ge(o_proj, t + 1)
                dve.tensor_tensor(xres[:, t, :], xres[:, t, :], pb[par][:, :], ALU.add).then_inc(o_added, 1)
                dve.wait_ge(o_added, t + 1)
                n2.statistics(dve, t)

            low(0)
            low(1)
            with dve.Fori(1, T // 2) as i:
                for par in range(2):
                    t = dve.snap(i * 2 + par)
                    low(t)
                    add(t - 2, par)
            add(T - 2, 0)
            add(T - 1, 1)

        @block.tensor
        def _(pe):
            wkv = w["Wkv"]

            def kv(out, stat, v):
                return split_matmuls(pe, out, stat, lambda s, c: wkv[s][:, c, v * D:(v + 1) * D], range(CC))

            def project(b, par, t, reuse):
                n = b * CT + t
                if t == 0:
                    pe.wait_ge(ctx_lo, b + 1)
                stat = lambda s, c: chl[s][:, par, c, t * P:(t + 1) * P]
                if reuse:
                    pe.wait_ge(k_feat, n - 1)
                kv(pb[t][:, :], stat, 0).then_inc(k_proj, 1)
                if reuse:
                    pe.wait_ge(v_ready, n - 1)
                kv(pb[2 + t][:, :], stat, 1).then_inc(v_proj, 1)

            pe.wait_ge(w_lo, 1)
            project(0, 0, 0, False)
            pe.wait_ge(consts, 2)
            norm.turn(pe, 0)
            norm.turn(pe, 1)
            project(0, 0, 1, False)
            norm.turn(pe, 2)
            norm.turn(pe, 3)
            project(1, 1, 0, True)
            norm.turn(pe, 4)
            norm.turn(pe, 5)
            project(1, 1, 1, True)
            norm.turn(pe, 6)
            norm.turn(pe, 7)
            pe.wait_ge(norm.lo_ready, T)
            pe.wait_ge(k_feat, 2 * CT)
            pe.wait_ge(v_ready, 2 * CT)
            for m in range(2):
                pe.wait_ge(w_lo, m + 2)
                ww = w[names[m + 1]]

                def chunk(j, reuse):
                    for half in range(2):
                        if reuse:
                            n = j * 2 + (half - 1)
                            pe.wait_ge(g_ready if m else q_feat, n)
                        split_matmuls(pe, pb[2 * m + half][:, :],
                                      lambda s, c: ww[s][:, c, bass.ds(j * P, P)],
                                      lambda s, c: xT[s][:, c, half * HALF:(half + 1) * HALF],
                                      range(CC)).then_inc(qg_proj, 1)

                chunk(0, False)
                with pe.Fori(1, CC) as j:
                    chunk(j, True)
            pe.wait_ge(last_lo, 1)
            kv(pb[4][0:B, :], lambda s, c: lhl[s][:, c, :], 0).then_inc(kl_proj, 1)
            kv(pb[5][0:B, :], lambda s, c: lhl[s][:, c, :], 1).then_inc(vl_proj, 1)

            def summary(b, par, reuse):
                pe.wait_ge(k_feat, CT * b + CT)
                pe.wait_ge(v_ready, CT * b + CT)
                pe.wait_ge(kl_sel, b + 1)
                if reuse:
                    pe.wait_ge(bd_ready, b)
                for c in range(CC):
                    out = pb[4 + c // 2][:, (c % 2) * W1:(c % 2 + 1) * W1]
                    for t in range(CT):
                        pe.matmul(out, ksb[:, par, t, c * P:(c + 1) * P], vsb[:, par, t, c, :],
                                  start=(t == 0), stop=False)
                    ins = pe.matmul(out, klsel[:, par, c * P:(c + 1) * P], vlast[:, c, :],
                                    start=False, stop=True)
                ins.then_inc(kvs_done, 1)

            def attend(b, reuse):
                pe.wait_ge(bd_ready, b + 1)
                if reuse:
                    pe.wait_ge(att_ready, b)
                for c in range(CC):
                    q = qT[:, c, bass.ds(b * L, L)]
                    pe.matmul(pb[6][:, c * L:(c + 1) * L], kvbd[:, c, :], q, start=True, stop=True)
                    ins = pe.matmul(pb[6][:, P + c * L:P + (c + 1) * L], ksbd[:, c, :], q, start=True, stop=True)
                ins.then_inc(att_done, 1)

            pe.wait_ge(q_feat, 2 * CC)
            pe.wait_ge(g_ready, 2 * CC)
            pe.wait_ge(vl_ready, 1)
            pe.wait_ge(kl_feat, 1)
            summary(0, 0, False)
            attend(0, False)
            with pe.Fori(1, B // 2) as i:
                for par in range(2):
                    b = pe.snap(i * 2 + par)
                    project(b, par, 0, True)
                    summary(b - 1, 1 - par, True)
                    project(b, par, 1, True)
                    attend(b - 1, True)
            summary(B - 1, 1, True)
            attend(B - 1, True)

            pe.wait_ge(w_lo, 4)

            def out_proj(t, par, reuse):
                pe.wait_ge(att_lo, t + 1)
                if reuse:
                    pe.wait_ge(o_added, t - 1)
                split_matmuls(pe, pb[par][:, :], lambda s, c: xT[s][:, c, bass.ds(t * P, P)],
                              lambda s, c: w["Wo"][s][:, c, :], range(CC)).then_inc(o_proj, 1)

            out_proj(0, 0, False)
            out_proj(1, 1, False)
            with pe.Fori(1, T // 2) as i:
                for par in range(2):
                    out_proj(pe.snap(i * 2 + par), par, True)


def stage_b(nc, a, g):
    xres, xT, ident, pb, psum = g["xres"], g["xT"], g["ident"], g["pb"], g["psum"]
    SCALE = float(P) ** -0.5
    GT = HG * P
    with ExitStack() as ctx:
        def sb(n, shape, dt=F32):
            return ctx.enter_context(nc.sbuf_tensor(n, shape, dt))

        def sem(n):
            return ctx.enter_context(nc.semaphore(n))

        bq, bk, bv = (sb(n + "_sb", [P, H]) for n in ("bq", "bk", "bv"))
        bo = sb("bo_sb", [P, D])
        zero = sb("zero", [P, DX])
        xn = sb("xn", [P, 2, D])
        stage, split = g["stage"], g["split"]
        v_w = tuple(split[:, s, :].rearrange("p (c n) -> p c n", c=CC) for s in (0, 1))
        qk_w = tuple(split[:, s, :].rearrange("p (b m c n) -> p b m c n", b=2, m=2, c=CC) for s in (2, 3))
        o_half = tuple(sb(f"o_w_{s}", [P, HG * D], F16) for s in ("hi", "lo"))
        o_w = tuple(t[:, :].rearrange("p (h n) -> p h n", h=HG) for t in o_half)
        o_sc = sb("o_sc", [P, HG * D])
        qT, kT = sb("qT_h", [P, N]), sb("kT_h", [P, N])
        vsb = sb("v_g", [P, T, GT])
        sc = sb("scores", [P, T, L])
        smax, ssum, srec = sb("smax", [P, T]), sb("ssum", [P, T]), sb("srec", [P, T])
        pT = sb("pT", [P, T, P])
        oT = tuple(sb(f"oT_{s}", [P, HG, N], F16) for s in ("hi", "lo"))

        bias_loaded = sem("bias_loaded")
        bo_added = sem("bo_added")
        zeroed = sem("zeroed")
        xbuf_zeroed = sem("xbuf_zeroed")
        v_proj = sem("b_v_proj")
        v_evac = sem("v_evac")
        q_proj = sem("b_q_proj")
        q_evac = sem("q_evac")
        k_proj = sem("b_k_proj")
        k_evac = sem("k_evac")
        s_done = sem("s_done")
        s_evac = sem("s_evac")
        s_steps = sem("s_steps")
        s_shift = sem("s_shift")
        s_exp = sem("s_exp")
        pt_ready = sem("pt_ready")
        pv_done = sem("pv_done")
        o_hi = sem("o_hi")
        o_lo = sem("o_lo")
        o_proj = sem("b_o_proj")
        o_added = sem("b_o_added")

        norm = g["n2"]
        norm.banks, norm.xn = [pb[0], pb[1]], xn
        dq_v, dq_qk, n3 = g["dq_v"], g["dq_qk"], g["n3"]
        dq_o = Dequant(nc, ctx, "o", [stage[:, 4, :]], [o_sc[:, :]], [o_half[0][:, :]], [o_half[1][:, :]], 1)
        S2 = psum[:, 4:6, :].rearrange("p b (t k) -> p (b t) k", k=P)

        def v_bank(t):
            return 4 + t % 2 if t < T - 2 else 6 + t % 2

        O2 = psum[:, 6:8, :].rearrange("p b n -> p (b n)")
        block = ctx.enter_context(nc.Block())

        @block.sync
        def _(sp):
            for dst, n in ((bq, "bq"), (bk, "bk"), (bv, "bv")):
                sp.dma_start(dst[:, :], a[n]).then_inc(bias_loaded, 16)
            sp.dma_start(bo[:, :], a["bo"].to_broadcast([P, D])).then_inc(bias_loaded, 16)

            dq_o.load(sp, 0, a["o_codes"][0], a["o_scales"][0])
            for e in range(4):
                sp.dma_start(g["w13"][:, e, :, :], a["w13"][e]).then_inc(g["ew_loaded"][e], 16)
                sp.dma_start(g["w2"][:, e, :, :], a["w2"][e]).then_inc(g["ew_loaded"][e], 16)
            sp.wait_ge(zeroed, 2)
            RT = 8
            for i in range(E // RT):
                dst = g["xbuf"].rearrange("(i r p) d -> i p r d", r=RT, p=P)[i]
                sp.dma_start(dst, zero[:, :].unsqueeze(1).to_broadcast([P, RT, DX])).then_inc(xbuf_zeroed, 16)

            def group(gr, last):
                for j in range(HG):
                    if last and j >= HG - 2:
                        break
                    h = gr * HG + j
                    sp.wait_ge(dq_qk.lo_ready, h + 1)
                    dq_qk.load(sp, j % 2, a["qk_codes"][h + 2], a["qk_scales"][h + 2])
                    if j == 0 and not last:
                        sp.wait_ge(dq_v.lo_ready, gr + 1)
                        dq_v.load(sp, 0, a["v_codes"][gr + 1], a["v_scales"][gr + 1])
                if not last:
                    sp.wait_ge(dq_o.lo_ready, gr + 1)
                    dq_o.load(sp, 0, a["o_codes"][gr + 1], a["o_scales"][gr + 1])

            with sp.Fori(0, G - 1) as gr:
                group(gr, False)
            group(G - 1, True)
            sp.wait_ge(xbuf_zeroed, 16 * (E // RT))

        @block.gpsimd
        def _(pool):
            pool.memset(pT[:, :, :], 0.0).then_inc(zeroed, 1)
            pool.memset(zero[:, :], 0.0).then_inc(zeroed, 1)
            pool.wait_ge(zeroed, 2)

            pool.wait_ge(norm.normed, T)
            pool.wait_ge(bias_loaded, 64)
            for t in range(T):
                pool.tensor_tensor(xres[:, t, :], xres[:, t, :], bo[:, :], ALU.add).then_inc(bo_added, 1)

            def group(gr, first, last):
                for j in range(HG):
                    h = gr * HG + j
                    if not (last and j >= HG - 2):
                        dq_qk.pool(pool, h + 2, j % 2, gr * 2 + (j // 2 + 2), (k_proj, h * 2 + 2))
                    if j == 0:
                        dq_o.pool(pool, gr, 0, gr + 1, None if first else (o_proj, gr * T))
                    if j == 1 and not last:
                        dq_v.pool(pool, gr + 1, 0, gr + 2, (v_proj, gr * T + T))

            group(0, True, False)
            with pool.Fori(1, G - 1) as gr:
                group(gr, False, False)
            group(G - 1, False, True)

        @block.scalar
        def _(act):
            def evac_q(h):
                act.wait_ge(q_proj, h + 1)
                act.activation(qT[:, :], psum[:, 0:2, :].rearrange("p b n -> p (b n)"), ACT.Identity,
                               bias=bq[:, bass.ds(h, 1)]).then_inc(q_evac, 1)

            def softmax(h):
                act.wait_ge(s_done, h + 1)
                for q in range(4):
                    r = slice(32 * q, 32 * q + 32)
                    ins = act.activation(sc[r, :, :], S2[r, :, r], ACT.Copy)
                ins.then_inc(s_evac, 1)
                act.wait_ge(s_shift, h + 1)
                act.activation(sc[:, :, :], sc[:, :, :], ACT.Exp, scale=SCALE).then_inc(s_exp, 1)

            def evac_o(h, j):
                act.wait_ge(pv_done, h + 1)
                act.activation(oT[0][:, j, :], O2, ACT.Identity, bias=bv[:, bass.ds(h, 1)]).then_inc(o_hi, 1)

            act.wait_ge(bias_loaded, 64)
            norm.root(act)

            def evac_v(gr, t):
                act.wait_ge(v_proj, gr * T + (t + 1))
                act.activation(vsb[:, t, :], pb[v_bank(t)][:, :], ACT.Copy).then_inc(v_evac, 1)

            for t in range(T):
                norm.high(act, t, t % 2)
                if t >= 2:
                    evac_v(0, t - 2)
            evac_q(0)
            evac_v(0, T - 2)
            evac_v(0, T - 1)

            def group(gr, first, last):
                for j in range(HG):
                    h = gr * HG + j
                    softmax(h)
                    if not (last and j >= HG - 2):
                        dq_qk.scalar(act, h + 2, j % 2, (k_proj, h * 2 + 2))
                    if j < HG - 1:
                        evac_q(h + 1)
                    evac_o(h, j)
                    if j == 0:
                        dq_o.scalar(act, gr, 0, None if first else (o_proj, gr * T))
                    if j == 1 and not last:
                        dq_v.scalar(act, gr + 1, 0, (v_proj, gr * T + T))
                if not last:
                    for t in range(T - 2):
                        evac_v(gr + 1, t)
                    evac_q(gr * HG + HG)
                    evac_v(gr + 1, T - 2)
                    evac_v(gr + 1, T - 1)

            group(0, True, False)
            with act.Fori(1, G - 1) as gr:
                group(gr, False, False)
            group(G - 1, False, True)

        @block.vector
        def _(dve):
            dve.wait_ge(norm.stats_ready, T)
            norm.vector(dve)
            st = Steps(dve, s_steps)
            dve.wait_ge(bias_loaded, 64)
            dve.wait_ge(zeroed, 1)
            dve.wait_ge(bo_added, T)

            def evac_k(h):
                for half in range(2):
                    dve.wait_ge(k_proj, h * 2 + (half + 1))
                    dve.tensor_scalar(kT[:, half * HALF:(half + 1) * HALF], pb[2 + half][:, :],
                                      bk[:, bass.ds(h, 1)], None, ALU.add).then_inc(k_evac, 1)

            def softmax(h):
                st.n = h * 4
                dve.wait_ge(s_evac, h + 1)
                st.done(dve.tensor_reduce(smax[:, :], sc[:, :, :], AX.X, ALU.max))
                st.wait()
                dve.tensor_tensor(sc[:, :, :], sc[:, :, :], smax[:, :].unsqueeze(2).to_broadcast([P, T, L]),
                                  ALU.subtract).then_inc(s_shift, 1)
                dve.wait_ge(s_exp, h + 1)
                st.done(dve.tensor_reduce(ssum[:, :], sc[:, :, :], AX.X, ALU.add))
                st.wait()
                st.done(dve.reciprocal(srec[:, :], ssum[:, :]))
                st.wait()
                st.done(dve.tensor_tensor(sc[:, :, :], sc[:, :, :],
                                          srec[:, :].unsqueeze(2).to_broadcast([P, T, L]), ALU.mult))
                st.wait()
                for q in range(4):
                    r = slice(32 * q, 32 * q + 32)
                    ins = dve.transpose(pT[r, :, r], sc[r, :, :])
                ins.then_inc(pt_ready, 1)

            def evac_o(h, j):
                dve.wait_ge(o_hi, h + 1)
                dve.scalar_tensor_tensor(out=oT[1][:, j, :], in0=O2, scalar=bv[:, bass.ds(h, 1)],
                                         in1=oT[0][:, j, :], op0=ALU.add, op1=ALU.subtract).then_inc(o_lo, 1)

            with dve.Fori(0, G) as gr:
                for j in range(HG):
                    h = dve.snap(gr * HG + j)
                    if j == 0:
                        evac_k(h)
                    softmax(h)
                    if j < HG - 1:
                        evac_k(h + 1)
                    evac_o(h, j)
                for t in range(T):
                    dve.wait_ge(o_proj, gr * T + (t + 1))
                    dve.tensor_tensor(xres[:, t, :], xres[:, t, :], pb[t % 4][:, :], ALU.add).then_inc(o_added, 1)
            for t in range(T):
                dve.wait_ge(o_added, (G - 1) * T + t + 1)
                n3.statistics(dve, t)

        @block.tensor
        def _(pe):
            def v_tile(gr, t):
                if t == 0:
                    pe.wait_ge(dq_v.lo_ready, gr + 1)
                if 2 <= t < T - 2:
                    pe.wait_ge(v_evac, gr * T + (t - 1))
                split_matmuls(pe, pb[v_bank(t)][:, :], lambda s, c: xT[s][:, c, t * P:(t + 1) * P],
                              lambda s, c: v_w[s][:, c, :], range(CC)).then_inc(v_proj, 1)

            def qk(h, par):
                pe.wait_ge(dq_qk.lo_ready, h + 1)
                for m in range(2):
                    for half in range(2):
                        ins = split_matmuls(pe, pb[2 * m + half][:, :], lambda s, c: qk_w[s][:, par, m, c, :],
                                            lambda s, c: xT[s][:, c, half * HALF:(half + 1) * HALF], range(CC))
                        if m:
                            ins.then_inc(k_proj, 1)
                    if not m:
                        ins.then_inc(q_proj, 1)

            def scores(h, first):
                pe.wait_ge(q_evac, h + 1)
                pe.wait_ge(k_evac, h * 2 + 2)
                if not (first and h == 0):
                    pe.wait_ge(s_evac, h)
                for t in range(T):
                    r = slice(t * P, (t + 1) * P)
                    ins = pe.matmul(S2[:, t, :], qT[:, r], kT[:, r], start=True, stop=True)
                ins.then_inc(s_done, 1)

            def values(h, j, first):
                pe.wait_ge(pt_ready, h + 1)
                if not (first and h == 0):
                    pe.wait_ge(o_lo, h)
                for t in range(T):
                    ins = pe.matmul(O2[:, t * P:(t + 1) * P], vsb[:, t, j * P:(j + 1) * P], pT[:, t, :],
                                    start=True, stop=True)
                ins.then_inc(pv_done, 1)

            def out_part(gr, t, heads):
                for j in heads:
                    for s, (u, v) in enumerate(((0, 0), (0, 1), (1, 0))):
                        ins = pe.matmul(pb[t % 4][:, :], oT[u][:, j, t * P:(t + 1) * P], o_w[v][:, j, :],
                                        start=(j == 0 and s == 0), stop=(j == HG - 1 and s == 2))
                return ins

            def group(gr, first, last):
                for j in range(HG):
                    h = gr * HG + j
                    if j == 0:
                        pe.wait_ge(v_evac, gr * T + T - 2)
                    scores(h, first)
                    if j < HG - 1:
                        qk(h + 1, (j + 1) % 2)
                    else:
                        pe.wait_ge(dq_o.lo_ready, gr + 1)
                        pe.wait_ge(o_lo, h)
                        for t in range(4):
                            out_part(gr, t, range(HG - 1))
                    if j == 0:
                        pe.wait_ge(v_evac, gr * T + T)
                    values(h, j, first)
                if not last:
                    for t in range(T - 2):
                        v_tile(gr + 1, t)
                pe.wait_ge(o_lo, gr * HG + HG)
                for t in range(4):
                    out_part(gr, t, [HG - 1]).then_inc(o_proj, 1)
                for t in range(4, T):
                    pe.wait_ge(o_added, gr * T + (t - 3))
                    out_part(gr, t, range(HG)).then_inc(o_proj, 1)
                if not last:
                    pe.wait_ge(o_added, gr * T + T)
                    qk(gr * HG + HG, 0)
                    for t in range(T - 2, T):
                        v_tile(gr + 1, t)

            norm.turn(pe, 0)
            norm.turn(pe, 1)
            for t in range(T - 2):
                pe.wait_ge(norm.lo_ready, t + 1)
                v_tile(0, t)
                norm.turn(pe, t + 2)
            pe.wait_ge(norm.lo_ready, T)
            qk(0, 0)
            for t in range(T - 2, T):
                v_tile(0, t)
            group(0, True, False)
            with pe.Fori(1, G - 1) as gr:
                group(gr, False, False)
            group(G - 1, False, True)


def stage_c(nc, a, g):
    xres, xT, ident, pb, psum = g["xres"], g["xT"], g["ident"], g["pb"], g["psum"]
    w13, w2, ew_loaded = g["w13"], g["w2"], g["ew_loaded"]
    xbuf, out = g["xbuf"], g["out"]
    FC = F // P
    PAD = 8
    LAST = E // 4 - 1
    with ExitStack() as ctx:
        def sb(n, shape, dt=F32):
            return ctx.enter_context(nc.sbuf_tensor(n, shape, dt))

        def sem(n):
            return ctx.enter_context(nc.semaphore(n))

        x3 = sb("x3", [P, T, DX])
        names = ["sg", "su", "sd"]
        raw = {n: g["stage"][:, i, :].rearrange("p (c n) -> p c n", c=CC) for i, n in enumerate(names)}
        w = {n: tuple(g["split"][:, 2 * i + s, :].rearrange("p (c n) -> p c n", c=CC) for s in (0, 1))
             for i, n in enumerate(names[:2])}
        w["sd"] = tuple(sb(f"sd_{s}", [P, CC, D], F16)[:, :, :] for s in ("hi", "lo"))
        gw_raw = sb("gw_raw", [P, CC, E])
        gw = (sb("gw_hi", [P, CC, E], F16), sb("gw_lo", [P, CC, E], F16))
        gb = sb("gb", [P, E])
        tri, tri_f = sb("tri", [P, P], F16), sb("tri_f", [P, P])
        ones = sb("ones16", [P, P], F16)
        e256i, e256 = sb("e256i", [P, E], I32), sb("e256", [P, E])
        score = sb("score", [P, T, E])
        biased = sb("biased", [P, T, E])
        m8 = sb("m8", [P, T * EG, 8])
        gs = sb("gs", [P, T, EG + PAD])
        gm8 = sb("gm8", [P, T, 8])
        gsel = sb("gsel", [P, T, EG + PAD])
        gmask = sb("gmask", [P, T, EG])
        tmp = sb("tmp", [P, T, E + PAD])
        em8 = sb("em8", [P, T, 8])
        esel = sb("esel", [P, T, E + PAD])
        chosen = sb("chosen", [P, T, E])
        chosen16 = sb("chosen16", [P, T, E], F16)
        wt = sb("wt", [P, T, E])
        wsum = sb("wsum", [P, T])
        pos = sb("pos", [P, T, E])
        key = sb("key", [P, T, E])
        k8 = sb("k8", [P, T, 8])
        numi = sb("numi", [P, T], I32)
        ki, kp, ke, kd = (sb(n, [P, T, K], I32) for n in ("ki", "kp", "ke", "kd"))
        scat = sb("scat", [P, T, K], I32)
        ssil, sup, sh = sb("ssil", [P, D]), sb("sup", [P, D]), sb("sh", [P, D])
        sT = tuple(sb(f"sT_{s}", [P, CC, N], F16) for s in ("hi", "lo"))
        s3, s4 = g["stage"][:, 3, :], g["stage"][:, 4, :]
        xe = s3[:, 0:2 * DX].rearrange("p (b n) -> p b n", b=2)
        xeT = s3[:, 2 * DX:2 * DX + D].rearrange("p (c n) -> p c n", c=CC)
        y = s4[:, 0:2 * D].rearrange("p (b n) -> p b n", b=2)
        hT = s4[:, 2 * D:2 * D + F].rearrange("p (f n) -> p f n", f=FC)
        hsil, hh = (s4[:, 2 * D + i * F:2 * D + (i + 1) * F] for i in (1, 2))
        we = sb("we", [P, 4])
        ne = sb("ne", [P, 4], I32)

        sh_loaded = {n: sem(f"{n}_loaded") for n in names}
        gw_loaded = sem("gw_loaded")
        w_hi = sem("c_w_hi")
        w_lo = sem("c_w_lo")
        consts = sem("c_consts")
        logits = sem("logits")
        score_ready = sem("score_ready")
        r_steps = sem("r_steps")
        chosen_ready = sem("chosen_ready")
        pos_done = sem("pos_done")
        idx_ready = sem("idx_ready")
        scattered = sem("scattered")
        sg_proj = sem("sg_proj")
        su_proj = sem("su_proj")
        s_silu = sem("s_silu")
        s_up = sem("s_up")
        s_h = sem("s_h")
        s_hi = sem("s_hi")
        s_lo = sem("s_lo")
        sd_proj = sem("sd_proj")
        s_added = sem("s_added")
        xe_loaded = [sem(f"xe_loaded{i}") for i in range(2)]
        xe_turned = sem("xe_turned")
        xeT_ready = sem("xeT_ready")
        up_done = sem("up_done")
        e_silu = sem("e_silu")
        h_ready = sem("h_ready")
        h_turned = sem("h_turned")
        hT_ready = sem("hT_ready")
        down_done = sem("down_done")
        y_ready = sem("y_ready")
        xe_used = sem("xe_used")
        y_added = sem("y_added")
        number_ready = sem("number_ready")
        out_stored = sem("out_stored")

        norm = g["n3"]
        norm.banks, norm.keep = [pb[4], pb[5]], x3[:, :, 0:D]
        LG = pb[6][:, 0:T * E].rearrange("p (t e) -> p t e", e=E)
        PS = pb[7][:, 0:T * E].rearrange("p (t e) -> p t e", e=E)

        def shared_half(eng, j, half, first):
            n = j * 2 + half
            if not first:
                eng.wait_ge(s_lo, n)
            eng.wait_ge(s_up, n + 1)
            eng.tensor_tensor(sh[:, :], ssil[:, :], sup[:, :], ALU.mult).then_inc(s_h, 1)
            eng.wait_ge(s_hi, n + 1)
            eng.tensor_tensor(sT[1][:, j, half * HALF:(half + 1) * HALF], sh[:, :],
                              sT[0][:, j, half * HALF:(half + 1) * HALF], ALU.subtract).then_inc(s_lo, 1)

        block = ctx.enter_context(nc.Block())

        @block.sync
        def _(sp):
            sp.dma_start(gw_raw[:, :, :], a["gate_w"]).then_inc(gw_loaded, 16)
            sp.dma_start(gb[:, :], a["gate_bias"].to_broadcast([P, E])).then_inc(gw_loaded, 16)
            for n in names:
                sp.dma_start(raw[n], a[n]).then_inc(sh_loaded[n], 16)
            sp.wait_ge(scattered, 16 * T * K)
            for e in range(2):
                sp.dma_start(xe[:, e, :], xbuf[e * CAP:(e + 1) * CAP, :]).then_inc(xe_loaded[e], 16)
            o = out.rearrange("(t p) d -> t p d", p=P)
            for t in range(T):
                sp.wait_ge(s_added, t + 1)
                sp.dma_start(o[t], xres[:, t, :]).then_inc(out_stored, 16)

            def loads(i, q, first, last):
                e = i * 4 + q
                if not (last and q >= 2):
                    sp.wait_ge(xe_used, e + 1)
                    sp.dma_start(xe[:, q % 2, :], xbuf[bass.ds((e + 2) * CAP, CAP), :]
                                 ).then_inc(xe_loaded[q % 2], 16)
                if (first and q == 0) or (last and q >= 1):
                    return
                sp.wait_ge(down_done, e)
                slot = (q + 3) % 4
                sp.dma_start(w13[:, slot, :, :], a["w13"][e + 3]).then_inc(ew_loaded[slot], 16)
                sp.dma_start(w2[:, slot, :, :], a["w2"][e + 3]).then_inc(ew_loaded[slot], 16)

            for q in range(4):
                loads(0, q, True, False)
            with sp.Fori(1, LAST) as i:
                for q in range(4):
                    loads(i, q, False, False)
            for q in range(4):
                loads(LAST, q, False, True)

        @block.gpsimd
        def _(pool):
            pool.memset(tri_f[:, :], 1.0).then_inc(consts, 1)
            pool.wait_ge(consts, 1)
            pool.affine_select(out=tri_f[:, :], in_=tri_f[:, :], compare_op=ALU.is_gt, fill=0.0, base=0,
                               pattern=[[1, P]], channel_multiplier=-1).then_inc(consts, 1)
            pool.wait_ge(consts, 2)
            pool.tensor_copy(tri[:, :], tri_f[:, :]).then_inc(consts, 1)
            pool.memset(ones[:, :], 1.0).then_inc(consts, 1)
            pool.iota(e256i[:, :], [[2 * CAP, E]], base=1, channel_multiplier=0).then_inc(consts, 1)
            pool.wait_ge(consts, 5)
            pool.tensor_copy(e256[:, :], e256i[:, :]).then_inc(consts, 1)
            pool.iota(numi[:, :], [[-P, T]], base=2 * N, channel_multiplier=-1).then_inc(number_ready, 1)
            pool.wait_ge(number_ready, 1)
            pool.tensor_copy(x3[:, :, NUM], numi[:, :]).then_inc(number_ready, 1)
            pool.memset(x3[:, :, NUM + 1:DX], 0.0).then_inc(number_ready, 1)
            pool.wait_ge(w_hi, 1)
            pool.tensor_tensor(gw[1][:, :, :], gw_raw[:, :, :], gw[0][:, :, :], ALU.subtract).then_inc(w_lo, 1)
            for k, n in enumerate(names):
                pool.wait_ge(w_hi, k + 2)
                pool.tensor_tensor(w[n][1], raw[n], w[n][0], ALU.subtract).then_inc(w_lo, 1)

            shared_half(pool, 0, 0, True)
            shared_half(pool, 0, 1, False)
            shared_half(pool, 1, 0, False)
            shared_half(pool, 1, 1, False)
            pool.wait_ge(number_ready, 3)
            pool.wait_ge(idx_ready, 1)
            for t in range(T):
                for k in range(K):
                    pool.indirect_dma_start(xbuf, bass.IndirectOffsetOnAxis(ap=scat[:, t, k:k + 1], axis=0),
                                            x3[:, t, :], None, bounds_check=E * CAP - 1,
                                            oob_is_err=False).then_inc(scattered, 16)
            pool.wait_ge(out_stored, 16 * T)

            for e in range(E):
                pool.wait_ge(y_ready, e + 1)
                if e:
                    pool.wait_ge(y_added, e * 16)
                pool.indirect_dma_start(out, bass.IndirectOffsetOnAxis(ap=ne[:, e % 4:e % 4 + 1], axis=0),
                                        y[:, e % 2, :], None, bounds_check=N - 1, oob_is_err=False,
                                        compute_op=ALU.add).then_inc(y_added, 16)
            pool.wait_ge(y_added, 16 * E)

        @block.scalar
        def _(act):
            norm.root(act)
            act.wait_ge(gw_loaded, 32)
            act.activation(gw[0][:, :, :], gw_raw[:, :, :], ACT.Copy).then_inc(w_hi, 1)
            norm.high(act, 0, 0)
            norm.high(act, 1, 1)
            for n in names:
                act.wait_ge(sh_loaded[n], 16)
                act.activation(w[n][0], raw[n], ACT.Copy).then_inc(w_hi, 1)
            for t in range(2, T):
                norm.high(act, t, t % 2)
            act.wait_ge(logits, 1)
            act.activation(score[:, :, :], LG, ACT.Sigmoid).then_inc(score_ready, 1)

            def gate_up(j, half, first):
                n = j * 2 + half
                act.wait_ge(sg_proj, n + 1)
                if not first:
                    act.wait_ge(s_h, n)
                act.activation(ssil[:, :], pb[half][:, :], ACT.Silu).then_inc(s_silu, 1)
                act.wait_ge(su_proj, n + 1)
                act.activation(sup[:, :], pb[2 + half][:, :], ACT.Copy).then_inc(s_up, 1)
                act.wait_ge(s_h, n + 1)
                act.activation(sT[0][:, j, half * HALF:(half + 1) * HALF], sh[:, :], ACT.Copy).then_inc(s_hi, 1)

            gate_up(0, 0, True)
            gate_up(0, 1, False)
            with act.Fori(1, CC) as j:
                gate_up(j, 0, False)
                gate_up(j, 1, False)

            def rows_out(e, slot, added):
                act.wait_ge(down_done, e + 1)
                if added is not None:
                    act.wait_ge(y_added, added)
                act.activation(y[:, slot % 2, :], pb[6][:, :], ACT.Copy, scale=we[:, slot:slot + 1]).then_inc(y_ready, 1)

            def expert(i, q, first):
                e = i * 4 + q
                act.wait_ge(up_done, e + 1)
                if not (first and q == 0):
                    act.wait_ge(h_ready, e)
                act.activation(hsil[:, :], pb[1][:, 0:F], ACT.Silu).then_inc(e_silu, 1)
                if not (first and q == 0):
                    rows_out(e - 1, (q + 3) % 4, None if first and q < 3 else e * 16 - 32)
                act.wait_ge(h_turned, e + 1)
                act.activation(hT[:, :, :], pb[3][:, 0:F].rearrange("p (c n) -> p c n", c=FC),
                               ACT.Copy).then_inc(hT_ready, 1)

            for q in range(4):
                expert(0, q, True)
            with act.Fori(1, E // 4) as i:
                for q in range(4):
                    expert(i, q, False)
            rows_out(E - 1, 3, 16 * (E - 2))

        @block.vector
        def _(dve):
            dve.wait_ge(norm.stats_ready, T)
            norm.vector(dve)
            st = Steps(dve, r_steps)

            def then(ins):
                st.done(ins)
                st.wait()

            st.done(dve.memset(gs[:, :, EG:EG + PAD], -BIG))
            st.done(dve.memset(tmp[:, :, E:E + PAD], -BIG))
            dve.wait_ge(score_ready, 1)
            then(dve.tensor_tensor(biased[:, :, :], score[:, :, :],
                                   gb[:, :].unsqueeze(1).to_broadcast([P, T, E]), ALU.add))
            per = E // EG
            for t in range(T):
                for gr in range(EG):
                    st.done(dve.max(m8[:, t * EG + gr, :], biased[:, t, gr * per:(gr + 1) * per]))
            st.wait()
            m8v = m8[:, :, :].rearrange("p (t g) k -> p t g k", g=EG)
            then(dve.tensor_tensor(gs[:, :, 0:EG], m8v[:, :, :, 0], m8v[:, :, :, 1], ALU.add))
            for t in range(T):
                st.done(dve.max(gm8[:, t, :], gs[:, t, :]))
            st.wait()
            then(dve.memset(gm8[:, :, 2:8], -BIG))
            for t in range(T):
                st.done(dve.match_replace(gsel[:, t, :], gm8[:, t, :], gs[:, t, :], BIG))
            st.wait()
            then(dve.tensor_scalar(gmask[:, :, :], gsel[:, :, 0:EG], BIG, None, ALU.is_equal))
            then(dve.tensor_tensor(tmp[:, :, 0:E].rearrange("p t (g n) -> p t g n", g=EG),
                                   biased[:, :, :].rearrange("p t (g n) -> p t g n", g=EG),
                                   gmask[:, :, :].unsqueeze(3).to_broadcast([P, T, EG, per]), ALU.mult))
            then(dve.tensor_scalar(tmp[:, :, 0:E], tmp[:, :, 0:E], 0.0, None, ALU.add))
            for t in range(T):
                st.done(dve.max(em8[:, t, :], tmp[:, t, 0:E]))
            st.wait()
            then(dve.memset(em8[:, :, K:8], -BIG))
            for t in range(T):
                st.done(dve.match_replace(esel[:, t, :], em8[:, t, :], tmp[:, t, :], BIG))
            st.wait()
            then(dve.tensor_scalar(chosen[:, :, :], esel[:, :, 0:E], BIG, None, ALU.is_equal))
            dve.tensor_copy(chosen16[:, :, :], chosen[:, :, :]).then_inc(chosen_ready, 1)
            then(dve.tensor_tensor(wt[:, :, :], score[:, :, :], chosen[:, :, :], ALU.mult))
            then(dve.tensor_reduce(wsum[:, :], wt[:, :, :], AX.X, ALU.add))
            then(dve.tensor_scalar(wsum[:, :], wsum[:, :], EPS_W, None, ALU.add))
            then(dve.reciprocal(wsum[:, :], wsum[:, :]))
            then(dve.tensor_scalar(wsum[:, :], wsum[:, :], ROUTE_SCALE, None, ALU.mult))
            then(dve.tensor_tensor(wt[:, :, :], wt[:, :, :], wsum[:, :].unsqueeze(2).to_broadcast([P, T, E]),
                                   ALU.mult))
            dve.wait_ge(pos_done, 1)
            dve.wait_ge(consts, 6)
            then(dve.tensor_scalar(pos[:, :, :], PS, float(CAP), None, ALU.min))
            st.done(dve.tensor_copy(x3[:, :, D:NUM], wt[:, :, :]))
            then(dve.tensor_tensor(pos[:, :, :], pos[:, :, :],
                                   e256[:, :].unsqueeze(1).to_broadcast([P, T, E]), ALU.add))
            then(dve.tensor_tensor(key[:, :, :], pos[:, :, :], chosen[:, :, :], ALU.mult))
            for t in range(T):
                st.done(dve.max(k8[:, t, :], key[:, t, :]))
            st.wait()
            then(dve.tensor_scalar(ki[:, :, :], k8[:, :, 0:K], -1.0, None, ALU.add))
            st.done(dve.tensor_scalar(ke[:, :, :], ki[:, :, :], 8, 7, ALU.logical_shift_right,
                                      ALU.logical_shift_left))
            then(dve.tensor_scalar(kp[:, :, :], ki[:, :, :], 255, None, ALU.bitwise_and))
            then(dve.tensor_scalar(kd[:, :, :], kp[:, :, :], 7, 13, ALU.logical_shift_right,
                                   ALU.logical_shift_left))
            then(dve.tensor_tensor(scat[:, :, :], ke[:, :, :], kp[:, :, :], ALU.add))
            dve.tensor_tensor(scat[:, :, :], scat[:, :, :], kd[:, :, :], ALU.add).then_inc(idx_ready, 1)
            with dve.Fori(2, CC) as j:
                shared_half(dve, j, 0, False)
                shared_half(dve, j, 1, False)
            with dve.Fori(0, T // 2) as i:
                for par in range(2):
                    t = dve.snap(i * 2 + par)
                    dve.wait_ge(sd_proj, t + 1)
                    dve.tensor_tensor(xres[:, t, :], xres[:, t, :], pb[4 + par][:, :], ALU.add).then_inc(s_added, 1)

            def rows(e, q, first):
                dve.wait_ge(xe_turned, e + 1)
                dve.tensor_copy(xeT[:, :, :], pb[0][:, :].rearrange("p (c n) -> p c n", c=CC)).then_inc(xeT_ready, 1)
                if not first:
                    dve.wait_ge(y_added, e * 16 - 48)
                dve.tensor_copy(we[:, q:q + 1], xe[:, q % 2, bass.ds(e + D, 1)])
                dve.tensor_scalar(ne[:, q:q + 1], xe[:, q % 2, NUM:NUM + 1], -1.0, 2.0 * N, ALU.mult,
                                  ALU.add).then_inc(xe_used, 1)

            def hidden(e):
                dve.wait_ge(e_silu, e + 1)
                dve.tensor_tensor(hh[:, :], hsil[:, :], pb[1][:, F:2 * F], ALU.mult).then_inc(h_ready, 1)

            rows(0, 0, True)
            for e in range(3):
                rows(e + 1, e + 1, True)
                hidden(e)
            with dve.Fori(1, E // 4) as i:
                for q in range(4):
                    e = dve.snap(i * 4 + q)
                    rows(e, q, False)
                    hidden(e - 1)
            hidden(E - 1)

        @block.tensor
        def _(pe):
            for t in range(T):
                norm.turn(pe, t)
            pe.wait_ge(norm.lo_ready, T)
            pe.wait_ge(w_lo, 1)
            for t in range(T):
                ins = split_matmuls(pe, LG[:, t, :], lambda s, c: xT[s][:, c, t * P:(t + 1) * P],
                                    lambda s, c: gw[s][:, c, :], range(CC))
            ins.then_inc(logits, 1)
            pe.wait_ge(w_lo, 3)

            def shared(j, reuse):
                for m, n in enumerate(("sg", "su")):
                    for half in range(2):
                        if reuse:
                            pe.wait_ge(s_up if m else s_silu, j * 2 + (half - 1))
                        split_matmuls(pe, pb[2 * m + half][:, :], lambda s, c: w[n][s][:, c, bass.ds(j * P, P)],
                                      lambda s, c: xT[s][:, c, half * HALF:(half + 1) * HALF],
                                      range(CC)).then_inc(su_proj if m else sg_proj, 1)

            shared(0, False)
            shared(1, True)
            pe.wait_ge(chosen_ready, 1)
            pe.wait_ge(consts, 4)
            for t in range(T):
                for u in range(t + 1):
                    ins = pe.matmul(PS[:, t, :], (tri if u == t else ones)[:, :], chosen16[:, u, :],
                                    start=(u == 0), stop=(u == t))
            ins.then_inc(pos_done, 1)
            with pe.Fori(2, CC) as j:
                shared(j, True)
            pe.wait_ge(s_lo, 2 * CC)
            pe.wait_ge(w_lo, 4)

            def down(t, par, reuse):
                if reuse:
                    pe.wait_ge(s_added, t - 1)
                split_matmuls(pe, pb[4 + par][:, :], lambda s, c: sT[s][:, c, bass.ds(t * P, P)],
                              lambda s, c: w["sd"][s][:, c, :], range(CC)).then_inc(sd_proj, 1)

            down(0, 0, False)
            down(1, 1, False)
            with pe.Fori(1, T // 2) as i:
                for par in range(2):
                    down(pe.snap(i * 2 + par), par, True)

            def turn_x(e, par, loads):
                pe.wait_ge(xe_loaded[par], loads)
                for c in range(CC):
                    ins = pe.transpose(pb[0][:, c * P:(c + 1) * P], xe[:, par, c * P:(c + 1) * P], ident)
                ins.then_inc(xe_turned, 1)

            def expert_down(e, slot, reuse):
                pe.wait_ge(hT_ready, e + 1)
                if reuse:
                    pe.wait_ge(y_ready, e)
                for f in range(FC):
                    ins = pe.matmul(pb[6][:, :], hT[:, f, :], w2[:, slot, f, :], start=(f == 0), stop=(f == FC - 1))
                ins.then_inc(down_done, 1)

            def expert(i, q, first, last):
                e = i * 4 + q
                pe.wait_ge(ew_loaded[q], i * 32 + 32)
                pe.wait_ge(xeT_ready, e + 1)
                for c in range(CC):
                    ins = pe.matmul(pb[1][:, :], xeT[:, c, :], w13[:, q, c, :], start=(c == 0), stop=(c == CC - 1))
                ins.then_inc(up_done, 1)
                if not (last and q == 3):
                    turn_x(e + 1, (q + 1) % 2, i * 32 + 16 * ((q + 1) // 2 + 1))
                if not (first and q == 0):
                    expert_down(e - 1, (q + 3) % 4, not (first and q == 1))
                pe.wait_ge(h_ready, e + 1)
                for f in range(FC):
                    ins = pe.transpose(pb[3][:, f * P:(f + 1) * P], hh[:, f * P:(f + 1) * P], ident)
                ins.then_inc(h_turned, 1)

            turn_x(0, 0, 16)
            for q in range(4):
                expert(0, q, True, False)
            with pe.Fori(1, LAST) as i:
                for q in range(4):
                    expert(i, q, False, False)
            for q in range(4):
                expert(LAST, q, False, True)
            expert_down(E - 1, 3, True)


def build(nc, a, out):
    with ExitStack() as ctx:
        g = {
            "xres": ctx.enter_context(nc.sbuf_tensor("xres", [P, T, D], F32)),
            "xT": tuple(ctx.enter_context(nc.sbuf_tensor(f"xT_{s}", [P, CC, N], F16)) for s in ("hi", "lo")),
            "ident": ctx.enter_context(nc.sbuf_tensor("ident", [P, P], F32)),
            "out": out,
        }
        psum = ctx.enter_context(nc.psum_tensor("psum", [P, 8, 512], F32))
        g["psum"] = psum
        g["pb"] = [psum[:, i, :] for i in range(8)]
        g["ident"] = g["ident"][:, :]
        stage = g["stage"] = ctx.enter_context(nc.sbuf_tensor("stage", [P, 5, CC * D], F32))
        split = g["split"] = ctx.enter_context(nc.sbuf_tensor("split", [P, 4, CC * D], F16))

        def two(ap):
            return [ap[:, i * CC * D // 2:(i + 1) * CC * D // 2] for i in range(2)]

        g["dq_v"] = Dequant(nc, ctx, "v", [stage[:, 0, :]], [stage[:, 1, :]], [split[:, 0, :]], [split[:, 1, :]], 1)
        g["dq_qk"] = Dequant(nc, ctx, "qk", two(stage[:, 2, :]), two(stage[:, 3, :]), two(split[:, 2, :]),
                             two(split[:, 3, :]), 2)
        g["n2"] = Norm(nc, ctx, "n2", g["xres"], g["ident"], g["xT"], None)
        g["n3"] = Norm(nc, ctx, "n3", g["xres"], g["ident"], g["xT"], None)
        stage_a(nc, a, g)
        g["w13"] = ctx.enter_context(nc.sbuf_tensor("w13_sb", [P, 4, CC, 2 * F], F32))
        g["w2"] = ctx.enter_context(nc.sbuf_tensor("w2_sb", [P, 4, F // P, D], F32))
        g["ew_loaded"] = [ctx.enter_context(nc.semaphore(f"ew_loaded{i}")) for i in range(4)]
        g["xbuf"] = nc.dram_tensor("xbuf", [E * CAP, DX], F32).ap()
        stage_b(nc, a, g)
        stage_c(nc, a, g)



def layouts(i):
    import numpy as np

    c=np.ascontiguousarray
    Pn=128
    def kc(m):
        return c(m.reshape(m.shape[0]//Pn,Pn,-1).transpose(1,0,2))
    o={}
    o['x']=c(i['x'].reshape(1024,512))
    ctx=i['ctx_2048']
    o['ctx']=c(ctx[:,:256].transpose(0,2,1).reshape(32,4,Pn,256).transpose(0,2,1,3))
    o['ctx_last']=c(ctx[:,256].T.reshape(4,Pn,32).transpose(1,0,2))
    for n in ('Wq','Wg','Wkv','Wo'): o[n]=kc(i['L0_xattn_'+n].T)
    o['bg']=c(i['L0_xattn_bg'].reshape(4,Pn).T)
    def sw(n): return i['L0_attn_w%s_codes'%n], i['L0_attn_w%s_scales'%n]
    def heads(w): return w.reshape(4,Pn,16,Pn).transpose(2,1,0,3)
    def hsc(w): return w.reshape(4,4,16,Pn).transpose(2,1,0,3)
    q,qs=sw('q'); k,ks=sw('k'); v,vs=sw('v'); w,ws=sw('o')
    o['qk_codes']=c(np.stack([heads(q),heads(k)],2).reshape(16,Pn,1024))
    o['qk_scales']=c(np.stack([hsc(qs),hsc(ks)],2).reshape(16,4,1024))
    o['v_codes']=c(v.reshape(4,Pn,4,512).transpose(2,1,0,3).reshape(4,Pn,2048))
    o['v_scales']=c(vs.reshape(4,4,4,512).transpose(2,1,0,3).reshape(4,4,2048))
    o['o_codes']=c(w.reshape(4,4,Pn,512).transpose(0,2,1,3).reshape(4,Pn,2048))
    o['o_scales']=c(ws.reshape(4,4,4,512).transpose(0,2,1,3).reshape(4,4,2048))
    for n in ('bq','bk','bv'): o[n]=c(i['L0_attn_'+n].reshape(16,Pn).T)
    o['gate_w']=kc(i['L0_ffn_gate_w'].T)
    o['gate_bias']=c(i['L0_ffn_gate_bias'].reshape(1,32))
    for n,m in (('sg','gate'),('su','up'),('sd','down')): o[n]=kc(i['L0_ffn_shared_'+m])
    w1=i['L0_ffn_w1'].reshape(32,4,Pn,256).transpose(0,2,1,3); w3=i['L0_ffn_w3'].reshape(32,4,Pn,256).transpose(0,2,1,3)
    o['w13']=c(np.concatenate([w1,w3],3))
    o['w2']=c(i['L0_ffn_w2'].reshape(32,2,Pn,512).transpose(0,2,1,3))
    o['bo']=c(i['L0_attn_bo'].reshape(1,512))
    return o


def kernel(**inputs):
    import numpy as np
    import concourse.bacc as bacc
    from concourse.bass_utils import run_bass_kernel_spmd

    arrays = layouts({n: np.asarray(v) for n, v in inputs.items()})
    nc = bacc.Bacc("TRN2", target_bir_lowering=False, num_devices=1)
    aps = {n: nc.dram_tensor(f"in_{n}", v.shape, mybir.dt.from_np(v.dtype), kind="ExternalInput").ap()
           for n, v in arrays.items()}
    out = nc.dram_tensor("out_y", (N, D), F32, kind="ExternalOutput").ap()
    build(nc, aps, out)
    r = run_bass_kernel_spmd(nc, [{f"in_{n}": v for n, v in arrays.items()}], core_ids=[0])
    return r.results[0]["out_y"].reshape(B, L, D)
```

```python
from contextlib import ExitStack

import concourse.bass as bass
from concourse import mybir

F32 = mybir.dt.float32
F16 = mybir.dt.float16
I32 = mybir.dt.int32
ALU = mybir.AluOpType
ACT = mybir.ActivationFunctionType
AX = mybir.AxisListType

P = 128
B = 32
L = 32
D = 512
S = 257
CC = D // P
T = B * L // P
N = B * L
H = 16
HL = D // H
HG = 4
G = H // HG
E = 32
EG = 4
K = 4
F = 256
CAP = 128
ROUTE_SCALE = 2.0
EPS_LN = 1e-5
EPS_Z = 1e-6
EPS_W = 1e-20
BIG = 3.0e38
PASSES = ((0, 0), (0, 1), (1, 0))
HALF = N // 2
DX = D + 48
NUM = D + E


class Steps:

    def __init__(self, eng, sem):
        self.eng, self.sem, self.n = eng, sem, 0

    def done(self, ins):
        ins.then_inc(self.sem, 1)
        self.n = self.n + 1

    def wait(self):
        self.eng.wait_ge(self.sem, self.n)


def split_matmuls(pe, out, lhs, rhs, chunks, rhs_lo_ready=None):
    passes = [(a, b, c) for c in chunks for a, b in PASSES]
    if rhs_lo_ready is not None:
        passes = [p for p in passes if p[1] == 0] + [p for p in passes if p[1] == 1]
    for k, (a, b, c) in enumerate(passes):
        if rhs_lo_ready is not None and b == 1 and passes[k - 1][1] == 0:
            pe.wait_ge(*rhs_lo_ready)
        ins = pe.matmul(out, lhs(a, c), rhs(b, c), start=(k == 0), stop=(k == len(passes) - 1))
    return ins


class Norm:

    def __init__(self, nc, ctx, name, xres, ident, xT, banks, xn=None, keep=None):
        def sb(n, shape, dt=F32):
            return ctx.enter_context(nc.sbuf_tensor(f"{name}_{n}", shape, dt))

        def sem(n):
            return ctx.enter_context(nc.semaphore(f"{name}_{n}"))

        self.xres, self.ident, self.xT, self.banks = xres, ident, xT, banks
        self.stats = sb("stats", [P, T, 6])
        self.mv = sb("mv", [P, T, 2])
        self.std = sb("std", [P, T])
        self.rstd = sb("rstd", [P, T])
        self.keep, self.xn = keep, xn
        self.normed = sem("normed")
        self.turned = sem("turned")
        self.hi_ready = sem("hi_ready")
        self.lo_ready = sem("lo_ready")
        self.steps = sem("dve_steps")

    def buf(self, t, par):
        return self.xn[:, par, :] if self.keep is None else self.keep[:, t, :]

    def statistics(self, dve, t):
        dve.bn_stats(self.stats[:, t, :], self.xres[:, t, :]).then_inc(self.steps, 1)

    def vector(self, dve, half, work={}):
        tiles = range(half * self.HT, (half + 1) * self.HT)
        h = slice(tiles[0], tiles[-1] + 1)
        st = Steps(dve, self.steps)
        st.n = half * self.HALF_STEPS + self.HT
        st.wait()
        for t in tiles:
            st.done(dve.bn_aggr(self.mv[:, t, :], self.stats[:, t, :]))
        st.wait()
        st.done(dve.tensor_scalar(self.std[:, h], self.mv[:, h, 1], EPS_LN, None, ALU.add))
        dve.wait_ge(self.hi_ready, half * (self.HT + 1) + 1)
        st.done(dve.reciprocal(self.rstd[:, h], self.std[:, h]))
        st.wait()

        def norm(t):
            if t >= 2 and self.keep is None:
                dve.wait_ge(self.turned, t - 1)
            dve.tensor_scalar(self.buf(t, t % 2), self.xres[:, t, :], self.mv[:, t, 0:1], self.rstd[:, t:t + 1],
                              ALU.subtract, ALU.mult).then_inc(self.normed, 1)

        norm(tiles[0])
        for t in tiles:
            if t != tiles[-1]:
                norm(t + 1)
            if t - 1 in work:
                work[t - 1]()
            dve.wait_ge(self.hi_ready, t + t // self.HT + 2)
            dve.tensor_tensor(self.xT[1][:, :, t * P:(t + 1) * P],
                              self.banks[t % 2][:, :].rearrange("p (c t) -> p c t", c=CC),
                              self.xT[0][:, :, t * P:(t + 1) * P], ALU.subtract).then_inc(self.lo_ready, 1)

    HT = T // 2
    HALF_STEPS = 2 * HT + 2

    def root(self, act, half):
        h = slice(half * self.HT, (half + 1) * self.HT)
        act.wait_ge(self.steps, half * self.HALF_STEPS + 2 * self.HT + 1)
        act.activation(self.std[:, h], self.std[:, h], ACT.Sqrt).then_inc(self.hi_ready, 1)

    def high(self, act, t, par):
        act.wait_ge(self.turned, t + 1)
        act.activation(self.xT[0][:, :, bass.ds(t * P, P)],
                       self.banks[par][:, :].rearrange("p (c t) -> p c t", c=CC), ACT.Copy).then_inc(self.hi_ready, 1)

    def turn(self, pe, t):
        pe.wait_ge(self.normed, t + 1)
        if t >= 2:
            pe.wait_ge(self.lo_ready, t - 1)
        for c in range(CC):
            ins = pe.transpose(self.banks[t % 2][:, c * P:(c + 1) * P],
                               self.buf(t, t % 2)[:, c * P:(c + 1) * P], self.ident)
        ins.then_inc(self.turned, 1)


class Dequant:

    def __init__(self, nc, ctx, name, raw, scale, hi, lo, loads):
        self.raw, self.scale, self.hi, self.lo = raw, scale, hi, lo
        self.loaded = [ctx.enter_context(nc.semaphore(f"{name}_loaded{i}")) for i in range(loads)]
        self.multiplied = ctx.enter_context(nc.semaphore(f"{name}_multiplied"))
        self.hi_ready = ctx.enter_context(nc.semaphore(f"{name}_hi_ready"))
        self.lo_ready = ctx.enter_context(nc.semaphore(f"{name}_lo_ready"))

    PER_LOAD = 5 * 16

    def load(self, sp, n_par, codes, scales):
        s = self.loaded[n_par]
        sp.dma_start(self.raw[n_par], codes).then_inc(s, 16)
        for q in range(4):
            dst = self.scale[n_par][32 * q:32 * q + 32, :]
            sp.dma_start(dst, scales[q:q + 1, :].to_broadcast([32, dst.shape[1]])).then_inc(s, 16)

    def multiply(self, pool, n, par, load):
        pool.wait_ge(self.loaded[par], load * self.PER_LOAD)
        pool.tensor_tensor(self.raw[par], self.raw[par], self.scale[par], ALU.mult).then_inc(self.multiplied, 1)

    def low(self, pool, n, par, used=None):
        pool.wait_ge(self.multiplied, n + 1)
        pool.wait_ge(self.hi_ready, n + 1)
        if used is not None:
            pool.wait_ge(used[0], used[1])
        pool.tensor_tensor(self.lo[par], self.raw[par], self.hi[par], ALU.subtract).then_inc(self.lo_ready, 1)

    def scalar(self, act, n, par, used=None):
        act.wait_ge(self.multiplied, n + 1)
        if used is not None:
            act.wait_ge(used[0], used[1])
        act.activation(self.hi[par], self.raw[par], ACT.Copy).then_inc(self.hi_ready, 1)


C_WEIGHTS = ("gw", "sg", "su", "sd")


def split_high(act, c, n):
    act.wait_ge(c["loaded"][n], 16)
    act.activation(c["w"][n][0], c["raw"][n], ACT.Copy).then_inc(c["w_hi"], 1)


def split_low(pool, c, n):
    pool.wait_ge(c["w_hi"], C_WEIGHTS.index(n) + 1)
    pool.tensor_tensor(c["w"][n][1], c["raw"][n], c["w"][n][0], ALU.subtract).then_inc(c["w_lo"], 1)


def stage_a(nc, a, g):
    xres, xT, ident, pb, psum = g["xres"], g["xT"], g["ident"], g["pb"], g["psum"]
    CM = S - 1
    CT = CM // P
    W1 = P + 1
    SUM_SCALE = 1.0 / 16
    with ExitStack() as ctx:
        def sb(n, shape, dt=F32):
            return ctx.enter_context(nc.sbuf_tensor(n, shape, dt))

        def sem(n):
            return ctx.enter_context(nc.semaphore(n))

        stage, split = g["stage"], g["split"]
        names = ["Wk", "Wv", "Wq", "Wg", "Wo"]

        def slot(ap):
            return ap.rearrange("p (c n) -> p c n", c=CC)

        raw = {n: slot(stage[:, i, :]) for n, i in (("Wq", 0), ("Wg", 1), ("Wk", 2), ("Wv", 3), ("Wo", 4))}
        w = {"Wq": tuple(slot(split[:, i, :]) for i in (0, 1)), "Wg": tuple(slot(split[:, i, :]) for i in (2, 3))}
        for n in ("Wk", "Wv", "Wo"):
            w[n] = tuple(sb(f"{n}_{i}", [P, CC, D], F16)[:, :, :] for i in ("hi", "lo"))
        bg = sb("bg", [P, CC])
        qT = tuple(sb(f"qT_{s}", [P, CC, N], F16) for s in ("hi", "lo"))
        gT = sb("gT", [P, CC, N])
        fneg = sb("fneg", [P, 2, D])
        craw = sb("craw", [P, 2, CC, CM])
        chl = (sb("c_hi", [P, 2, CC, CM], F16), sb("c_lo", [P, 2, CC, CM], F16))
        lraw = sb("lraw", [P, CC, B])
        lhl = (sb("l_hi", [P, CC, 4, B], F16), sb("l_lo", [P, CC, 4, B], F16))
        klast = sb("klast", [P, D], F16)
        klsel = sb("klsel", [P, 2, D], F16)
        vlast = sb("vlast", [P, CC, W1], F16)
        pick = sb("pick", [P, B])
        ksb = sb("ksb", [P, 2, 2, CT, D], F16)
        vsb = sb("vsb", [P, 2, 2, CT, CC, W1], F16)
        quad = sb("quad", [P, P])
        bd = sb("bd", [P, 2, CC, P])
        bds = sb("bds", [P, 2, 2, CC, P], F16)
        den = sb("den", [P, CC, L])
        rden = sb("rden", [P, CC, L])
        att = sb("att", [P, CC, L])
        gated = sb("gated", [P, CC, L])

        x_loaded = [sem(f"x_loaded{i}") for i in range(2)]
        w_loaded = {n: sem(f"{n}_loaded") for n in names}
        small_loaded = sem("small_loaded")
        w_hi = sem("w_hi")
        w_lo = sem("w_lo")
        last_hi = sem("last_hi")
        last_lo = sem("last_lo")
        consts = sem("consts")
        ones_set = sem("ones_set")
        qg_proj = sem("qg_proj")
        q_neg = sem("q_neg")
        q_exp = sem("q_exp")
        q_feat = sem("q_feat")
        g_ready = sem("g_ready")
        kl_proj = sem("kl_proj")
        vl_proj = sem("vl_proj")
        kl_neg = sem("kl_neg")
        kl_exp = sem("kl_exp")
        kl_feat = sem("kl_feat")
        kl_hi = sem("kl_hi")
        kl_lo = sem("kl_lo")
        vl_hi = sem("vl_hi")
        vl_lo = sem("vl_lo")
        q_hi = sem("q_hi")
        q_lo = sem("q_lo")
        ctx_loaded = [sem(f"ctx_loaded{i}") for i in range(2)]
        ctx_hi = sem("ctx_hi")
        ctx_lo = sem("ctx_lo")
        k_proj = sem("k_proj")
        v_proj = sem("v_proj")
        k_neg = sem("k_neg")
        k_exp = sem("k_exp")
        k_feat = sem("k_feat")
        k_hi = sem("k_hi")
        k_lo = sem("k_lo")
        v_hi = sem("v_hi")
        v_lo = sem("v_lo")
        kl_sel = sem("kl_sel")
        kvs_done = sem("kvs_done")
        bd_ready = sem("bd_ready")
        bd_hi = sem("bd_hi")
        bd_lo = sem("bd_lo")
        att_done = sem("att_done")
        out_steps = sem("out_steps")
        att_z = sem("att_z")
        att_hi = sem("att_hi")
        att_lo = sem("att_lo")
        o_proj = sem("o_proj")
        o_added = sem("o_added")

        norm = Norm(nc, ctx, "n1", xres, ident, xT, [pb[6], pb[7]],
                    xn=gT[:, 0, :].rearrange("p (b n) -> p b n", b=2))
        dq_v, dq_qk, n2 = g["dq_v"], g["dq_qk"], g["n2"]
        block = ctx.enter_context(nc.Block())

        @block.sync
        def _(sp):
            sp.dma_start(craw[:, 0, :, :], a["ctx"][0]).then_inc(ctx_loaded[0], 16)
            for n in ("Wk", "Wv"):
                sp.dma_start(raw[n], a[n]).then_inc(w_loaded[n], 16)
            xt = a["x"].rearrange("(t p) d -> p t d", p=P)
            for i in range(2):
                r = slice(i * T // 2, (i + 1) * T // 2)
                sp.dma_start(xres[:, r, :], xt[:, r, :]).then_inc(x_loaded[i], 16)
            sp.dma_start(craw[:, 1, :, :], a["ctx"][1]).then_inc(ctx_loaded[1], 16)
            sp.dma_start(raw["Wq"], a["Wq"]).then_inc(w_loaded["Wq"], 16)
            sp.dma_start(raw["Wg"], a["Wg"]).then_inc(w_loaded["Wg"], 16)
            sp.dma_start(bg[:, :], a["bg"]).then_inc(small_loaded, 16)
            sp.dma_start(lraw[:, :, :], a["ctx_last"]).then_inc(small_loaded, 16)
            sp.dma_start(raw["Wo"], a["Wo"]).then_inc(w_loaded["Wo"], 16)
            with sp.Fori(1, B // 2) as i:
                for par in range(2):
                    b = sp.snap(i * 2 + par)
                    sp.wait_ge(ctx_lo, b - 1)
                    sp.dma_start(craw[:, par, :, :], a["ctx"][b]).then_inc(ctx_loaded[par], 16)
            sp.wait_ge(w_lo, 4)
            dq_v.load(sp, 0, a["v_codes"][0], a["v_scales"][0])
            for h in range(2):
                dq_qk.load(sp, h, a["qk_codes"][h], a["qk_scales"][h])

        @block.gpsimd
        def _(pool):
            pool.memset(ident[:, :], 0.0).then_inc(consts, 1)
            pool.wait_ge(consts, 1)
            pool.affine_select(out=ident[:, :], in_=ident[:, :], compare_op=ALU.not_equal, fill=1.0, base=0,
                               pattern=[[-1, P]], channel_multiplier=1).then_inc(consts, 1)
            pool.memset(quad[:, :], 0.0).then_inc(consts, 1)
            pool.wait_ge(consts, 3)
            for q in range(4):
                pool.memset(quad[32 * q:32 * q + 32, 32 * q:32 * q + 32], SUM_SCALE).then_inc(consts, 1)
            pool.wait_ge(consts, 7)
            pool.memset(vlast[:, :, P:W1], 1.0).then_inc(ones_set, 1)
            for part in range(2):
                for par in range(2):
                    pool.memset(vsb[:, par, part, :, :, P:W1], 1.0 - part).then_inc(ones_set, 1)
            pool.memset(pick[:, :], 0.0).then_inc(ones_set, 1)
            pool.wait_ge(ones_set, 6)
            pool.memset(vlast[32:64, :, P:W1], 0.0).then_inc(ones_set, 1)
            for q in range(3):
                r = slice(32 * q, 32 * q + 32)
                pool.tensor_copy(pick[r, :], ident[r, r]).then_inc(ones_set, 1)
            pool.wait_ge(ones_set, 10)

            def low(b, par, reuse):
                pool.wait_ge(ctx_hi, b + 1)
                if reuse:
                    pool.wait_ge(v_proj, CT * (b - 1))
                pool.tensor_tensor(chl[1][:, par, :, :], craw[:, par, :, :], chl[0][:, par, :, :],
                                   ALU.subtract).then_inc(ctx_lo, 1)

            def k_low(b, par, t, reuse):
                pool.wait_ge(k_hi, b * CT + (t + 1))
                pool.tensor_tensor(ksb[:, par, 1, t, :], fneg[:, t, :], ksb[:, par, 0, t, :],
                                   ALU.subtract).then_inc(k_lo, 1)

            low(0, 0, False)
            low(1, 1, False)
            for b in range(2):
                for t in range(CT):
                    k_low(b, b, t, False)
            low(2, 0, True)
            with pool.Fori(1, B // 2 - 1) as i:
                for par in range(2):
                    b = pool.snap(i * 2 + par)
                    k_low(b, par, 0, True)
                    low(b + 1, 1 - par, True)
                    k_low(b, par, 1, True)
            dq_v.multiply(pool, 0, 0, 1)
            k_low(B - 2, 0, 0, True)
            low(B - 1, 1, True)
            dq_qk.multiply(pool, 0, 0, 1)
            k_low(B - 2, 0, 1, True)
            dq_qk.multiply(pool, 1, 1, 1)
            k_low(B - 1, 1, 0, True)
            k_low(B - 1, 1, 1, True)
            dq_v.low(pool, 0, 0)
            for h in range(2):
                dq_qk.low(pool, h, h)

        @block.scalar
        def _(act):
            def w_high(n):
                act.wait_ge(w_loaded[n], 16)
                act.activation(w[n][0], raw[n], ACT.Copy).then_inc(w_hi, 1)

            def high(b, par, loads, reuse):
                act.wait_ge(ctx_loaded[par], loads)
                if reuse:
                    act.wait_ge(v_proj, CT * (b - 1))
                act.activation(chl[0][:, par, :, :], craw[:, par, :, :], ACT.Copy).then_inc(ctx_hi, 1)

            def tiles(b, par, t, first):
                n = b * CT + t
                act.wait_ge(k_proj, n + 1)
                if not (first and par == 0):
                    act.wait_ge(k_lo, n - 1)
                act.activation(fneg[:, t, :], pb[t][:, :], ACT.Relu, scale=-1.0).then_inc(k_neg, 1)
                act.wait_ge(k_neg, n + 1)
                act.activation(fneg[:, t, :], fneg[:, t, :], ACT.Exp, scale=-1.0).then_inc(k_exp, 1)
                act.wait_ge(v_proj, n + 1)
                if not first:
                    act.wait_ge(kvs_done, b - 1)
                act.activation(vsb[:, par, 0, t, :, 0:P], pb[2 + t][:, :].rearrange("p (c n) -> p c n", c=CC),
                               ACT.Copy).then_inc(v_hi, 1)

            def k_high(b, par, t):
                act.wait_ge(k_feat, b * CT + (t + 1))
                act.activation(ksb[:, par, 0, t, :], fneg[:, t, :], ACT.Copy).then_inc(k_hi, 1)

            high(0, 0, 16, False)
            w_high("Wk")
            w_high("Wv")
            norm.root(act, 0)
            act.wait_ge(ones_set, 10)
            high(1, 1, 16, False)
            tiles(0, 0, 0, True)
            norm.high(act, 0, 0)
            norm.high(act, 1, 1)
            tiles(0, 0, 1, True)
            k_high(0, 0, 0)
            norm.high(act, 2, 0)
            k_high(0, 0, 1)
            w_high("Wq")
            norm.high(act, 3, 1)
            tiles(1, 1, 0, True)
            norm.root(act, 1)
            norm.high(act, 4, 0)
            k_high(1, 1, 0)
            norm.high(act, 5, 1)
            tiles(1, 1, 1, True)
            norm.high(act, 6, 0)
            k_high(1, 1, 1)
            norm.high(act, 7, 1)
            w_high("Wg")
            act.wait_ge(small_loaded, 32)
            act.activation(lhl[0][:, :, :, :], lraw[:, :, :].unsqueeze(2).to_broadcast([P, CC, 4, B]),
                           ACT.Copy).then_inc(last_hi, 1)
            w_high("Wo")
            act.wait_ge(k_lo, 2 * CT)

            def q_chunk(j, reuse):
                for half in range(2):
                    n = j * 2 + half
                    act.wait_ge(qg_proj, n + 1)
                    if reuse:
                        act.wait_ge(q_lo, j * 2 + (half - 1))
                    act.activation(fneg[:, half, :], pb[half][:, :], ACT.Relu, scale=-1.0).then_inc(q_neg, 1)
                    act.wait_ge(q_neg, n + 1)
                    act.activation(fneg[:, half, :], fneg[:, half, :], ACT.Exp, scale=-1.0).then_inc(q_exp, 1)
                for half in range(2):
                    act.wait_ge(q_feat, j * 2 + (half + 1))
                    act.activation(qT[0][:, j, half * HALF:(half + 1) * HALF], fneg[:, half, :],
                                   ACT.Copy).then_inc(q_hi, 1)

            q_chunk(0, False)
            with act.Fori(1, CC) as j:
                q_chunk(j, True)
            act.wait_ge(kl_proj, 1)
            act.wait_ge(q_lo, 2 * CC)
            act.activation(fneg[:, 0, :], pb[4][:, :], ACT.Relu, scale=-1.0).then_inc(kl_neg, 1)
            act.wait_ge(kl_neg, 1)
            act.activation(fneg[:, 0, :], fneg[:, 0, :], ACT.Exp, scale=-1.0).then_inc(kl_exp, 1)
            act.wait_ge(vl_proj, 1)
            act.activation(vlast[:, :, 0:P], pb[5][:, :].rearrange("p (c n) -> p c n", c=CC),
                           ACT.Copy).then_inc(vl_hi, 1)
            act.wait_ge(kl_feat, 1)
            act.activation(klast[:, :], fneg[:, 0, :], ACT.Copy).then_inc(kl_hi, 1)

            def bd_high(b, reuse):
                act.wait_ge(bd_ready, b + 1)
                if reuse:
                    act.wait_ge(att_done, b)
                act.activation(bds[:, 0, :, :, :], bd[:, :, :, :], ACT.Copy).then_inc(bd_hi, 1)

            def pair(i, last):
                for par in range(2):
                    b = act.snap(i * 2 + par)
                    tiles(b, par, 0, False)
                    k_high(b, par, 0)
                    if not last:
                        high(b + 1, 1 - par, i * 16 + 16 * (par + 1), True)
                    elif par == 0:
                        high(b + 1, 1, i * 16 + 16, True)
                    bd_high(b - 1, True)
                    tiles(b, par, 1, False)
                    k_high(b, par, 1)

            def gate(first, last):
                with act.Fori(first, last) as j:
                    for half in range(2):
                        n = act.snap(j * 2 + half)
                        act.wait_ge(qg_proj, n + 2 * CC + 1)
                        act.activation(gT[:, j, half * HALF:(half + 1) * HALF], pb[2 + half][:, :], ACT.Sigmoid,
                                       bias=bg[:, bass.ds(j, 1)]).then_inc(g_ready, 1)

            high(2, 0, 32, True)
            gate(0, 2)
            bd_high(0, False)
            gate(2, CC)
            act.wait_ge(kl_lo, 1)
            with act.Fori(1, B // 2 - 1) as i:
                pair(i, False)
            pair(B // 2 - 1, True)
            bd_high(B - 1, True)
            dq_v.scalar(act, 0, 0)
            for h in range(2):
                dq_qk.scalar(act, h, h)
            n2.root(act, 0)
            for t in range(n2.HT):
                n2.high(act, t, t % 2)

        @block.vector
        def _(dve):
            def w_low(k):
                n = names[k]
                dve.wait_ge(w_hi, k + 1)
                dve.tensor_tensor(w[n][1], raw[n], w[n][0], ALU.subtract).then_inc(w_lo, 1)

            def feature(b, par, t):
                dve.wait_ge(k_exp, b * CT + (t + 1))
                dve.scalar_tensor_tensor(out=fneg[:, t, :], in0=pb[t][:, :], scalar=1.0,
                                         in1=fneg[:, t, :], op0=ALU.add, op1=ALU.max).then_inc(k_feat, 1)

            def v_low(b, par, t):
                dve.wait_ge(v_hi, b * CT + (t + 1))
                dve.tensor_tensor(vsb[:, par, 1, t, :, 0:P], pb[2 + t][:, :].rearrange("p (c n) -> p c n", c=CC),
                                  vsb[:, par, 0, t, :, 0:P], ALU.subtract).then_inc(v_lo, 1)

            w_low(0)
            w_low(1)
            dve.wait_ge(ones_set, 10)

            def kv_part(b, t):
                feature(b, b, t)
                v_low(b, b, t)

            work = {0: lambda: kv_part(0, 0), 1: lambda: kv_part(0, 1), 3: lambda: kv_part(1, 0),
                    4: lambda: w_low(2), 5: lambda: kv_part(1, 1)}
            for half in range(2):
                dve.wait_ge(x_loaded[half], 16)
                for t in range(half * norm.HT, (half + 1) * norm.HT):
                    norm.statistics(dve, t)
                norm.vector(dve, half, work)
            w_low(3)
            dve.wait_ge(last_hi, 1)
            dve.tensor_tensor(lhl[1][:, :, :, :], lraw[:, :, :].unsqueeze(2).to_broadcast([P, CC, 4, B]),
                              lhl[0][:, :, :, :], ALU.subtract).then_inc(last_lo, 1)
            w_low(4)

            with dve.Fori(0, CC) as j:
                for half in range(2):
                    dve.wait_ge(q_exp, j * 2 + (half + 1))
                    dve.scalar_tensor_tensor(out=fneg[:, half, :], in0=pb[half][:, :], scalar=1.0,
                                             in1=fneg[:, half, :], op0=ALU.add, op1=ALU.max).then_inc(q_feat, 1)
                for half in range(2):
                    dve.wait_ge(q_hi, j * 2 + (half + 1))
                    dve.tensor_tensor(qT[1][:, j, half * HALF:(half + 1) * HALF], fneg[:, half, :],
                                      qT[0][:, j, half * HALF:(half + 1) * HALF], ALU.subtract).then_inc(q_lo, 1)
            dve.wait_ge(kl_exp, 1)
            dve.scalar_tensor_tensor(out=fneg[:, 0, :], in0=pb[4][:, :], scalar=1.0, in1=fneg[:, 0, :],
                                     op0=ALU.add, op1=ALU.max).then_inc(kl_feat, 1)
            dve.wait_ge(vl_hi, 1)
            dve.tensor_tensor(vlast[32:64, :, 0:P], pb[5][32:64, :].rearrange("p (c n) -> p c n", c=CC),
                              vlast[32:64, :, 0:P], ALU.subtract).then_inc(vl_lo, 1)
            dve.wait_ge(kl_hi, 1)
            dve.tensor_tensor(klast[64:96, :], fneg[64:96, 0, :], klast[64:96, :], ALU.subtract).then_inc(kl_lo, 1)
            dve.wait_ge(consts, 7)
            dve.wait_ge(kl_lo, 1)

            def select(b, par, reuse):
                if reuse:
                    dve.wait_ge(kvs_done, b - 1)
                dve.tensor_scalar(klsel[:, par, :], klast[:, :], pick[:, bass.ds(b, 1)], None,
                                  ALU.mult).then_inc(kl_sel, 1)

            def diagonal(b, reuse):
                dve.wait_ge(kvs_done, b + 1)
                if reuse:
                    dve.wait_ge(bd_lo, b)
                kv = psum[:, 4:6, 0:2 * W1].rearrange("p u (c n) -> p u c n", c=2)
                m = quad[:, :].unsqueeze(1).unsqueeze(1).to_broadcast([P, 2, 2, P])
                dve.tensor_tensor(bd[:, 0, :, :].rearrange("p (u c) n -> p u c n", c=2), kv[:, :, :, 0:P], m, ALU.mult)
                dve.tensor_tensor(bd[:, 1, :, :].rearrange("p (u c) n -> p u c n", c=2),
                                  kv[:, :, :, P:W1].to_broadcast([P, 2, 2, P]), m, ALU.mult).then_inc(bd_ready, 1)

            def diagonal_low(b):
                dve.wait_ge(bd_hi, b + 1)
                dve.tensor_tensor(bds[:, 1, :, :, :], bd[:, :, :, :], bds[:, 0, :, :, :],
                                  ALU.subtract).then_inc(bd_lo, 1)

            def output(b):
                num = pb[6][:, 0:P].rearrange("p (c l) -> p c l", c=CC)
                dn = pb[6][:, P:2 * P].rearrange("p (c l) -> p c l", c=CC)
                dve.wait_ge(att_done, b + 1)
                dve.tensor_scalar(den[:, :, :], dn, EPS_Z * SUM_SCALE, None, ALU.add).then_inc(out_steps, 1)
                dve.wait_ge(out_steps, b * 3 + 1)
                dve.reciprocal(rden[:, :, :], den[:, :, :]).then_inc(out_steps, 1)
                dve.wait_ge(out_steps, b * 3 + 2)
                dve.tensor_tensor(att[:, :, :], num, rden[:, :, :], ALU.mult).then_inc(att_z, 1)
                dve.wait_ge(att_z, b + 1)
                dve.tensor_tensor(gated[:, :, :], att[:, :, :], gT[:, :, bass.ds(b * L, L)],
                                  ALU.mult).then_inc(out_steps, 1)
                dve.wait_ge(out_steps, b * 3 + 3)
                dve.tensor_copy(xT[0][:, :, bass.ds(b * L, L)], gated[:, :, :]).then_inc(att_hi, 1)
                dve.wait_ge(att_hi, b + 1)
                dve.tensor_tensor(xT[1][:, :, bass.ds(b * L, L)], gated[:, :, :], xT[0][:, :, bass.ds(b * L, L)],
                                  ALU.subtract).then_inc(att_lo, 1)

            select(0, 0, False)
            select(1, 1, False)
            diagonal(0, False)
            diagonal_low(0)
            dve.wait_ge(g_ready, 2 * CC)
            output(0)
            with dve.Fori(1, B // 2) as i:
                for par in range(2):
                    b = dve.snap(i * 2 + par)
                    feature(b, par, 0)
                    v_low(b, par, 0)
                    diagonal(b - 1, True)
                    select(b, par, True)
                    diagonal_low(b - 1)
                    feature(b, par, 1)
                    v_low(b, par, 1)
                    output(b - 1)

            def add(t):
                dve.wait_ge(o_proj, t + 1)
                dve.tensor_tensor(xres[:, t, :], xres[:, t, :], pb[t % 4][:, :], ALU.add).then_inc(o_added, 1)
                dve.wait_ge(o_added, t + 1)
                n2.statistics(dve, t)

            diagonal(B - 1, True)
            diagonal_low(B - 1)
            add(0)
            output(B - 1)
            for t in range(1, n2.HT):
                add(t)
            n2.vector(dve, 0, {0: lambda: add(4), 1: lambda: add(5), 2: lambda: add(6)})
            add(T - 1)

        @block.tensor
        def _(pe):
            def kv(out, stat, name, lo_ready=None):
                return split_matmuls(pe, out, stat, lambda s, c: w[name][s][:, c, :], range(CC), lo_ready)

            def project(b, par, t, reuse):
                n = b * CT + t
                if t == 0:
                    pe.wait_ge(ctx_lo, b + 1)
                stat = lambda s, c: chl[s][:, par, c, t * P:(t + 1) * P]
                if reuse:
                    pe.wait_ge(k_feat, n - 1)
                    kv(pb[t][:, :], stat, "Wk").then_inc(k_proj, 1)
                    pe.wait_ge(v_lo, n - 1)
                    kv(pb[2 + t][:, :], stat, "Wv").then_inc(v_proj, 1)
                else:
                    pe.wait_ge(w_hi, 1)
                    kv(pb[t][:, :], stat, "Wk", (w_lo, 1)).then_inc(k_proj, 1)
                    pe.wait_ge(w_hi, 2)
                    kv(pb[2 + t][:, :], stat, "Wv", (w_lo, 2)).then_inc(v_proj, 1)

            project(0, 0, 0, False)
            pe.wait_ge(consts, 2)
            norm.turn(pe, 0)
            norm.turn(pe, 1)
            project(0, 0, 1, False)
            norm.turn(pe, 2)
            norm.turn(pe, 3)
            project(1, 1, 0, True)
            norm.turn(pe, 4)
            norm.turn(pe, 5)
            project(1, 1, 1, True)
            norm.turn(pe, 6)
            norm.turn(pe, 7)
            pe.wait_ge(norm.lo_ready, T)
            pe.wait_ge(k_feat, 2 * CT)
            pe.wait_ge(v_lo, 2 * CT)

            def chunk(m, j, reuse):
                for half in range(2):
                    if reuse:
                        pe.wait_ge(g_ready if m else q_feat, j * 2 + (half - 1))
                    split_matmuls(pe, pb[2 * m + half][:, :],
                                  lambda s, c: w[("Wq", "Wg")[m]][s][:, c, bass.ds(j * P, P)],
                                  lambda s, c: xT[s][:, c, half * HALF:(half + 1) * HALF],
                                  range(CC)).then_inc(qg_proj, 1)

            def summary(b, par, reuse):
                pe.wait_ge(k_lo, CT * b + CT)
                pe.wait_ge(v_lo, CT * b + CT)
                pe.wait_ge(kl_sel, b + 1)
                if reuse:
                    pe.wait_ge(bd_ready, b)
                for c in range(CC):
                    out = pb[4 + c // 2][:, (c % 2) * W1:(c % 2 + 1) * W1]
                    f = slice(c * P, (c + 1) * P)
                    for t in range(CT):
                        for n, (u, v) in enumerate(PASSES):
                            pe.matmul(out, ksb[:, par, u, t, f], vsb[:, par, v, t, c, :],
                                      start=(t == 0 and n == 0), stop=False)
                    ins = pe.matmul(out, klsel[:, par, f], vlast[:, c, :], start=False, stop=True)
                ins.then_inc(kvs_done, 1)

            def attend(b, reuse):
                pe.wait_ge(bd_lo, b + 1)
                if reuse:
                    pe.wait_ge(att_z, b)
                for c in range(CC):
                    for kind in range(2):
                        out = pb[6][:, kind * P + c * L:kind * P + (c + 1) * L]
                        for n, (u, v) in enumerate(PASSES):
                            ins = pe.matmul(out, bds[:, u, kind, c, :], qT[v][:, c, bass.ds(b * L, L)],
                                            start=(n == 0), stop=(n == 2))
                ins.then_inc(att_done, 1)

            pe.wait_ge(w_lo, 3)
            chunk(0, 0, False)
            with pe.Fori(1, CC) as j:
                chunk(0, j, True)
            pe.wait_ge(last_lo, 1)
            kv(pb[4][:, :], lambda s, c: lhl[s][:, c, :, :], "Wk").then_inc(kl_proj, 1)
            kv(pb[5][:, :], lambda s, c: lhl[s][:, c, :, :], "Wv").then_inc(vl_proj, 1)
            pe.wait_ge(w_lo, 4)
            chunk(1, 0, False)
            chunk(1, 1, True)
            pe.wait_ge(vl_lo, 1)
            pe.wait_ge(q_feat, 2 * CC)
            summary(0, 0, False)
            with pe.Fori(2, CC) as j:
                chunk(1, j, True)
            pe.wait_ge(q_lo, 2 * CC)
            attend(0, False)
            pe.wait_ge(g_ready, 2 * CC)
            with pe.Fori(1, B // 2) as i:
                for par in range(2):
                    b = pe.snap(i * 2 + par)
                    project(b, par, 0, True)
                    summary(b - 1, 1 - par, True)
                    project(b, par, 1, True)
                    attend(b - 1, True)
            summary(B - 1, 1, True)
            pe.wait_ge(w_lo, 5)

            def out_proj(t):
                pe.wait_ge(att_lo, (t + 1) * (P // L))
                if t >= 4:
                    pe.wait_ge(o_added, t - 3)
                split_matmuls(pe, pb[t % 4][:, :], lambda s, c: xT[s][:, c, t * P:(t + 1) * P],
                              lambda s, c: w["Wo"][s][:, c, :], range(CC)).then_inc(o_proj, 1)

            out_proj(0)
            out_proj(1)
            attend(B - 1, True)
            for t in range(2, 4):
                out_proj(t)
            out_proj(4)
            n2.turn(pe, 0)
            n2.turn(pe, 1)
            out_proj(5)
            n2.turn(pe, 2)
            out_proj(6)
            n2.turn(pe, 3)
            out_proj(7)


def stage_b(nc, a, g):
    xres, xT, ident, pb, psum = g["xres"], g["xT"], g["ident"], g["pb"], g["psum"]
    SCALE = float(P) ** -0.5
    GT = HG * P
    with ExitStack() as ctx:
        def sb(n, shape, dt=F32):
            return ctx.enter_context(nc.sbuf_tensor(n, shape, dt))

        def sem(n):
            return ctx.enter_context(nc.semaphore(n))

        bq, bk, bv = (sb(n + "_sb", [P, H]) for n in ("bq", "bk", "bv"))
        bo = sb("bo_sb", [P, D])
        zero = sb("zero", [P, DX])
        stage, split = g["stage"], g["split"]
        v_w = tuple(split[:, s, :].rearrange("p (c n) -> p c n", c=CC) for s in (0, 1))
        qk_w = tuple(split[:, s, :].rearrange("p (b m c n) -> p b m c n", b=2, m=2, c=CC) for s in (2, 3))
        o_half = tuple(sb(f"o_w_{s}", [P, HG * D], F16) for s in ("hi", "lo"))
        o_w = tuple(t[:, :].rearrange("p (h n) -> p h n", h=HG) for t in o_half)
        o_sc = sb("o_sc", [P, HG * D])
        qT_h, kT_h = sb("qT_h", [P, 2, N], F16), sb("kT_h", [P, 2, N], F16)
        qT, kT = ([t[:, s, :] for s in range(2)] for t in (qT_h, kT_h))
        vsb = tuple(sb(f"v_g_{s}", [P, T, GT], F16) for s in ("hi", "lo"))
        bk_head = sb("bk_head", [P, 1])
        sc = sb("scores", [P, T, L])
        smax, ssum, srec = sb("smax", [P, T]), sb("ssum", [P, T]), sb("srec", [P, T])
        p16 = sb("p16", [P, 2, T, L], F16)
        pT = sb("pT", [P, 2, T, P], F16)
        oT = tuple(sb(f"oT_{s}", [P, HG, N], F16) for s in ("hi", "lo"))

        bias_loaded = sem("bias_loaded")
        bo_added = sem("bo_added")
        zeroed = sem("zeroed")
        xbuf_zeroed = sem("xbuf_zeroed")
        v_proj = sem("b_v_proj")
        v_hi = sem("b_v_hi")
        v_lo = sem("b_v_lo")
        q_proj = sem("b_q_proj")
        q_hi = sem("b_q_hi")
        q_lo = sem("b_q_lo")
        k_proj = sem("b_k_proj")
        k_hi = sem("b_k_hi")
        k_lo = sem("b_k_lo")
        s_done = sem("s_done")
        s_evac = sem("s_evac")
        s_steps = sem("s_steps")
        s_shift = sem("s_shift")
        s_exp = sem("s_exp")
        p_hi = sem("p_hi")
        p_lo = sem("p_lo")
        pt_ready = sem("pt_ready")
        pv_done = sem("pv_done")
        bk_set = sem("bk_set")
        o_hi = sem("o_hi")
        o_lo = sem("o_lo")
        o_proj = sem("b_o_proj")
        o_added = sem("b_o_added")

        norm = g["n2"]
        dq_v, dq_qk, n3, c = g["dq_v"], g["dq_qk"], g["n3"], g["c"]
        dq_o = Dequant(nc, ctx, "o", [stage[:, 4, :]], [o_sc[:, :]], [o_half[0][:, :]], [o_half[1][:, :]], 1)
        S2 = psum[:, 4:6, :].rearrange("p b (t k) -> p (b t) k", k=P)

        def v_bank(t):
            return 4 + t % 2 if t < T - 2 else 6 + t % 2

        def o_bank(t, last):
            return t if last and t < 6 else t % 4

        O2 = psum[:, 6:8, :].rearrange("p b n -> p (b n)")
        block = ctx.enter_context(nc.Block())

        @block.sync
        def _(sp):
            for dst, n in ((bq, "bq"), (bk, "bk"), (bv, "bv")):
                sp.dma_start(dst[:, :], a[n]).then_inc(bias_loaded, 16)
            sp.dma_start(bo[:, :], a["bo"].to_broadcast([P, D])).then_inc(bias_loaded, 16)

            sp.wait_ge(norm.turned, T)
            dq_o.load(sp, 0, a["o_codes"][0], a["o_scales"][0])
            sp.wait_ge(zeroed, 2)
            RT = E // (2 * HG)

            def group(gr, first, last):
                for j in range(HG):
                    if last and j >= HG - 2:
                        break
                    h = gr * HG + j
                    sp.wait_ge(dq_qk.lo_ready, h + 1)
                    dq_qk.load(sp, j % 2, a["qk_codes"][h + 2], a["qk_scales"][h + 2])
                    if first:
                        sp.dma_start(g["w13"][:, j, :, :], a["w13"][j]).then_inc(g["ew_loaded"][j], 16)
                        sp.dma_start(g["w2"][:, j, :, :], a["w2"][j]).then_inc(g["ew_loaded"][j], 16)
                    elif not last:
                        slots = bass.ds((gr * HG + (j - HG)) * (RT * P), RT * P)
                        sp.dma_start(g["xbuf"][slots, :].rearrange("(r p) d -> p r d", p=P),
                                     zero[:, :].unsqueeze(1).to_broadcast([P, RT, DX])).then_inc(xbuf_zeroed, 16)
                    if j == 0 and not last:
                        sp.wait_ge(dq_v.lo_ready, gr + 1)
                        dq_v.load(sp, 0, a["v_codes"][gr + 1], a["v_scales"][gr + 1])
                if not last:
                    sp.wait_ge(dq_o.lo_ready, gr + 1)
                    dq_o.load(sp, 0, a["o_codes"][gr + 1], a["o_scales"][gr + 1])

            group(0, True, False)
            with sp.Fori(1, G - 1) as gr:
                group(gr, False, False)
            sp.dma_start(c["raw"]["gw"], a["gate_w"]).then_inc(c["loaded"]["gw"], 16)
            sp.wait_ge(dq_v.lo_ready, G)
            for n in ("sg", "su"):
                sp.dma_start(c["raw"][n], a[n]).then_inc(c["loaded"][n], 16)
            group(G - 1, False, True)
            sp.wait_ge(dq_o.lo_ready, G)
            sp.dma_start(c["raw"]["sd"], a["sd"]).then_inc(c["loaded"]["sd"], 16)
            sp.wait_ge(xbuf_zeroed, 16 * (E // RT))

        @block.gpsimd
        def _(pool):
            pool.memset(pT[:, :, :, :], 0.0).then_inc(zeroed, 1)
            pool.memset(zero[:, :], 0.0).then_inc(zeroed, 1)
            pool.wait_ge(zeroed, 2)

            pool.wait_ge(norm.normed, T)
            pool.wait_ge(bias_loaded, 64)
            for t in range(T):
                pool.tensor_tensor(xres[:, t, :], xres[:, t, :], bo[:, :], ALU.add).then_inc(bo_added, 1)

            def group(gr, first, last):
                for j in range(HG):
                    h = gr * HG + j
                    if not (last and j >= HG - 2):
                        dq_qk.low(pool, h + 2, j % 2, (k_proj, h * 2 + 2))
                    if not (last and j >= HG - 3):
                        dq_qk.multiply(pool, h + 3, (j + 1) % 2, gr * 2 + ((j + 3) // 2 + 1))
                    if j == 0:
                        dq_o.multiply(pool, gr, 0, gr + 1)
                    if j == 1:
                        dq_o.low(pool, gr, 0, None if first else (o_proj, gr * T))
                    if j == 1 and not last:
                        dq_v.multiply(pool, gr + 1, 0, gr + 2)
                    if j == 2 and not last:
                        dq_v.low(pool, gr + 1, 0, (v_proj, gr * T + T))
                    if j == 2 and last:
                        split_low(pool, c, "gw")
                        split_low(pool, c, "sg")
                    if j == 3 and last:
                        split_low(pool, c, "su")

            dq_qk.multiply(pool, 2, 0, 2)
            group(0, True, False)
            with pool.Fori(1, G - 1) as gr:
                group(gr, False, False)
            group(G - 1, False, True)

        @block.scalar
        def _(act):
            def qk_high(h):
                act.wait_ge(q_proj, h + 1)
                act.activation(qT[0][:, :], psum[:, 0:2, :].rearrange("p b n -> p (b n)"), ACT.Identity,
                               bias=bq[:, bass.ds(h, 1)]).then_inc(q_hi, 1)
                act.wait_ge(bk_set, h + 1)
                for half in range(2):
                    act.wait_ge(k_proj, h * 2 + (half + 1))
                    act.activation(kT[0][:, half * HALF:(half + 1) * HALF], pb[2 + half][:, :], ACT.Identity,
                                   bias=bk_head[:, :]).then_inc(k_hi, 1)

            def softmax(h, splits):
                act.wait_ge(s_done, h + 1)
                for q in range(4):
                    r = slice(32 * q, 32 * q + 32)
                    ins = act.activation(sc[r, :, :], S2[r, :, r], ACT.Copy)
                ins.then_inc(s_evac, 1)
                act.wait_ge(s_shift, h + 1)
                act.activation(sc[:, :, :], sc[:, :, :], ACT.Exp, scale=SCALE).then_inc(s_exp, 1)
                splits()
                act.wait_ge(s_steps, h * 4 + 4)
                act.activation(p16[:, 0, :, :], sc[:, :, :], ACT.Copy).then_inc(p_hi, 1)

            def evac_o(h, j):
                act.wait_ge(pv_done, h + 1)
                act.activation(oT[0][:, j, :], O2, ACT.Identity, bias=bv[:, bass.ds(h, 1)]).then_inc(o_hi, 1)

            norm.root(act, 1)

            def evac_v(gr, t):
                act.wait_ge(v_proj, gr * T + (t + 1))
                act.activation(vsb[0][:, t, :], pb[v_bank(t)][:, :], ACT.Copy).then_inc(v_hi, 1)

            evac_v(0, 0)
            evac_v(0, 1)
            norm.high(act, 4, 0)
            norm.high(act, 5, 1)
            evac_v(0, 2)
            norm.high(act, 6, 0)
            evac_v(0, 3)
            norm.high(act, 7, 1)
            evac_v(0, 4)
            evac_v(0, 5)
            act.wait_ge(bias_loaded, 64)
            qk_high(0)
            evac_v(0, T - 2)
            evac_v(0, T - 1)

            def group(gr, first, last):
                for j in range(HG):
                    h = gr * HG + j
                    def splits():
                        if not (last and j >= HG - 2):
                            dq_qk.scalar(act, h + 2, j % 2, (k_proj, h * 2 + 2))
                        if j == 1:
                            dq_o.scalar(act, gr, 0, None if first else (o_proj, gr * T))
                        if j == 2 and not last:
                            dq_v.scalar(act, gr + 1, 0, (v_proj, gr * T + T))
                        if j == 2 and last:
                            act.wait_ge(v_proj, G * T)
                            split_high(act, c, "gw")
                            split_high(act, c, "sg")
                        if j == 3 and last:
                            act.wait_ge(k_proj, 2 * H)
                            split_high(act, c, "su")

                    softmax(h, splits)
                    if j < HG - 1:
                        qk_high(h + 1)
                    evac_o(h, j)
                if not last:
                    for t in range(T - 2):
                        evac_v(gr + 1, t)
                    qk_high(gr * HG + HG)
                    evac_v(gr + 1, T - 2)
                    evac_v(gr + 1, T - 1)

            group(0, True, False)
            with act.Fori(1, G - 1) as gr:
                group(gr, False, False)
            group(G - 1, False, True)
            n3.root(act, 0)
            for t in range(n3.HT):
                n3.high(act, t, t % 2)

        @block.vector
        def _(dve):
            st = Steps(dve, s_steps)

            def set_bk(h, reuse):
                if reuse:
                    dve.wait_ge(k_hi, h * 2)
                dve.tensor_copy(bk_head[:, :], bk[:, bass.ds(h, 1)]).then_inc(bk_set, 1)

            def qk_low(h):
                for half in range(2):
                    r = slice(half * HALF, (half + 1) * HALF)
                    if half == 0:
                        dve.wait_ge(q_hi, h + 1)
                    dve.scalar_tensor_tensor(out=qT[1][:, r], in0=pb[half][:, :], scalar=bq[:, bass.ds(h, 1)],
                                             in1=qT[0][:, r], op0=ALU.add, op1=ALU.subtract).then_inc(q_lo, 1)
                for half in range(2):
                    r = slice(half * HALF, (half + 1) * HALF)
                    dve.wait_ge(k_hi, h * 2 + (half + 1))
                    dve.scalar_tensor_tensor(out=kT[1][:, r], in0=pb[2 + half][:, :], scalar=bk_head[:, :],
                                             in1=kT[0][:, r], op0=ALU.add, op1=ALU.subtract).then_inc(k_lo, 1)

            def v_low(gr, t):
                dve.wait_ge(v_hi, gr * T + (t + 1))
                dve.tensor_tensor(vsb[1][:, t, :], pb[v_bank(t)][:, :], vsb[0][:, t, :],
                                  ALU.subtract).then_inc(v_lo, 1)

            def v_first():
                v_low(0, 0)
                v_low(0, 1)

            norm.vector(dve, 1, {3: v_first, 5: lambda: v_low(0, 2), 6: lambda: v_low(0, 3)})
            v_low(0, 4)
            v_low(0, 5)
            dve.wait_ge(bias_loaded, 64)
            set_bk(0, False)
            qk_low(0)
            v_low(0, T - 2)
            v_low(0, T - 1)
            dve.wait_ge(zeroed, 1)
            dve.wait_ge(bo_added, T)

            def softmax(h):
                st.n = h * 4
                dve.wait_ge(s_evac, h + 1)
                st.done(dve.tensor_reduce(smax[:, :], sc[:, :, :], AX.X, ALU.max))
                st.wait()
                dve.tensor_tensor(sc[:, :, :], sc[:, :, :], smax[:, :].unsqueeze(2).to_broadcast([P, T, L]),
                                  ALU.subtract).then_inc(s_shift, 1)
                dve.wait_ge(s_exp, h + 1)
                st.done(dve.tensor_reduce(ssum[:, :], sc[:, :, :], AX.X, ALU.add))
                st.wait()
                st.done(dve.reciprocal(srec[:, :], ssum[:, :]))
                st.wait()
                st.done(dve.tensor_tensor(sc[:, :, :], sc[:, :, :],
                                          srec[:, :].unsqueeze(2).to_broadcast([P, T, L]), ALU.mult))
                st.wait()
                dve.wait_ge(p_hi, h + 1)
                dve.tensor_tensor(p16[:, 1, :, :], sc[:, :, :], p16[:, 0, :, :], ALU.subtract).then_inc(p_lo, 1)
                dve.wait_ge(p_lo, h + 1)
                for q in range(4):
                    r = slice(32 * q, 32 * q + 32)
                    for part in range(2):
                        ins = dve.transpose(pT[r, part, :, r], p16[r, part, :, :])
                ins.then_inc(pt_ready, 1)

            def evac_o(h, j):
                dve.wait_ge(o_hi, h + 1)
                dve.scalar_tensor_tensor(out=oT[1][:, j, :], in0=O2, scalar=bv[:, bass.ds(h, 1)],
                                         in1=oT[0][:, j, :], op0=ALU.add, op1=ALU.subtract).then_inc(o_lo, 1)

            def group(gr, last):
                for j in range(HG):
                    h = gr * HG + j if last else dve.snap(gr * HG + j)
                    softmax(h)
                    if not (last and j == HG - 1):
                        set_bk(h + 1, True)
                    if j < HG - 1:
                        qk_low(h + 1)
                    evac_o(h, j)
                if not last:
                    for t in range(T - 2):
                        v_low(gr + 1, t)
                for t in range(n3.HT if last else T):
                    add(gr, t, last)
                if not last:
                    qk_low(gr * HG + HG)
                    v_low(gr + 1, T - 2)
                    v_low(gr + 1, T - 1)

            def add(gr, t, last):
                dve.wait_ge(o_proj, gr * T + (t + 1))
                dve.tensor_tensor(xres[:, t, :], xres[:, t, :], pb[o_bank(t, last)][:, :],
                                  ALU.add).then_inc(o_added, 1)
                if last:
                    dve.wait_ge(o_added, gr * T + (t + 1))
                    n3.statistics(dve, t)

            with dve.Fori(0, G - 1) as gr:
                group(gr, False)
            group(G - 1, True)
            dve.wait_ge(c["w_lo"], 3)
            n3.vector(dve, 0, {t: (lambda t=t: add(G - 1, t + 4, True)) for t in range(3)})
            add(G - 1, T - 1, True)

        @block.tensor
        def _(pe):
            def v_tile(gr, t):
                if t == 0:
                    pe.wait_ge(dq_v.lo_ready, gr + 1)
                if 2 <= t < T - 2:
                    pe.wait_ge(v_lo, gr * T + (t - 1))
                split_matmuls(pe, pb[v_bank(t)][:, :], lambda s, c: xT[s][:, c, t * P:(t + 1) * P],
                              lambda s, c: v_w[s][:, c, :], range(CC)).then_inc(v_proj, 1)

            def qk(h, par):
                pe.wait_ge(dq_qk.lo_ready, h + 1)
                for m in range(2):
                    for half in range(2):
                        ins = split_matmuls(pe, pb[2 * m + half][:, :], lambda s, c: qk_w[s][:, par, m, c, :],
                                            lambda s, c: xT[s][:, c, half * HALF:(half + 1) * HALF], range(CC))
                        if m:
                            ins.then_inc(k_proj, 1)
                    if not m:
                        ins.then_inc(q_proj, 1)

            def scores(h, first):
                pe.wait_ge(q_lo, h * 2 + 2)
                if not (first and h == 0):
                    pe.wait_ge(s_evac, h)
                for t in range(T):
                    if t % (T // 2) == 0:
                        pe.wait_ge(k_lo, h * 2 + (1 + t // (T // 2)))
                    r = slice(t * P, (t + 1) * P)
                    for n, (u, v) in enumerate(PASSES):
                        ins = pe.matmul(S2[:, t, :], qT[u][:, r], kT[v][:, r], start=(n == 0), stop=(n == 2))
                ins.then_inc(s_done, 1)

            def values(h, j, first):
                pe.wait_ge(pt_ready, h + 1)
                if not (first and h == 0):
                    pe.wait_ge(o_lo, h)
                for t in range(T):
                    for n, (u, v) in enumerate(PASSES):
                        ins = pe.matmul(O2[:, t * P:(t + 1) * P], vsb[u][:, t, j * P:(j + 1) * P], pT[:, v, t, :],
                                        start=(n == 0), stop=(n == 2))
                ins.then_inc(pv_done, 1)

            def out_part(gr, t, heads, last):
                for j in heads:
                    for s, (u, v) in enumerate(PASSES):
                        ins = pe.matmul(pb[o_bank(t, last)][:, :], oT[u][:, j, t * P:(t + 1) * P], o_w[v][:, j, :],
                                        start=(j == 0 and s == 0), stop=(j == HG - 1 and s == 2))
                return ins

            LN3_TURNS = {4: (), 5: (), 6: (0, 1), 7: (2, 3)}

            def group(gr, first, last):
                for j in range(HG):
                    h = gr * HG + j
                    if j == 0:
                        pe.wait_ge(v_lo, gr * T + T - 2)
                    scores(h, first)
                    if j < HG - 1:
                        qk(h + 1, (j + 1) % 2)
                    else:
                        pe.wait_ge(dq_o.lo_ready, gr + 1)
                        pe.wait_ge(o_lo, h - 1)
                        for t in range(4):
                            out_part(gr, t, range(HG - 2), last)
                        pe.wait_ge(o_lo, h)
                        for t in range(4):
                            out_part(gr, t, [HG - 2], last)
                    if j == 0:
                        pe.wait_ge(v_lo, gr * T + T)
                    values(h, j, first)
                if not last:
                    for t in range(T - 2):
                        v_tile(gr + 1, t)
                else:
                    for t in (4, 5):
                        out_part(gr, t, range(HG - 1), last)
                pe.wait_ge(o_lo, gr * HG + HG)
                for t in range(4):
                    out_part(gr, t, [HG - 1], last).then_inc(o_proj, 1)
                for t in range(4, T):
                    begun = last and t in (4, 5)
                    if not begun:
                        pe.wait_ge(o_added, gr * T + (t - 3))
                    out_part(gr, t, [HG - 1] if begun else range(HG), last).then_inc(o_proj, 1)
                    for u in LN3_TURNS[t] if last else ():
                        n3.turn(pe, u)
                if not last:
                    pe.wait_ge(o_added, gr * T + T)
                    qk(gr * HG + HG, 0)
                    for t in range(T - 2, T):
                        v_tile(gr + 1, t)

            v_tile(0, 0)
            v_tile(0, 1)
            norm.turn(pe, 4)
            norm.turn(pe, 5)
            v_tile(0, 2)
            norm.turn(pe, 6)
            v_tile(0, 3)
            norm.turn(pe, 7)
            pe.wait_ge(norm.lo_ready, T)
            v_tile(0, 4)
            v_tile(0, 5)
            qk(0, 0)
            for t in range(T - 2, T):
                v_tile(0, t)
            group(0, True, False)
            with pe.Fori(1, G - 1) as gr:
                group(gr, False, False)
            group(G - 1, False, True)


def stage_c(nc, a, g):
    xres, xT, ident, pb, psum = g["xres"], g["xT"], g["ident"], g["pb"], g["psum"]
    w13, w2, ew_loaded = g["w13"], g["w2"], g["ew_loaded"]
    xbuf, out = g["xbuf"], g["out"]
    FC = F // P
    PAD = 8
    LAST = E // 4 - 1
    with ExitStack() as ctx:
        def sb(n, shape, dt=F32):
            return ctx.enter_context(nc.sbuf_tensor(n, shape, dt))

        def sem(n):
            return ctx.enter_context(nc.semaphore(n))

        x3 = g["x3"]
        c3, w = g["c"], g["c"]["w"]
        w["sd"] = tuple(sb(f"sd_{s}", [P, CC, D], F16)[:, :, :] for s in ("hi", "lo"))
        gb = sb("gb", [P, E])
        tri, tri_f = sb("tri", [P, P], F16), sb("tri_f", [P, P])
        ones = sb("ones16", [P, P], F16)
        e256i, e256 = sb("e256i", [P, E], I32), sb("e256", [P, E])
        score = sb("score", [P, T, E])
        biased = sb("biased", [P, T, E])
        m8 = sb("m8", [P, T * EG, 8])
        gs = sb("gs", [P, T, EG + PAD])
        gm8 = sb("gm8", [P, T, 8])
        gsel = sb("gsel", [P, T, EG + PAD])
        gmask = sb("gmask", [P, T, EG])
        tmp = sb("tmp", [P, T, E + PAD])
        em8 = sb("em8", [P, T, 8])
        esel = sb("esel", [P, T, E + PAD])
        chosen = sb("chosen", [P, T, E])
        chosen16 = sb("chosen16", [P, T, E], F16)
        wt = sb("wt", [P, T, E])
        wsum = sb("wsum", [P, T])
        pos = sb("pos", [P, T, E])
        key = sb("key", [P, T, E])
        k8 = sb("k8", [P, T, 8])
        numi = sb("numi", [P, T], I32)
        ki, kp, ke, kd = (sb(n, [P, T, K], I32) for n in ("ki", "kp", "ke", "kd"))
        scat = sb("scat", [P, T, K], I32)
        ssil, sup, sh = sb("ssil", [P, D]), sb("sup", [P, D]), sb("sh", [P, D])
        sT = tuple(sb(f"sT_{s}", [P, CC, N], F16) for s in ("hi", "lo"))
        xe = sb("xe", [P, 2, DX])
        xeT = sb("xeT", [P, CC, P])
        y = sb("y", [P, 2, D])
        hT = sb("hT", [P, FC, P])
        hsil, hh = sb("hsil", [P, F]), sb("hh", [P, F])
        we = sb("we", [P, 4])
        ne = sb("ne", [P, 4], I32)

        gb_loaded = sem("gb_loaded")
        w_lo = c3["w_lo"]
        consts = sem("c_consts")
        logits = sem("logits")
        score_ready = sem("score_ready")
        r_steps = sem("r_steps")
        chosen_ready = sem("chosen_ready")
        pos_done = sem("pos_done")
        idx_ready = sem("idx_ready")
        scattered = sem("scattered")
        sg_proj = sem("sg_proj")
        su_proj = sem("su_proj")
        s_silu = sem("s_silu")
        s_up = sem("s_up")
        s_h = sem("s_h")
        s_hi = sem("s_hi")
        s_lo = sem("s_lo")
        sd_proj = sem("sd_proj")
        s_added = sem("s_added")
        xe_loaded = [sem(f"xe_loaded{i}") for i in range(2)]
        xe_turned = sem("xe_turned")
        xeT_ready = sem("xeT_ready")
        up_done = sem("up_done")
        e_silu = sem("e_silu")
        h_ready = sem("h_ready")
        h_turned = sem("h_turned")
        hT_ready = sem("hT_ready")
        down_done = sem("down_done")
        y_ready = sem("y_ready")
        xe_used = sem("xe_used")
        y_added = sem("y_added")
        number_ready = sem("number_ready")
        out_stored = sem("out_stored")

        norm = g["n3"]
        LG = pb[6][:, 0:T * E].rearrange("p (t e) -> p t e", e=E)
        PS = pb[7][:, 0:T * E].rearrange("p (t e) -> p t e", e=E)

        def shared_half(eng, j, half, first):
            n = j * 2 + half
            if not first:
                eng.wait_ge(s_lo, n)
            eng.wait_ge(s_up, n + 1)
            eng.tensor_tensor(sh[:, :], ssil[:, :], sup[:, :], ALU.mult).then_inc(s_h, 1)
            eng.wait_ge(s_hi, n + 1)
            eng.tensor_tensor(sT[1][:, j, half * HALF:(half + 1) * HALF], sh[:, :],
                              sT[0][:, j, half * HALF:(half + 1) * HALF], ALU.subtract).then_inc(s_lo, 1)

        block = ctx.enter_context(nc.Block())

        @block.sync
        def _(sp):
            sp.dma_start(gb[:, :], a["gate_bias"].to_broadcast([P, E])).then_inc(gb_loaded, 16)
            sp.wait_ge(scattered, 16 * T * K)
            for e in range(2):
                sp.dma_start(xe[:, e, :], xbuf[e * CAP:(e + 1) * CAP, :]).then_inc(xe_loaded[e], 16)
            o = out.rearrange("(t p) d -> t p d", p=P)
            for t in range(T):
                sp.wait_ge(s_added, t + 1)
                sp.dma_start(o[t], xres[:, t, :]).then_inc(out_stored, 16)

            def loads(i, q, first, last):
                e = i * 4 + q
                if not (last and q >= 2):
                    sp.wait_ge(xe_used, e + 1)
                    sp.dma_start(xe[:, q % 2, :], xbuf[bass.ds((e + 2) * CAP, CAP), :]
                                 ).then_inc(xe_loaded[q % 2], 16)
                if (first and q == 0) or (last and q >= 1):
                    return
                sp.wait_ge(down_done, e)
                slot = (q + 3) % 4
                sp.dma_start(w13[:, slot, :, :], a["w13"][e + 3]).then_inc(ew_loaded[slot], 16)
                sp.dma_start(w2[:, slot, :, :], a["w2"][e + 3]).then_inc(ew_loaded[slot], 16)

            for q in range(4):
                loads(0, q, True, False)
            with sp.Fori(1, LAST) as i:
                for q in range(4):
                    loads(i, q, False, False)
            for q in range(4):
                loads(LAST, q, False, True)

        @block.gpsimd
        def _(pool):
            pool.memset(tri_f[:, :], 1.0).then_inc(consts, 1)
            pool.wait_ge(consts, 1)
            pool.affine_select(out=tri_f[:, :], in_=tri_f[:, :], compare_op=ALU.is_gt, fill=0.0, base=0,
                               pattern=[[1, P]], channel_multiplier=-1).then_inc(consts, 1)
            pool.wait_ge(consts, 2)
            pool.tensor_copy(tri[:, :], tri_f[:, :]).then_inc(consts, 1)
            pool.memset(ones[:, :], 1.0).then_inc(consts, 1)
            pool.iota(e256i[:, :], [[2 * CAP, E]], base=1, channel_multiplier=0).then_inc(consts, 1)
            pool.wait_ge(consts, 5)
            pool.tensor_copy(e256[:, :], e256i[:, :]).then_inc(consts, 1)
            pool.iota(numi[:, :], [[-P, T]], base=2 * N, channel_multiplier=-1).then_inc(number_ready, 1)
            pool.wait_ge(number_ready, 1)
            pool.tensor_copy(x3[:, :, NUM], numi[:, :]).then_inc(number_ready, 1)
            pool.memset(x3[:, :, NUM + 1:DX], 0.0).then_inc(number_ready, 1)
            split_low(pool, c3, "sd")

            shared_half(pool, 0, 0, True)
            shared_half(pool, 0, 1, False)
            shared_half(pool, 1, 0, False)
            pool.wait_ge(number_ready, 3)
            pool.wait_ge(idx_ready, 1)
            for t in range(T):
                for k in range(K):
                    pool.indirect_dma_start(xbuf, bass.IndirectOffsetOnAxis(ap=scat[:, t, k:k + 1], axis=0),
                                            x3[:, t, :], None, bounds_check=E * CAP - 1,
                                            oob_is_err=False).then_inc(scattered, 16)
            pool.wait_ge(out_stored, 16 * T)
            for e in range(E):
                pool.wait_ge(y_ready, e + 1)
                if e:
                    pool.wait_ge(y_added, e * 16)
                pool.indirect_dma_start(out, bass.IndirectOffsetOnAxis(ap=ne[:, e % 4:e % 4 + 1], axis=0),
                                        y[:, e % 2, :], None, bounds_check=N - 1, oob_is_err=False,
                                        compute_op=ALU.add).then_inc(y_added, 16)
            pool.wait_ge(y_added, 16 * E)

        @block.scalar
        def _(act):
            norm.root(act, 1)
            for t in range(norm.HT, T):
                norm.high(act, t, t % 2)
            act.wait_ge(logits, 1)
            act.activation(score[:, :, :], LG, ACT.Sigmoid).then_inc(score_ready, 1)
            split_high(act, c3, "sd")

            def gate_up(j, half, first):
                n = j * 2 + half
                act.wait_ge(sg_proj, n + 1)
                if not first:
                    act.wait_ge(s_h, n)
                act.activation(ssil[:, :], pb[half][:, :], ACT.Silu).then_inc(s_silu, 1)
                act.wait_ge(su_proj, n + 1)
                act.activation(sup[:, :], pb[2 + half][:, :], ACT.Copy).then_inc(s_up, 1)
                act.wait_ge(s_h, n + 1)
                act.activation(sT[0][:, j, half * HALF:(half + 1) * HALF], sh[:, :], ACT.Copy).then_inc(s_hi, 1)

            gate_up(0, 0, True)
            gate_up(0, 1, False)
            with act.Fori(1, CC) as j:
                gate_up(j, 0, False)
                gate_up(j, 1, False)

            def rows_out(e, slot, added):
                act.wait_ge(down_done, e + 1)
                if added is not None:
                    act.wait_ge(y_added, added)
                act.activation(y[:, slot % 2, :], pb[6][:, :], ACT.Copy, scale=we[:, slot:slot + 1]).then_inc(y_ready, 1)

            def expert(i, q, first):
                e = i * 4 + q
                act.wait_ge(up_done, e + 1)
                if not (first and q == 0):
                    act.wait_ge(h_ready, e)
                act.activation(hsil[:, :], pb[1][:, 0:F], ACT.Silu).then_inc(e_silu, 1)
                if not (first and q == 0):
                    rows_out(e - 1, (q + 3) % 4, None if first and q < 3 else e * 16 - 32)
                act.wait_ge(h_turned, e + 1)
                act.activation(hT[:, :, :], pb[3][:, 0:F].rearrange("p (c n) -> p c n", c=FC),
                               ACT.Copy).then_inc(hT_ready, 1)

            for q in range(4):
                expert(0, q, True)
            with act.Fori(1, E // 4) as i:
                for q in range(4):
                    expert(i, q, False)
            rows_out(E - 1, 3, 16 * (E - 2))

        @block.vector
        def _(dve):
            norm.vector(dve, 1)
            st = Steps(dve, r_steps)

            def then(ins):
                st.done(ins)
                st.wait()

            st.done(dve.memset(gs[:, :, EG:EG + PAD], -BIG))
            st.done(dve.memset(tmp[:, :, E:E + PAD], -BIG))
            dve.wait_ge(gb_loaded, 16)
            dve.wait_ge(score_ready, 1)
            then(dve.tensor_tensor(biased[:, :, :], score[:, :, :],
                                   gb[:, :].unsqueeze(1).to_broadcast([P, T, E]), ALU.add))
            per = E // EG
            for t in range(T):
                for gr in range(EG):
                    st.done(dve.max(m8[:, t * EG + gr, :], biased[:, t, gr * per:(gr + 1) * per]))
            st.wait()
            m8v = m8[:, :, :].rearrange("p (t g) k -> p t g k", g=EG)
            then(dve.tensor_tensor(gs[:, :, 0:EG], m8v[:, :, :, 0], m8v[:, :, :, 1], ALU.add))
            for t in range(T):
                st.done(dve.max(gm8[:, t, :], gs[:, t, :]))
            st.wait()
            then(dve.memset(gm8[:, :, 2:8], -BIG))
            for t in range(T):
                st.done(dve.match_replace(gsel[:, t, :], gm8[:, t, :], gs[:, t, :], BIG))
            st.wait()
            then(dve.tensor_scalar(gmask[:, :, :], gsel[:, :, 0:EG], BIG, None, ALU.is_equal))
            then(dve.tensor_tensor(tmp[:, :, 0:E].rearrange("p t (g n) -> p t g n", g=EG),
                                   biased[:, :, :].rearrange("p t (g n) -> p t g n", g=EG),
                                   gmask[:, :, :].unsqueeze(3).to_broadcast([P, T, EG, per]), ALU.mult))
            then(dve.tensor_scalar(tmp[:, :, 0:E], tmp[:, :, 0:E], 0.0, None, ALU.add))
            for t in range(T):
                st.done(dve.max(em8[:, t, :], tmp[:, t, 0:E]))
            st.wait()
            then(dve.memset(em8[:, :, K:8], -BIG))
            for t in range(T):
                st.done(dve.match_replace(esel[:, t, :], em8[:, t, :], tmp[:, t, :], BIG))
            st.wait()
            then(dve.tensor_scalar(chosen[:, :, :], esel[:, :, 0:E], BIG, None, ALU.is_equal))
            dve.tensor_copy(chosen16[:, :, :], chosen[:, :, :]).then_inc(chosen_ready, 1)
            then(dve.tensor_tensor(wt[:, :, :], score[:, :, :], chosen[:, :, :], ALU.mult))
            then(dve.tensor_reduce(wsum[:, :], wt[:, :, :], AX.X, ALU.add))
            then(dve.tensor_scalar(wsum[:, :], wsum[:, :], EPS_W, None, ALU.add))
            then(dve.reciprocal(wsum[:, :], wsum[:, :]))
            then(dve.tensor_scalar(wsum[:, :], wsum[:, :], ROUTE_SCALE, None, ALU.mult))
            then(dve.tensor_tensor(wt[:, :, :], wt[:, :, :], wsum[:, :].unsqueeze(2).to_broadcast([P, T, E]),
                                   ALU.mult))
            dve.wait_ge(pos_done, 1)
            dve.wait_ge(consts, 6)
            then(dve.tensor_scalar(pos[:, :, :], PS, float(CAP), None, ALU.min))
            st.done(dve.tensor_copy(x3[:, :, D:NUM], wt[:, :, :]))
            then(dve.tensor_tensor(pos[:, :, :], pos[:, :, :],
                                   e256[:, :].unsqueeze(1).to_broadcast([P, T, E]), ALU.add))
            then(dve.tensor_tensor(key[:, :, :], pos[:, :, :], chosen[:, :, :], ALU.mult))
            for t in range(T):
                st.done(dve.max(k8[:, t, :], key[:, t, :]))
            st.wait()
            then(dve.tensor_scalar(ki[:, :, :], k8[:, :, 0:K], -1.0, None, ALU.add))
            st.done(dve.tensor_scalar(ke[:, :, :], ki[:, :, :], 8, 7, ALU.logical_shift_right,
                                      ALU.logical_shift_left))
            then(dve.tensor_scalar(kp[:, :, :], ki[:, :, :], 255, None, ALU.bitwise_and))
            then(dve.tensor_scalar(kd[:, :, :], kp[:, :, :], 7, 13, ALU.logical_shift_right,
                                   ALU.logical_shift_left))
            then(dve.tensor_tensor(scat[:, :, :], ke[:, :, :], kp[:, :, :], ALU.add))
            dve.tensor_tensor(scat[:, :, :], scat[:, :, :], kd[:, :, :], ALU.add).then_inc(idx_ready, 1)
            shared_half(dve, 1, 1, False)
            with dve.Fori(2, CC) as j:
                shared_half(dve, j, 0, False)
                shared_half(dve, j, 1, False)
            def add(t):
                dve.wait_ge(sd_proj, t + 1)
                dve.tensor_tensor(xres[:, t, :], xres[:, t, :], pb[4 + t % 2][:, :], ALU.add).then_inc(s_added, 1)

            for t in range(T - 1):
                add(t)

            def rows(e, q, first):
                dve.wait_ge(xe_turned, e + 1)
                dve.tensor_copy(xeT[:, :, :], pb[0][:, :].rearrange("p (c n) -> p c n", c=CC)).then_inc(xeT_ready, 1)
                if not first:
                    dve.wait_ge(y_added, e * 16 - 48)
                dve.tensor_copy(we[:, q:q + 1], xe[:, q % 2, bass.ds(e + D, 1)])
                dve.tensor_scalar(ne[:, q:q + 1], xe[:, q % 2, NUM:NUM + 1], -1.0, 2.0 * N, ALU.mult,
                                  ALU.add).then_inc(xe_used, 1)

            def hidden(e):
                dve.wait_ge(e_silu, e + 1)
                dve.tensor_tensor(hh[:, :], hsil[:, :], pb[1][:, F:2 * F], ALU.mult).then_inc(h_ready, 1)

            rows(0, 0, True)
            add(T - 1)
            for e in range(3):
                rows(e + 1, e + 1, True)
                hidden(e)
            with dve.Fori(1, E // 4) as i:
                for q in range(4):
                    e = dve.snap(i * 4 + q)
                    rows(e, q, False)
                    hidden(e - 1)
            hidden(E - 1)

        @block.tensor
        def _(pe):
            def gate_up(m, j, half, reuse):
                if reuse:
                    pe.wait_ge(s_up if m else s_silu, j * 2 + (half - 1))
                split_matmuls(pe, pb[2 * m + half][:, :], lambda s, c: w[("sg", "su")[m]][s][:, c, bass.ds(j * P, P)],
                              lambda s, c: xT[s][:, c, half * HALF:(half + 1) * HALF],
                              range(CC)).then_inc(su_proj if m else sg_proj, 1)

            def shared(j):
                for half in range(2):
                    for m in range(2):
                        gate_up(m, j, half, True)

            pe.wait_ge(w_lo, 3)
            gate_up(0, 0, 0, False)
            norm.turn(pe, 4)
            norm.turn(pe, 5)
            gate_up(1, 0, 0, False)
            norm.turn(pe, 6)
            norm.turn(pe, 7)
            pe.wait_ge(norm.lo_ready, T)
            for t in range(T):
                ins = split_matmuls(pe, LG[:, t, :], lambda s, c: xT[s][:, c, t * P:(t + 1) * P],
                                    lambda s, c: w["gw"][s][:, c, :], range(CC))
            ins.then_inc(logits, 1)
            gate_up(0, 0, 1, False)
            gate_up(1, 0, 1, False)
            gate_up(0, 1, 0, True)
            gate_up(1, 1, 0, True)
            pe.wait_ge(chosen_ready, 1)
            pe.wait_ge(consts, 4)
            for t in range(T):
                for u in range(t + 1):
                    ins = pe.matmul(PS[:, t, :], (tri if u == t else ones)[:, :], chosen16[:, u, :],
                                    start=(u == 0), stop=(u == t))
            ins.then_inc(pos_done, 1)
            gate_up(0, 1, 1, True)
            gate_up(1, 1, 1, True)
            with pe.Fori(2, CC) as j:
                shared(j)
            pe.wait_ge(w_lo, 4)

            def down(t):
                pe.wait_ge(s_lo, 2 * CC - (t < T // 2))
                if t >= 2:
                    pe.wait_ge(s_added, t - 1)
                split_matmuls(pe, pb[4 + t % 2][:, :], lambda s, c: sT[s][:, c, t * P:(t + 1) * P],
                              lambda s, c: w["sd"][s][:, c, :], range(CC)).then_inc(sd_proj, 1)

            def turn_x(e, par, loads):
                pe.wait_ge(xe_loaded[par], loads)
                for c in range(CC):
                    ins = pe.transpose(pb[0][:, c * P:(c + 1) * P], xe[:, par, c * P:(c + 1) * P], ident)
                ins.then_inc(xe_turned, 1)

            def expert_down(e, slot, reuse):
                pe.wait_ge(hT_ready, e + 1)
                if reuse:
                    pe.wait_ge(y_ready, e)
                for f in range(FC):
                    ins = pe.matmul(pb[6][:, :], hT[:, f, :], w2[:, slot, f, :], start=(f == 0), stop=(f == FC - 1))
                ins.then_inc(down_done, 1)

            def expert(i, q, first, last):
                e = i * 4 + q
                pe.wait_ge(ew_loaded[q], i * 32 + 32)
                pe.wait_ge(xeT_ready, e + 1)
                for c in range(CC):
                    ins = pe.matmul(pb[1][:, :], xeT[:, c, :], w13[:, q, c, :], start=(c == 0), stop=(c == CC - 1))
                ins.then_inc(up_done, 1)
                if not (last and q == 3):
                    turn_x(e + 1, (q + 1) % 2, i * 32 + 16 * ((q + 1) // 2 + 1))
                if not (first and q == 0):
                    expert_down(e - 1, (q + 3) % 4, not (first and q == 1))
                pe.wait_ge(h_ready, e + 1)
                for f in range(FC):
                    ins = pe.transpose(pb[3][:, f * P:(f + 1) * P], hh[:, f * P:(f + 1) * P], ident)
                ins.then_inc(h_turned, 1)

            for t in range(T - 1):
                down(t)
            turn_x(0, 0, 16)
            down(T - 1)
            for q in range(4):
                expert(0, q, True, False)
            with pe.Fori(1, LAST) as i:
                for q in range(4):
                    expert(i, q, False, False)
            for q in range(4):
                expert(LAST, q, False, True)
            expert_down(E - 1, 3, True)


def build(nc, a, out):
    with ExitStack() as ctx:
        g = {
            "xres": ctx.enter_context(nc.sbuf_tensor("xres", [P, T, D], F32)),
            "xT": tuple(ctx.enter_context(nc.sbuf_tensor(f"xT_{s}", [P, CC, N], F16)) for s in ("hi", "lo")),
            "ident": ctx.enter_context(nc.sbuf_tensor("ident", [P, P], F32)),
            "out": out,
        }
        psum = ctx.enter_context(nc.psum_tensor("psum", [P, 8, 512], F32))
        g["psum"] = psum
        g["pb"] = [psum[:, i, :] for i in range(8)]
        g["ident"] = g["ident"][:, :]
        stage = g["stage"] = ctx.enter_context(nc.sbuf_tensor("stage", [P, 5, CC * D], F32))
        split = g["split"] = ctx.enter_context(nc.sbuf_tensor("split", [P, 4, CC * D], F16))

        def two(ap):
            return [ap[:, i * CC * D // 2:(i + 1) * CC * D // 2] for i in range(2)]

        g["dq_v"] = Dequant(nc, ctx, "v", [stage[:, 0, :]], [stage[:, 1, :]], [split[:, 0, :]], [split[:, 1, :]], 1)
        g["dq_qk"] = Dequant(nc, ctx, "qk", two(stage[:, 2, :]), two(stage[:, 3, :]), two(split[:, 2, :]),
                             two(split[:, 3, :]), 2)
        def slot(ap):
            return ap.rearrange("p (c n) -> p c n", c=CC)

        gw_raw = ctx.enter_context(nc.sbuf_tensor("gw_raw", [P, CC, E], F32))[:, :, :]
        gw = tuple(ctx.enter_context(nc.sbuf_tensor(f"gw_{s}", [P, CC, E], F16))[:, :, :] for s in ("hi", "lo"))
        g["c"] = {
            "raw": {"gw": gw_raw, "sg": slot(stage[:, 0, :]), "su": slot(stage[:, 1, :]), "sd": slot(stage[:, 4, :])},
            "w": {"gw": gw, "sg": tuple(slot(split[:, i, :]) for i in (0, 1)),
                  "su": tuple(slot(split[:, i, :]) for i in (2, 3))},
            "loaded": {n: ctx.enter_context(nc.semaphore(f"{n}_loaded")) for n in C_WEIGHTS},
            "w_hi": ctx.enter_context(nc.semaphore("c_w_hi")),
            "w_lo": ctx.enter_context(nc.semaphore("c_w_lo")),
        }
        g["n2"] = Norm(nc, ctx, "n2", g["xres"], g["ident"], g["xT"], g["pb"][6:8],
                       xn=stage[:, 4, 0:2 * D].rearrange("p (b n) -> p b n", b=2))
        x3 = g["x3"] = stage[:, :, :].rearrange("p s n -> p (s n)")[:, 0:T * DX].rearrange("p (t n) -> p t n", t=T)
        g["n3"] = Norm(nc, ctx, "n3", g["xres"], g["ident"], g["xT"], g["pb"][6:8], keep=x3[:, :, 0:D])
        stage_a(nc, a, g)
        g["w13"] = ctx.enter_context(nc.sbuf_tensor("w13_sb", [P, 4, CC, 2 * F], F32))
        g["w2"] = ctx.enter_context(nc.sbuf_tensor("w2_sb", [P, 4, F // P, D], F32))
        g["ew_loaded"] = [ctx.enter_context(nc.semaphore(f"ew_loaded{i}")) for i in range(4)]
        g["xbuf"] = nc.dram_tensor("xbuf", [E * CAP, DX], F32).ap()
        stage_b(nc, a, g)
        stage_c(nc, a, g)


def layouts(i):
    import numpy as np

    tidy = np.ascontiguousarray

    def by_partition(m):
        return tidy(m.reshape(m.shape[0] // P, P, -1).transpose(1, 0, 2))

    o = {"x": tidy(i["x"].reshape(N, D))}
    ctx = i["ctx_2048"]
    full = S - 1
    o["ctx"] = tidy(ctx[:, :full].transpose(0, 2, 1).reshape(B, CC, P, full).transpose(0, 2, 1, 3))
    o["ctx_last"] = by_partition(ctx[:, full].T)
    for n in ("Wq", "Wg", "Wo"):
        o[n] = by_partition(i["L0_xattn_" + n].T)
    o["Wk"], o["Wv"] = (by_partition(m.T) for m in np.split(i["L0_xattn_Wkv"], 2, 0))
    o["bg"] = tidy(i["L0_xattn_bg"].reshape(CC, P).T)

    def heads(name, rows):
        parts = [i[f"L0_attn_w{m}_{name}"].reshape(CC, rows, H, P).transpose(2, 1, 0, 3) for m in "qk"]
        return tidy(np.stack(parts, 2).reshape(H, rows, 2 * CC * P))

    def groups(name, rows):
        w = i[f"L0_attn_wv_{name}"].reshape(CC, rows, G, HG * P).transpose(2, 1, 0, 3)
        return tidy(w.reshape(G, rows, CC * HG * P))

    def out_groups(name, rows):
        w = i[f"L0_attn_wo_{name}"].reshape(G, HG, rows, D).transpose(0, 2, 1, 3)
        return tidy(w.reshape(G, rows, HG * D))

    for n, rows in (("codes", P), ("scales", P // 32)):
        o["qk_" + n], o["v_" + n], o["o_" + n] = heads(n, rows), groups(n, rows), out_groups(n, rows)
    for n in ("bq", "bk", "bv"):
        o[n] = tidy(i["L0_attn_" + n].reshape(H, P).T)
    o["bo"] = tidy(i["L0_attn_bo"].reshape(1, D))
    o["gate_w"] = by_partition(i["L0_ffn_gate_w"].T)
    o["gate_bias"] = tidy(i["L0_ffn_gate_bias"].reshape(1, E))
    for n, m in (("sg", "gate"), ("su", "up"), ("sd", "down")):
        o[n] = by_partition(i["L0_ffn_shared_" + m])
    w1, w3 = (i["L0_ffn_" + n].reshape(E, CC, P, F).transpose(0, 2, 1, 3) for n in ("w1", "w3"))
    o["w13"] = tidy(np.concatenate([w1, w3], 3))
    o["w2"] = tidy(i["L0_ffn_w2"].reshape(E, F // P, P, D).transpose(0, 2, 1, 3))
    return o


def kernel(**inputs):
    import numpy as np
    import concourse.bacc as bacc
    from concourse.bass_utils import run_bass_kernel_spmd

    arrays = layouts({n: np.asarray(v) for n, v in inputs.items()})
    nc = bacc.Bacc("TRN2", target_bir_lowering=False, num_devices=1)
    aps = {n: nc.dram_tensor(f"in_{n}", v.shape, mybir.dt.from_np(v.dtype), kind="ExternalInput").ap()
           for n, v in arrays.items()}
    out = nc.dram_tensor("out_y", (N, D), F32, kind="ExternalOutput").ap()
    build(nc, aps, out)
    r = run_bass_kernel_spmd(nc, [{f"in_{n}": v for n, v in arrays.items()}], core_ids=[0])
    return r.results[0]["out_y"].reshape(B, L, D)
```
